# Optimizing a Trainium2 kernel written in Bass

```python
import numpy as np
import jax
import jax.numpy as jnp

def _softmax(x, axis=-1):
    return jax.nn.softmax(x, axis=axis)

def _gelu(x):
    return jax.nn.gelu(x, approximate=True)

def _silu(x):
    return jax.nn.silu(x)

def _sigmoid(x):
    return jax.nn.sigmoid(x)

def _layernorm(x, axis=-1, eps=1e-05):
    m = jnp.mean(x, axis=axis, keepdims=True)
    v = jnp.var(x, axis=axis, keepdims=True)
    return (x - m) / jnp.sqrt(v + eps)

def _scatter_add(tgt, idx, src, axis=0):
    return tgt.at[idx].add(src)

def _segment_sum(src, seg, n):
    return jax.ops.segment_sum(src, seg, n)
kernel_name = 'mk_recurrent_d2_jaxref_r8_7c6531'

def setup_inputs(seed: int=0):
    np.random.seed(seed)
    _w = jnp.asarray

    def _L0_attn_setup():
        import math
        import jax, jax.numpy as jnp
        import numpy as np
        D_MODEL = 128
        NUM_HEADS = 16
        NUM_KV_HEADS = 4
        D_HEAD = D_MODEL // NUM_HEADS
        SEQ = 512
        BATCH = 1
        key = jax.random.key(seed)
        ks = jax.random.split(key, 9)
        s = 0.02
        dkv = NUM_KV_HEADS * D_HEAD
        inp = {'qkv': jax.random.normal(ks[0], (BATCH, SEQ, D_MODEL), jnp.float32), 'Wq': jax.random.normal(ks[1], (D_MODEL, D_MODEL), jnp.float32) * s, 'bq': jnp.zeros((D_MODEL,), jnp.float32), 'Wk': jax.random.normal(ks[2], (D_MODEL, dkv), jnp.float32) * s, 'bk': jnp.zeros((dkv,), jnp.float32), 'Wv': jax.random.normal(ks[3], (D_MODEL, dkv), jnp.float32) * s, 'bv': jnp.zeros((dkv,), jnp.float32), 'Wo': jax.random.normal(ks[4], (D_MODEL, D_MODEL), jnp.float32) * s, 'bo': jnp.zeros((D_MODEL,), jnp.float32), 'slopes': jnp.exp2(-jnp.linspace(0.0, 7.0, NUM_HEADS)).astype(jnp.float32)}
        return inp
    _L0_attn_in = _L0_attn_setup()

    def _L0_ffn_setup():
        import jax, jax.numpy as jnp
        import numpy as np
        import math
        B, L, D = (4, 512, 128)
        F = 512
        E = 16
        CAP_FACTOR = 1.0
        EPS = 1e-05
        key = jax.random.key(seed)
        ks = jax.random.split(key, 8)
        std = 0.02
        return {'x': jax.random.normal(ks[0], (B, L, D), dtype=jnp.float32), 'norm_weight': jnp.ones((D,), dtype=jnp.float32), 'router_weight': jax.random.normal(ks[1], (E, D), dtype=jnp.float32) * std, 'router_bias': jnp.zeros((E,), dtype=jnp.float32), 'fc1_weight': jax.random.normal(ks[2], (E, F, D), dtype=jnp.float32) * std, 'fc1_bias': jnp.zeros((E, F), dtype=jnp.float32), 'fc2_weight': jax.random.normal(ks[3], (E, D, F), dtype=jnp.float32) * std, 'fc2_bias': jnp.zeros((E, D), dtype=jnp.float32)}
    _L0_ffn_in = _L0_ffn_setup()

    def _L1_attn_setup():
        import jax, jax.numpy as jnp
        import numpy as np
        NEG_BIG = -1e+38

        def _wkv_scan(w, u, k, v, aa0, bb0, pp0):
            kT = jnp.moveaxis(k, 1, 0)
            vT = jnp.moveaxis(v, 1, 0)

            def step(carry, kv):
                aa, bb, pp = carry
                kt, vt = kv
                ww = u + kt
                p = jnp.maximum(pp, ww)
                e1 = jnp.exp(pp - p)
                e2 = jnp.exp(ww - p)
                y = (e1 * aa + e2 * vt) / (e1 * bb + e2)
                ww2 = pp + w
                p2 = jnp.maximum(ww2, kt)
                e1 = jnp.exp(ww2 - p2)
                e2 = jnp.exp(kt - p2)
                return ((e1 * aa + e2 * vt, e1 * bb + e2, p2), y)
            (aa, bb, pp), yT = jax.lax.scan(step, (aa0, bb0, pp0), (kT, vT))
            return (jnp.moveaxis(yT, 0, 1), aa, bb, pp)

        def _reference_tuple_inner(x, W_rvk, W_out, time_decay, time_first):
            B, T, C = x.shape
            rvk = jnp.einsum('btc,dc->btd', x, W_rvk)
            r, v, k = jnp.split(rvk, 3, axis=-1)
            w = -jnp.exp(time_decay)
            u = time_first
            aa0 = jnp.zeros((B, C), dtype=x.dtype)
            bb0 = jnp.zeros((B, C), dtype=x.dtype)
            pp0 = jnp.full((B, C), NEG_BIG, dtype=x.dtype)
            wkv, aa, bb, pp = _wkv_scan(w, u, k, v, aa0, bb0, pp0)
            rwkv = jax.nn.sigmoid(r) * wkv
            out = jnp.einsum('btc,dc->btd', rwkv, W_out)
            h = aa
            c = jnp.stack([bb, pp], axis=-1).reshape(B, 2 * C)
            return (out, h, c)
        key = jax.random.key(seed)
        k1, k2, k3 = jax.random.split(key, 3)
        B, T, C = (32, 128, 128)
        x = jax.random.normal(k1, (B, T, C), dtype=jnp.float32)
        W_rvk = jax.random.normal(k2, (3 * C, C), dtype=jnp.float32) * (1.0 / np.sqrt(C))
        W_out = jax.random.normal(k3, (C, C), dtype=jnp.float32) * (1.0 / np.sqrt(C))
        time_decay = jnp.ones((C,), dtype=jnp.float32)
        time_first = jnp.ones((C,), dtype=jnp.float32)
        return {'x': x, 'W_rvk': W_rvk, 'W_out': W_out, 'time_decay': time_decay, 'time_first': time_first}
    _L1_attn_in = _L1_attn_setup()

    def _L1_ffn_setup():
        import jax, jax.numpy as jnp
        import numpy as np
        B, S, DIM = (4, 256, 128)
        E, K, HID = (8, 2, 512)
        key = jax.random.key(seed)
        ks = jax.random.split(key, 8)
        init = lambda k, sh: jax.random.normal(k, sh, jnp.float32) * 0.02
        return {'x': jax.random.normal(ks[0], (B, S, DIM), jnp.float32), 'gate_w': init(ks[1], (DIM, E)), 'gate_b': jnp.zeros((E,), jnp.float32), 'w1': init(ks[2], (E, DIM, HID)), 'b1': jnp.zeros((E, HID), jnp.float32), 'w2': init(ks[3], (E, HID, DIM)), 'b2': jnp.zeros((E, DIM), jnp.float32), 'ws1': init(ks[4], (DIM, HID)), 'bs1': jnp.zeros((HID,), jnp.float32), 'ws2': init(ks[5], (HID, DIM)), 'bs2': jnp.zeros((DIM,), jnp.float32)}
    _L1_ffn_in = _L1_ffn_setup()
    _d = {'L0_attn_qkv': _L0_attn_in['qkv'], 'L0_attn_Wq': _L0_attn_in['Wq'], 'L0_attn_bq': _L0_attn_in['bq'], 'L0_attn_Wk': _L0_attn_in['Wk'], 'L0_attn_bk': _L0_attn_in['bk'], 'L0_attn_Wv': _L0_attn_in['Wv'], 'L0_attn_bv': _L0_attn_in['bv'], 'L0_attn_Wo': _L0_attn_in['Wo'], 'L0_attn_bo': _L0_attn_in['bo'], 'L0_attn_slopes': _L0_attn_in['slopes'], 'L0_ffn_norm_weight': _L0_ffn_in['norm_weight'], 'L0_ffn_router_weight': _L0_ffn_in['router_weight'], 'L0_ffn_router_bias': _L0_ffn_in['router_bias'], 'L0_ffn_fc1_weight': _L0_ffn_in['fc1_weight'], 'L0_ffn_fc1_bias': _L0_ffn_in['fc1_bias'], 'L0_ffn_fc2_weight': _L0_ffn_in['fc2_weight'], 'L0_ffn_fc2_bias': _L0_ffn_in['fc2_bias'], 'L1_attn_W_rvk': _L1_attn_in['W_rvk'], 'L1_attn_W_out': _L1_attn_in['W_out'], 'L1_attn_time_decay': _L1_attn_in['time_decay'], 'L1_attn_time_first': _L1_attn_in['time_first'], 'L1_ffn_gate_w': _L1_ffn_in['gate_w'], 'L1_ffn_gate_b': _L1_ffn_in['gate_b'], 'L1_ffn_w1': _L1_ffn_in['w1'], 'L1_ffn_b1': _L1_ffn_in['b1'], 'L1_ffn_w2': _L1_ffn_in['w2'], 'L1_ffn_b2': _L1_ffn_in['b2'], 'L1_ffn_ws1': _L1_ffn_in['ws1'], 'L1_ffn_bs1': _L1_ffn_in['bs1'], 'L1_ffn_ws2': _L1_ffn_in['ws2'], 'L1_ffn_bs2': _L1_ffn_in['bs2']}
    _x0 = _d['L0_attn_qkv']
    _d['L0_attn_qkv'] = jax.random.normal(jax.random.fold_in(jax.random.key(seed), 1), (1, 2048, 128), dtype=_x0.dtype)
    del _x0
    return _d

def reference(L0_attn_qkv, L0_attn_Wq, L0_attn_bq, L0_attn_Wk, L0_attn_bk, L0_attn_Wv, L0_attn_bv, L0_attn_Wo, L0_attn_bo, L0_attn_slopes, L0_ffn_norm_weight, L0_ffn_router_weight, L0_ffn_router_bias, L0_ffn_fc1_weight, L0_ffn_fc1_bias, L0_ffn_fc2_weight, L0_ffn_fc2_bias, L1_attn_W_rvk, L1_attn_W_out, L1_attn_time_decay, L1_attn_time_first, L1_ffn_gate_w, L1_ffn_gate_b, L1_ffn_w1, L1_ffn_b1, L1_ffn_w2, L1_ffn_b2, L1_ffn_ws1, L1_ffn_bs1, L1_ffn_ws2, L1_ffn_bs2):

    def _L0_attn_ref(qkv, Wq, bq, Wk, bk, Wv, bv, Wo, bo, slopes):
        import math
        import jax, jax.numpy as jnp
        import numpy as np
        D_MODEL = 128
        NUM_HEADS = 16
        NUM_KV_HEADS = 4
        D_HEAD = D_MODEL // NUM_HEADS
        SEQ = 512
        BATCH = 1
        B, S, D = qkv.shape
        H, KVH, dh = (NUM_HEADS, NUM_KV_HEADS, D_HEAD)
        G = H // KVH
        scale = 1.0 / math.sqrt(dh)
        q = (qkv @ Wq + bq).reshape(B, S, H, dh).transpose(0, 2, 1, 3)
        k = (qkv @ Wk + bk).reshape(B, S, KVH, dh).transpose(0, 2, 1, 3)
        v = (qkv @ Wv + bv).reshape(B, S, KVH, dh).transpose(0, 2, 1, 3)
        qg = q.reshape(B, KVH, G, S, dh)
        scores = jnp.einsum('bhgqd,bhkd->bhgqk', qg, k) * scale
        rel = jnp.arange(S, dtype=jnp.float32)[None, :] - jnp.arange(S, dtype=jnp.float32)[:, None]
        bias = slopes.reshape(KVH, G, 1, 1) * rel
        causal = jnp.tril(jnp.ones((S, S), dtype=bool))
        bias = jnp.where(causal, bias, -jnp.inf)
        attn = jax.nn.softmax(scores + bias[None], axis=-1)
        out = jnp.einsum('bhgqk,bhkd->bhgqd', attn, v)
        out = out.reshape(B, H, S, dh).transpose(0, 2, 1, 3).reshape(B, S, D)
        return out @ Wo + bo

    def _L0_ffn_ref(x, norm_weight, router_weight, router_bias, fc1_weight, fc1_bias, fc2_weight, fc2_bias):
        import jax, jax.numpy as jnp
        import numpy as np
        import math
        B, L, D = (4, 512, 128)
        F = 512
        E = 16
        CAP_FACTOR = 1.0
        EPS = 1e-05
        b, l, d = x.shape
        n_tokens = b * l
        n_experts = router_weight.shape[0]
        capacity = max(1, math.ceil(CAP_FACTOR * n_tokens / n_experts))
        top_k = min(capacity, n_tokens)
        xf = x.reshape(n_tokens, d)
        rms = jnp.sqrt(jnp.mean(xf * xf, axis=-1, keepdims=True) + EPS)
        xn = xf / rms * norm_weight
        logits = xn @ router_weight.T + router_bias
        probs = jax.nn.softmax(logits, axis=-1)
        _, idx = jax.lax.top_k(logits.T, top_k)
        xe = xn[idx]
        h = jnp.einsum('ecd,efd->ecf', xe, fc1_weight) + fc1_bias[:, None, :]
        h = jax.nn.gelu(h, approximate=False)
        y = jnp.einsum('ecf,edf->ecd', h, fc2_weight) + fc2_bias[:, None, :]
        gates = jnp.take_along_axis(probs.T, idx, axis=1)
        flat_idx = idx.reshape(-1)
        contrib = (y * gates[:, :, None]).reshape(-1, d)
        output = jnp.zeros((n_tokens, d), dtype=x.dtype).at[flat_idx].add(contrib)
        gate_sums = jnp.zeros((n_tokens, 1), dtype=x.dtype).at[flat_idx].add(gates.reshape(-1, 1))
        assigned = gate_sums > 0
        output = jnp.where(assigned, output / jnp.where(assigned, gate_sums, 1.0), output)
        return output.reshape(b, l, d)

    def _L1_attn_ref(x, W_rvk, W_out, time_decay, time_first):
        import jax, jax.numpy as jnp
        import numpy as np
        NEG_BIG = -1e+38

        def _wkv_scan(w, u, k, v, aa0, bb0, pp0):
            kT = jnp.moveaxis(k, 1, 0)
            vT = jnp.moveaxis(v, 1, 0)

            def step(carry, kv):
                aa, bb, pp = carry
                kt, vt = kv
                ww = u + kt
                p = jnp.maximum(pp, ww)
                e1 = jnp.exp(pp - p)
                e2 = jnp.exp(ww - p)
                y = (e1 * aa + e2 * vt) / (e1 * bb + e2)
                ww2 = pp + w
                p2 = jnp.maximum(ww2, kt)
                e1 = jnp.exp(ww2 - p2)
                e2 = jnp.exp(kt - p2)
                return ((e1 * aa + e2 * vt, e1 * bb + e2, p2), y)
            (aa, bb, pp), yT = jax.lax.scan(step, (aa0, bb0, pp0), (kT, vT))
            return (jnp.moveaxis(yT, 0, 1), aa, bb, pp)

        def _reference_tuple_inner(x, W_rvk, W_out, time_decay, time_first):
            B, T, C = x.shape
            rvk = jnp.einsum('btc,dc->btd', x, W_rvk)
            r, v, k = jnp.split(rvk, 3, axis=-1)
            w = -jnp.exp(time_decay)
            u = time_first
            aa0 = jnp.zeros((B, C), dtype=x.dtype)
            bb0 = jnp.zeros((B, C), dtype=x.dtype)
            pp0 = jnp.full((B, C), NEG_BIG, dtype=x.dtype)
            wkv, aa, bb, pp = _wkv_scan(w, u, k, v, aa0, bb0, pp0)
            rwkv = jax.nn.sigmoid(r) * wkv
            out = jnp.einsum('btc,dc->btd', rwkv, W_out)
            h = aa
            c = jnp.stack([bb, pp], axis=-1).reshape(B, 2 * C)
            return (out, h, c)
        return _reference_tuple_inner(x, W_rvk, W_out, time_decay, time_first)[0]

    def _L1_ffn_ref(x, gate_w, gate_b, w1, b1, w2, b2, ws1, bs1, ws2, bs2):
        import jax, jax.numpy as jnp
        import numpy as np
        B, S, DIM = (4, 256, 128)
        E, K, HID = (8, 2, 512)
        orig_shape = x.shape
        xf = x.reshape(-1, DIM)
        logits = xf @ gate_w + gate_b
        top_w, top_i = jax.lax.top_k(logits, K)
        gw = jax.nn.softmax(top_w, axis=-1).astype(xf.dtype)
        combine = (gw[:, :, None] * jax.nn.one_hot(top_i, E, dtype=xf.dtype)).sum(axis=1)
        out = jnp.zeros_like(xf)
        for e in range(E):
            h = jax.nn.gelu(xf @ w1[e] + b1[e], approximate=False)
            out = out + combine[:, e:e + 1] * (h @ w2[e] + b2[e])
        shared = jax.nn.gelu(xf @ ws1 + bs1, approximate=False) @ ws2 + bs2
        return (out + shared).reshape(orig_shape)
    x = L0_attn_qkv
    xn = _layernorm(x, axis=-1)
    s = _L0_attn_ref(xn, L0_attn_Wq, L0_attn_bq, L0_attn_Wk, L0_attn_bk, L0_attn_Wv, L0_attn_bv, L0_attn_Wo, L0_attn_bo, L0_attn_slopes)
    g = _silu(_L0_ffn_ref(xn, L0_ffn_norm_weight, L0_ffn_router_weight, L0_ffn_router_bias, L0_ffn_fc1_weight, L0_ffn_fc1_bias, L0_ffn_fc2_weight, L0_ffn_fc2_bias))
    x = x + s * g
    xn = _layernorm(x, axis=-1)
    s = _L1_attn_ref(xn, L1_attn_W_rvk, L1_attn_W_out, L1_attn_time_decay, L1_attn_time_first)
    g = _silu(_L1_ffn_ref(xn, L1_ffn_gate_w, L1_ffn_gate_b, L1_ffn_w1, L1_ffn_b1, L1_ffn_w2, L1_ffn_b2, L1_ffn_ws1, L1_ffn_bs1, L1_ffn_ws2, L1_ffn_bs2))
    x = x + s * g
    return x

_drawn_inputs = setup_inputs


def setup_inputs(seed=0):
    import zlib

    import numpy as np

    out = dict(_drawn_inputs(seed))
    spreads = {'L0_attn_bq': (0.0, 0.8),
     'L0_attn_bk': (0.0, 2.0),
     'L0_attn_bv': (0.0, 0.8),
     'L0_attn_bo': (0.0, 0.8),
     'L0_ffn_norm_weight': (1.0, 0.6),
     'L0_ffn_router_bias': (0.0, 0.8),
     'L0_ffn_fc1_bias': (0.0, 0.8),
     'L0_ffn_fc2_bias': (0.0, 0.8),
     'L1_attn_time_decay': (1.0, 0.6),
     'L1_attn_time_first': (1.0, 0.6),
     'L1_ffn_gate_b': (0.0, 0.765),
     'L1_ffn_b1': (0.0, 0.8),
     'L1_ffn_b2': (0.0, 2.0),
     'L1_ffn_bs1': (0.0, 2.0),
     'L1_ffn_bs2': (0.0, 2.0)}
    factors = {'L0_attn_Wq': 8.0,
     'L0_attn_Wk': 8.0,
     'L0_attn_Wv': 8.0,
     'L0_attn_Wo': 8.0,
     'L0_attn_slopes': 8.0,
     'L0_ffn_router_weight': 8.0,
     'L0_ffn_fc1_weight': 8.0,
     'L0_ffn_fc2_weight': 8.0,
     'L1_ffn_gate_w': 3.384,
     'L1_ffn_w1': 6.455,
     'L1_ffn_w2': 5.845,
     'L1_ffn_ws1': 4.545,
     'L1_ffn_ws2': 4.173}
    for name, (base, spread) in spreads.items():
        noise = np.random.default_rng([zlib.crc32(name.encode()), seed]).standard_normal(out[name].shape)
        drawn = base * np.exp(spread * noise) if base else spread * noise
        out[name] = jnp.asarray(drawn.astype(out[name].dtype))
    for name, factor in factors.items():
        out[name] = (out[name] * factor).astype(out[name].dtype)
    return out
```

```python
import concourse.bass as bass
import numpy as np
from concourse import mybir
from contextlib import ExitStack

F32, BF16, U32 = mybir.dt.float32, mybir.dt.bfloat16, mybir.dt.uint32
ALU, ACT, AX = mybir.AluOpType, mybir.ActivationFunctionType, mybir.AxisListType

T, D, P = 2048, 128, 128
TT = T // P
QC = 512
NCH = T // QC
TPC = QC // P
EPS = 1e-5

H, KVH, DH = 16, 4, 8
G = H // KVH
SCALE = float(DH) ** -0.5
BLK = 32
BIAS_ROWS = 8
KROWS = 3 * BLK
HIDDEN = -1e30
E0, F0 = 16, 512
CAP = T // E0
FT = F0 // P
TAB = D + E0
ACCW = D + 1
E1, F1 = 8, 512
LOWEST = -3.0e38
NEG_BIG = -1e38


def attention_schedule():
    max_units = [(g, j, qt, kc) for g in range(KVH) for j in range(G) for qt in range(TT)
                 for kc in range(qt // TPC + 1)]
    quads = [(g, c, kt) for g in range(KVH) for c in range(NCH) for kt in range(TPC * (c + 1))]
    per_group = len(max_units) // KVH
    lead = per_group + 24
    order, done_max = [], 0
    turn_at = {per_group * (g + 1) + 7: g for g in range(KVH - 1)}

    def emit_max(n):
        nonlocal done_max
        for _ in range(n):
            if done_max < len(max_units):
                order.append(("max", done_max))
                done_max += 1
                if done_max in turn_at:
                    order.append(("turn_max", turn_at[done_max]))

    emit_max(lead)
    turn_out = []
    for m, (g, c, kt) in enumerate(quads):
        for j in range(G):
            order.append(("exp", m * G + j))
            emit_max(1)
        if done_max == len(max_units) and ("turn_max", KVH - 1) not in order:
            order.append(("turn_max", KVH - 1))
        if m:
            order.append(("pv", m - 1))
        if turn_out and turn_out[0][0] <= m:
            order.append(("turn_out", turn_out.pop(0)[1]))
        if kt == TPC * (c + 1) - 1:
            turn_out.append((m + 2, g * NCH + c))
    order.append(("pv", len(quads) - 1))
    order += [("turn_out", ch) for _, ch in turn_out]
    return max_units, quads, order


def two_layers(nc, x_d, Wq_d, bq_d, Wk_d, bk_d, Wv_d, bv_d, Wo_d, bo_d, slopes_d, nw_d, rw_d, rb_d, fc1_d, fc1b_d,
               fc2_d, fc2b_d, Wrvk_d, Wout_d, decay_d, first_d, gw_d, gb_d, w1_d, b1_d, w2_d, b2_d, ws1_d, bs1_d,
               ws2_d, bs2_d, out_d):
    max_units, quads, order = attention_schedule()
    per_group = len(max_units) // KVH
    with ExitStack() as ctx:
        def sb(name, shape, dt=F32):
            return ctx.enter_context(nc.sbuf_tensor(name, shape, dt))

        def sem(name):
            return ctx.enter_context(nc.semaphore(name))

        def scratch(name, shape, dt=F32):
            return nc.dram_tensor(name, shape, dt, kind="Internal").ap()

        bank = [ctx.enter_context(nc.psum_tensor(f"bank{i}", [P, QC], F32)) for i in range(8)]

        q_parts_d = scratch("q_parts_d", (3, D, T), BF16)
        k_parts_d = scratch("k_parts_d", (3, KVH * DH, T), BF16)
        rows_d = scratch("rows_d", (4, T), BF16)
        table_d = scratch("table_d", (T, TAB))
        sums_d = scratch("sums_d", (T, ACCW))

        q_stack = sb("q_stack", [P, H, T], BF16)
        k_stack = sb("k_stack", [P, KVH, T], BF16)
        x = sb("x", [P, TT, D])
        xn = sb("xn", [P, TT, D])
        xnT = sb("xnT", [P, T])
        v_aug = sb("v_aug", [P, TT, KVH, BLK])
        arena = sb("arena", [P, 16384])
        routeT = sb("routeT", [P, TT * ACCW])

        Wq = sb("Wq", [D, D])
        Wk = sb("Wk", [D, KVH * DH])
        Wv = sb("Wv", [D, KVH * DH])
        Wo = sb("Wo", [D, D])
        bq = sb("bq", [D, 1])
        bqs = sb("bqs", [D, 1])
        bk = sb("bk", [KVH * DH, 1])
        bv_rows = sb("bv_rows", [P, KVH, DH])
        bo_rows = sb("bo_rows", [P, D])
        nw_rows = sb("nw_rows", [P, D])
        nw_col = sb("nw_col", [D, 1])
        rw = sb("rw", [E0, D])
        rwT = sb("rwT", [D, E0])
        rb_rows = sb("rb_rows", [P, E0])
        slopes = sb("slopes", [H, 1])
        hid_bias_in = sb("hid_bias_in", [E0 * FT + E1 * FT + FT, P])
        hid_bias = sb("hid_bias", [P, E0 * FT + E1 * FT + FT])
        ident = sb("ident", [P, P])
        ident_b = sb("ident_b", [P, P], BF16)
        hide_q = sb("hide_q", [P, P], BF16)
        hide_k = sb("hide_k", [P, P], BF16)
        ones_row = sb("ones_row", [1, P])
        zeros = sb("zeros", [P, ACCW])
        bn = sb("bn", [P, TT, 6])
        mv = sb("mv", [P, TT, 2])
        var_eps = sb("var_eps", [P, TT])
        rstd = sb("rstd", [P, TT])
        minus_half = sb("minus_half", [P, TT])
        sumsq = sb("sumsq", [P, TT])
        rrms = sb("rrms", [P, TT])
        square_out = sb("square_out", [P, D])
        logits = sb("logits", [P, TT, E0])
        probs = sb("probs", [P, TT, E0])
        row_max = sb("row_max", [P, TT])
        row_sum = sb("row_sum", [P, TT])
        top8 = sb("top8", [E0, 8])
        top_at = sb("top_at", [E0, CAP], U32)
        top_at_f = sb("top_at_f", [E0, CAP])
        token_of = sb("token_of", [CAP, E0], U32)
        part_max = sb("part_max", [P, 2, G, TT, NCH])
        neg_max = sb("neg_max", [P, KVH, G * TT])
        max_part = sb("max_part", [G * TT, 3, P], BF16)
        max_rest = sb("max_rest", [G * TT, 2, P])
        out_rec = sb("out_rec", [P, TPC, G])
        gates1 = sb("gates1", [P, TT, E1])
        top1 = sb("top1", [P, TT, 8])
        top1_at = sb("top1_at", [P, TT, 8], U32)
        combine = sb("combine", [P, TT, E1 + 1])
        b2_all = sb("b2_all", [E1 + 1, D])
        gw = sb("gw", [D, E1])
        gb_rows = sb("gb_rows", [P, E1])
        decay = sb("decay", [D, 1])
        w_col = sb("w_col", [D, 1])
        first = sb("first", [D, 1])
        sm1 = sb("sm1", [P, 4, TT])
        hot = sb("hot", [P, 2, TT, E1])
        iota8 = sb("iota8", [P, E1])

        def part(lo, *shape):
            n = int(np.prod(shape))
            v = arena[:, lo:lo + n]
            return v if len(shape) == 1 else v.rearrange("p (a b) -> p a b", a=shape[0])

        q_f, q_rest = part(0, T), part(2048, T)
        q_part = arena[:, 4096:7168].bitcast(BF16).rearrange("p (a t) -> p a t", a=3)
        k_f, k_rest = arena[0:KVH * DH, 7168:9216], arena[0:KVH * DH, 9216:11264]
        k_part = arena[0:KVH * DH, 11264:14336].bitcast(BF16).rearrange("p (a t) -> p a t", a=3)
        x_route = part(14336, TT, D)
        lo_w = arena[0:H, 0:6144].bitcast(BF16).rearrange("p (a t) -> p a t", a=6)
        slope_w = arena[0:H, 6144:9216].bitcast(BF16).rearrange("p (a t) -> p a t", a=3)
        hi_w = arena[0:H, 9216:15360].bitcast(BF16).rearrange("p (a t) -> p a t", a=6)
        j_rows = xnT[0:1, :].bitcast(BF16).rearrange("p (a t) -> p a t", a=2)
        fc2b = xn[0:1, :, :].rearrange("p a d -> p (a d)")
        NP = 8
        probsT = part(0, NP, QC)
        out_tok = part(4096, TT, D)
        fc1_raw, fc2_raw = part(6144, 2, F0), part(7168, 2, F0)
        fc1T, fc2T = part(8192, 2, F0), part(9216, 2, F0)
        out_sb = part(10240, 2, QC)
        taken = part(11264, 2, TAB)
        takenT = part(11552, 2, CAP)
        hidden0 = part(11808, 2, F0)
        weighted = part(12832, 2, ACCW)
        attnT = part(13096, T)
        lay1 = q_stack[:, :, :].rearrange("p h t -> p (h t)").bitcast(F32)
        lay1k = k_stack[:, :, :].rearrange("p h t -> p (h t)").bitcast(F32)
        w1 = lay1[:, 0:4096].rearrange("p (e f) -> p e f", e=E1)
        w2 = lay1[:, 4096:8192].rearrange("p (e f) -> p e f", e=E1 * FT)
        ws1 = lay1[:, 8192:8704]
        ws2 = lay1[:, 8704:9216].rearrange("p (e f) -> p e f", e=FT)
        PP = lay1[:, 9216:9216 + T + 1]
        AA = lay1[:, 11272:11272 + T + 1]
        BB = lay1[:, 13328:13328 + T + 1]
        Wrvk = lay1[:, 15384:15384 + 384].rearrange("p (a c) -> p a c", a=3)
        Wout = lay1[:, 15768:15896]
        WT = lay1[:, 15896:15896 + 0]
        r_T, k_T = lay1k[:, 0:T], lay1k[:, T:2 * T]
        NHS = 8
        hid1 = part(0, NHS, QC)
        v_T = part(4096, T)
        keep_w, add_w = part(6144, T), part(8192, T)
        old_w, new_w = part(10240, T), part(12288, T)
        tmp = part(14336, T)
        combineT = tmp[0:E1 + 1, :]
        tmp2 = routeT[:, 0:T]
        moe = v_aug[:, :, :, :].rearrange("p a b c -> p (a b c)")
        moe_t = moe.rearrange("p (a b) -> p a b", a=TT)
        wT = sb("wT", [P, 4, P])

        slope_rest = sb("slope_rest", [H, 2])
        slope_b = sb("slope_b", [H, 3], BF16)
        slope_f = sb("slope_f", [H, 3])
        i_hi, hi_f = routeT[0:H, 0:TT], routeT[0:H, TT:2 * TT]
        i_lo, lo_f = routeT[0:H, 128:256], routeT[0:H, 256:384]
        hi_b = routeT[0:H, 384:432].bitcast(BF16).rearrange("p (a b) -> p a b", a=6)
        lo_b = routeT[0:H, 512:896].bitcast(BF16).rearrange("p (a b) -> p a b", a=6)
        sl_b = routeT[0:H, 896:1088].bitcast(BF16).rearrange("p (a b) -> p a b", a=3)

        one_zero = routeT[0:TT, 1088:1216].bitcast(BF16).rearrange("p (a b) -> p a b", a=2)

        x_in = [sem(f"x_in{i}") for i in range(NCH)]
        weights_in = sem("weights_in")
        consts_ready = sem("consts_ready")
        stats_ready = sem("stats_ready")
        rstd_ready = sem("rstd_ready")
        xn_ready = sem("xn_ready")
        turned_ps = sem("turned_ps")
        xnT_ready = sem("xnT_ready")
        bias_turned = sem("bias_turned")
        hid_bias_ready = sem("hid_bias_ready")
        rwT_ready = sem("rwT_ready")
        q_ps = sem("q_ps")
        q_f_ready = sem("q_f_ready")
        k_ps = sem("k_ps")
        k_f_ready = sem("k_f_ready")
        v_ps = sem("v_ps")
        v_ready = sem("v_ready")
        bqs_ready = sem("bqs_ready")
        route_ps = sem("route_ps")
        sumsq_ready = sem("sumsq_ready")
        rrms_ready = sem("rrms_ready")
        x_route_ready = sem("x_route_ready")
        logits_ready = sem("logits_ready")
        shifted_ready = sem("shifted_ready")
        exp0_ready = sem("exp0_ready")
        probs_ready = sem("probs_ready")
        logitsT_ps = sem("logitsT_ps")
        routeT_ready = sem("routeT_ready")
        q_part_ready = sem("q_part_ready")
        k_part_ready = sem("k_part_ready")
        q_part_out = [sem(f"q_part_out{i}") for i in range(3)]
        k_part_out = sem("k_part_out")
        const_rows_ready = sem("const_rows_ready")
        const_rows_out = sem("const_rows_out")
        bias_tables = sem("bias_tables")
        wide_ready = sem("wide_ready")
        slope_in = sem("slope_in")
        bias_rows_in = sem("bias_rows_in")
        k_rows_in = sem("k_rows_in")
        q_rows_in = [sem(f"q_rows_in{g}") for g in range(KVH)]
        table_out = sem("table_out")
        sums_zero = sem("sums_zero")
        max_ps = sem("max_ps")
        max_read = sem("max_read")
        neg_max_ready = sem("neg_max_ready")
        max_turned = sem("max_turned")
        max_rows_ready = sem("max_rows_ready")
        max_rows_in = sem("max_rows_in")
        turn_bank_read = sem("turn_bank_read")
        exp_ps = sem("exp_ps")
        probsT_ready = sem("probsT_ready")
        pv_done = sem("pv_done")
        out_sb_ready = sem("out_sb_ready")
        out_turned = sem("out_turned")
        out_tok_ready = sem("out_tok_ready")
        top_ready = sem("top_ready")
        top_turned = sem("top_turned")
        token_of_ready = sem("token_of_ready")
        fc_in = [sem(f"fc_in{i}") for i in range(2)]
        fc2b_in = sem("fc2b_in")
        fc_turned = sem("fc_turned")
        fcT_ready = sem("fcT_ready")
        taken_in = [sem(f"taken_in{i}") for i in range(2)]
        taken_turned = sem("taken_turned")
        takenT_ready = sem("takenT_ready")
        hidden0_ps = sem("hidden0_ps")
        hidden0_ready = sem("hidden0_ready")
        y0_ps = sem("y0_ps")
        weighted_ready = sem("weighted_ready")
        scattered = sem("scattered")
        sums_in = sem("sums_in")
        attn_turned = sem("attn_turned")
        attnT_ready = sem("attnT_ready")
        s0_ps = sem("s0_ps")
        s0_read = sem("s0_read")
        f0_ready = sem("f0_ready")
        silu0_ready = sem("silu0_ready")
        x1_ready = sem("x1_ready")
        lay1_in = sem("lay1_in")
        wT_ps = sem("wT_ps")
        wT_ready = sem("wT_ready")
        rvk_ps = sem("rvk_ps")
        rvk_ready = sem("rvk_ready")
        gate_ps = sem("gate_ps")
        gate_diff_ready = sem("gate_diff_ready")
        gate_exp_ready = sem("gate_exp_ready")
        combine_ready = sem("combine_ready")
        combine_turned = sem("combine_turned")
        combineT_ready = sem("combineT_ready")
        moe_bias_ps = sem("moe_bias_ps")
        moe_bias_read = sem("moe_bias_read")
        hid1_ps = sem("hid1_ps")
        hid1_ready = sem("hid1_ready")
        y1_ps = sem("y1_ps")
        y1_read = sem("y1_read")
        decay_ready = sem("decay_ready")
        w_ready = sem("w_ready")
        exps_wanted = sem("exps_wanted")
        exps_ready = sem("exps_ready")
        rwkv_ready = sem("rwkv_ready")
        s1_ps = sem("s1_ps")
        silu1_ready = sem("silu1_ready")
        x2_ready = sem("x2_ready")
        x2_out = sem("x2_out")
        dve_step = sem("dve_step")
        pool_step = sem("pool_step")
        act_step = sem("act_step")

        block = ctx.enter_context(nc.Block())
        units1 = [(e, c) for e in range(E1 + 1) for c in range(NCH)]
        N_WEIGHTS = 28

        @block.sync
        def _(sp):
            x_v = x_d[0].rearrange("(a p) d -> p a d", p=P)
            for i in range(NCH):
                sp.dma_start(x[:, TPC * i:TPC * (i + 1), :], x_v[:, TPC * i:TPC * (i + 1), :]).then_inc(x_in[i], 16)
            col = lambda v: v.rearrange("(p a) -> p a", a=1)
            row = lambda v: v.rearrange("(a p) -> a p", a=1)
            sp.dma_start(slopes[:, :], col(slopes_d)).then_inc(slope_in, 16)
            NB = E0 * FT
            loads = [
                (Wq[:, :], Wq_d), (Wk[:, :], Wk_d), (Wv[:, :], Wv_d), (Wo[:, :], Wo_d),
                (bq[:, :], col(bq_d)), (bk[:, :], col(bk_d)), (nw_col[:, :], col(nw_d)),
                (bv_rows[:, :, :], bv_d.rearrange("(a k d) -> a k d", a=1, k=KVH).broadcast_to([P, KVH, DH])),
                (bo_rows[:, :], row(bo_d).broadcast_to([P, D])), (nw_rows[:, :], row(nw_d).broadcast_to([P, D])),
                (rw[:, :], rw_d), (rb_rows[:, :], row(rb_d).broadcast_to([P, E0])),
                (hid_bias_in[0:NB, :], fc1b_d.rearrange("e (a p) -> (e a) p", p=P)),
                (hid_bias_in[NB:NB + E1 * FT, :], b1_d.rearrange("e (a p) -> (e a) p", p=P)),
                (hid_bias_in[NB + E1 * FT:NB + E1 * FT + FT, :], bs1_d.rearrange("(a p) -> a p", p=P)),
                (gw[:, :], gw_d), (gb_rows[:, :], row(gb_d).broadcast_to([P, E1])),
                (b2_all[0:E1, :], b2_d), (b2_all[E1:E1 + 1, :], row(bs2_d)),
                (decay[:, :], col(decay_d)), (first[:, :], col(first_d)),
            ]
            assert len(loads) == 21
            for dst, src in loads:
                sp.dma_start(dst, src).then_inc(weights_in, 16)
            sp.wait_ge(const_rows_ready, 1)
            sp.dma_start(rows_d[0:2, :].rearrange("(o a) t -> o a t", o=1), j_rows).then_inc(const_rows_out, 16)
            for n in range(2):
                sp.dma_start(rows_d[2 + n].rearrange("(a b) -> a b", a=TT), one_zero[:, n, :]).then_inc(const_rows_out, 16)
            sp.wait_ge(const_rows_out, 48)
            for a in range(3):
                r = BLK * a
                sp.dma_start(k_stack[r:r + 2, :, :], rows_d[0:2, :].unsqueeze(1).broadcast_to([2, KVH, T])
                             ).then_inc(k_rows_in, 16)
                sp.dma_start(k_stack[r + 2:r + 8, :, :],
                             rows_d[2:3, :].unsqueeze(1).broadcast_to([6, KVH, T])).then_inc(k_rows_in, 16)
                sp.dma_start(q_stack[r + 6:r + 8, :, :],
                             rows_d[3:4, :].unsqueeze(1).broadcast_to([2, H, T])).then_inc(k_rows_in, 16)
            sp.wait_ge(wide_ready, 2)
            for a in range(3):
                r = BLK * a
                for n in range(2):
                    for lo, src in ((0, slope_w[:, a, :]), (2, hi_w[:, 2 * a + n, :]), (4, lo_w[:, 2 * a + n, :])):
                        sp.dma_start(q_stack[r + lo + n:r + lo + n + 1, :, :], src).then_inc(bias_rows_in, 16)
            sp.dma_start(sums_d.rearrange("(a p) w -> p a w", p=P),
                         zeros[:, :].unsqueeze(1).broadcast_to([P, TT, ACCW])).then_inc(sums_zero, 16)
            sp.wait_ge(k_part_ready, 3)
            sp.dma_start(k_parts_d.rearrange("a p t -> p a t"), k_part).then_inc(k_part_out, 16)
            sp.wait_ge(k_part_out, 16)
            for a in range(3):
                for b in range(3):
                    lo = BLK * a + BIAS_ROWS + DH * b
                    sp.dma_start(k_stack[lo:lo + DH, :, :],
                                 k_parts_d[b].rearrange("(g d) t -> d g t", g=KVH)).then_inc(k_rows_in, 16)
            for a in range(3):
                sp.wait_ge(q_part_ready, a + 1)
                sp.dma_start(q_parts_d[a], q_part[:, a, :]).then_inc(q_part_out[a], 16)
            for a in range(3):
                sp.wait_ge(q_part_out[a], 16)
            for g in range(KVH):
                for a in range(3):
                    for b in range(3):
                        lo = BLK * a + BIAS_ROWS + DH * b
                        sp.dma_start(q_stack[lo:lo + DH, G * g:G * (g + 1), :],
                                     q_parts_d[a, G * DH * g:G * DH * (g + 1), :].rearrange("(h d) t -> d h t", h=G)
                                     ).then_inc(q_rows_in[g], 16)
            sp.wait_ge(x_route_ready, 1)
            table_v = table_d.rearrange("(a p) w -> p a w", p=P)
            sp.dma_start(table_v[:, :, 0:D], x_route).then_inc(table_out, 16)
            sp.wait_ge(probs_ready, 1)
            sp.dma_start(table_v[:, :, D:TAB], probs[:, :, :]).then_inc(table_out, 16)
            for g in range(KVH):
                sp.wait_ge(max_rows_ready, g + 1)
                for n, r in enumerate((6, 7, BLK + 6)):
                    sp.dma_start(q_stack[r:r + 1, G * g:G * (g + 1), :].rearrange("o h (a b) -> o (h a) b", b=P),
                                 max_part[:, n, :]).then_inc(max_rows_in, 16)
            sp.wait_ge(turned_ps, NCH)
            sp.dma_start(fc2b, fc2b_d.rearrange("(o e) d -> o (e d)", o=1)).then_inc(fc2b_in, 16)
            sp.wait_ge(table_out, 32)
            for e in range(E0):
                if e >= 2:
                    sp.wait_ge(fc_turned, e - 1)
                sp.dma_start(fc1_raw[:, e % 2, :].rearrange("p (a d) -> p a d", a=FT),
                             fc1_d[e].rearrange("(a p) d -> p a d", p=P)).then_inc(fc_in[e % 2], 16)
                sp.dma_start(fc2_raw[:, e % 2, :], fc2_d[e]).then_inc(fc_in[e % 2], 16)
            sp.wait_ge(pv_done, len(quads))
            lay1_loads = [
                (Wrvk, Wrvk_d.rearrange("(a p) c -> p a c", p=P)), (Wout, Wout_d),
                (ws1, ws1_d), (w1, w1_d.rearrange("e d f -> d e f")),
                (ws2, ws2_d.rearrange("(a p) d -> p a d", p=P)), (w2, w2_d.rearrange("e (a p) d -> p (e a) d", p=P)),
            ]
            for dst, src in lay1_loads:
                sp.dma_start(dst, src).then_inc(lay1_in, 16)
            sp.wait_ge(scattered, 16 * E0)
            sp.dma_start(routeT[:, :].rearrange("p (a w) -> p a w", a=TT),
                         sums_d.rearrange("(a p) w -> p a w", p=P)).then_inc(sums_in, 16)
            out_v = out_d[0].rearrange("(a p) d -> p a d", p=P)
            for i in range(NCH):
                sp.wait_ge(x2_ready, i + 1)
                sp.dma_start(out_v[:, TPC * i:TPC * (i + 1), :], x[:, TPC * i:TPC * (i + 1), :]).then_inc(x2_out, 16)
            sp.wait_ge(x2_out, 16 * NCH)

        @block.gpsimd
        def _(pool):
            steps = [0]

            def link(ins):
                steps[0] += 1
                ins.then_inc(pool_step, 1)
                pool.wait_ge(pool_step, steps[0])

            pool.memset(one_zero[:, 0, :], 1.0)
            pool.memset(one_zero[:, 1, :], 0.0)
            pool.iota(j_rows[:, 0, :].rearrange("o (a b) -> o a b", a=TT), pattern=[[P, TT], [0, P]], base=0,
                      channel_multiplier=0, allow_small_or_imprecise_dtypes=True)
            pool.iota(j_rows[:, 1, :].rearrange("o (a b) -> o a b", a=TT), pattern=[[0, TT], [1, P]], base=0,
                      channel_multiplier=0, allow_small_or_imprecise_dtypes=True).then_inc(const_rows_ready, 1)
            link(pool.memset(ident[:, :], 0.0))
            pool.memset(hide_q[:, :], 0.0)
            pool.memset(ones_row[:, :], 1.0)
            pool.memset(zeros[:, :], 0.0)
            pool.memset(minus_half[:, :], -0.5)
            link(pool.memset(hide_k[:, :], 0.0))
            link(pool.affine_select(out=ident[:, :], in_=ident[:, :], compare_op=ALU.not_equal, fill=1.0, base=0,
                                    pattern=[[-1, P]], channel_multiplier=1))
            pool.affine_select(out=hide_q[:, :], in_=hide_q[:, :], compare_op=ALU.is_ge, fill=HIDDEN, base=0,
                               pattern=[[-1, P]], channel_multiplier=1)
            pool.affine_select(out=hide_k[:, :], in_=hide_k[:, :], compare_op=ALU.is_ge, fill=HIDDEN, base=0,
                               pattern=[[1, P]], channel_multiplier=-1)
            pool.iota(iota8[:, :], pattern=[[1, E1]], base=0, channel_multiplier=0, allow_small_or_imprecise_dtypes=True)
            pool.tensor_copy(ident_b[:, :], ident[:, :]).then_inc(consts_ready, 1)

            pool.iota(i_hi[:, :], pattern=[[P, TT]], base=0, channel_multiplier=0, allow_small_or_imprecise_dtypes=True)
            link(pool.iota(i_lo[:, :], pattern=[[1, P]], base=0, channel_multiplier=0,
                           allow_small_or_imprecise_dtypes=True))
            pool.wait_ge(slope_in, 16)
            link(pool.tensor_copy(slope_b[:, 0:1], slopes[:, :]))
            link(pool.tensor_tensor(slope_rest[:, 0:1], slopes[:, :], slope_b[:, 0:1], ALU.subtract))
            link(pool.tensor_copy(slope_b[:, 1:2], slope_rest[:, 0:1]))
            link(pool.tensor_tensor(slope_rest[:, 1:2], slope_rest[:, 0:1], slope_b[:, 1:2], ALU.subtract))
            link(pool.tensor_copy(slope_b[:, 2:3], slope_rest[:, 1:2]))
            link(pool.tensor_copy(slope_f[:, :], slope_b[:, :]))
            for a in range(3):
                s = slope_f[:, a:a + 1]
                pool.tensor_copy(sl_b[:, a, :], slope_b[:, a:a + 1].broadcast_to([H, P]))
                pool.tensor_scalar(hi_f[:, :], i_hi[:, :], s, -1.0, ALU.mult, ALU.mult)
                link(pool.tensor_scalar(lo_f[:, :], i_lo[:, :], s, -1.0, ALU.mult, ALU.mult))
                pool.tensor_copy(hi_b[:, 2 * a, :], hi_f[:, :])
                link(pool.tensor_copy(lo_b[:, 2 * a, :], lo_f[:, :]))
                pool.tensor_tensor(hi_b[:, 2 * a + 1, :], hi_f[:, :], hi_b[:, 2 * a, :], ALU.subtract)
                link(pool.tensor_tensor(lo_b[:, 2 * a + 1, :], lo_f[:, :], lo_b[:, 2 * a, :], ALU.subtract))
            pool.engine_nop().then_inc(bias_tables, 1)

            def inverse_root(out, in_, scale):
                link(pool.tensor_scalar(var_eps[:, :], in_, scale, EPS, ALU.mult, ALU.add))
                return pool.tensor_tensor(out, var_eps[:, :], minus_half[:, :], ALU.pow)

            pool.wait_ge(stats_ready, 1)
            inverse_root(rstd[:, :], mv[:, :, 1], 1.0).then_inc(rstd_ready, 1)

            for n in range(6):
                last = pool.tensor_copy(hi_w[:, n, :].rearrange("p (a b) -> p a b", a=TT),
                                        hi_b[:, n, :].unsqueeze(2).broadcast_to([H, TT, P]))
            last.then_inc(wide_ready, 1)

            pool.wait_ge(k_f_ready, NCH)
            link(pool.tensor_copy(k_part[:, 0, :], k_f))
            link(pool.tensor_tensor(k_rest, k_f, k_part[:, 0, :], ALU.subtract))
            link(pool.tensor_copy(k_part[:, 1, :], k_rest))
            link(pool.tensor_tensor(k_rest, k_rest, k_part[:, 1, :], ALU.subtract))
            pool.tensor_copy(k_part[:, 2, :], k_rest).then_inc(k_part_ready, 3)

            pool.wait_ge(sumsq_ready, 1)
            inverse_root(rrms[:, :], sumsq[:, :], 1.0 / D).then_inc(rrms_ready, 1)

            pool.wait_ge(token_of_ready, 1)
            pool.wait_ge(table_out, 32)
            pool.wait_ge(sums_zero, 16)

            def gather(e):
                if e >= 2:
                    pool.wait_ge(weighted_ready, e - 1)
                    pool.wait_ge(taken_turned, e - 1)
                pool.indirect_dma_start(
                    taken[:, e % 2, :], None, table_d,
                    bass.IndirectOffsetOnAxis(ap=token_of[:, e:e + 1], axis=0)).then_inc(taken_in[e % 2], 16)

            def scatter(e):
                pool.wait_ge(weighted_ready, e + 1)
                if e:
                    pool.wait_ge(scattered, 16 * e)
                pool.indirect_dma_start(
                    sums_d, bass.IndirectOffsetOnAxis(ap=token_of[:, e:e + 1], axis=0), weighted[:, e % 2, :], None,
                    compute_op=ALU.add).then_inc(scattered, 16)

            gather(0)
            for e in range(E0):
                if e + 1 < E0:
                    gather(e + 1)
                scatter(e)
            pool.wait_ge(stats_ready, 2)
            inverse_root(rstd[:, :], mv[:, :, 1], 1.0).then_inc(rstd_ready, 1)

        @block.scalar
        def _(act):
            steps = [0]

            def link(ins):
                steps[0] += 1
                ins.then_inc(act_step, 1)
                act.wait_ge(act_step, steps[0])

            act.wait_ge(bias_turned, 2)
            act.activation(hid_bias[:, :], bank[7][:, 0:hid_bias.shape[1]], ACT.Copy).then_inc(hid_bias_ready, 1)

            def evacuate_xnT(layer):
                for i in range(NCH):
                    act.wait_ge(turned_ps, NCH * layer + i + 1)
                    act.activation(xnT[:, QC * i:QC * (i + 1)], bank[i][:, :], ACT.Copy).then_inc(xnT_ready, 1)

            act.wait_ge(const_rows_out, 48)
            evacuate_xnT(0)
            act.wait_ge(bqs_ready, 1)
            act.wait_ge(bias_rows_in, 16 * 18)
            for i in range(NCH):
                act.wait_ge(q_ps, i + 1)
                act.activation(q_f[:, QC * i:QC * (i + 1)], bank[4 + i][:, :], ACT.Identity, bias=bqs[:, :],
                               scale=SCALE).then_inc(q_f_ready, 1)
            for i in range(NCH):
                act.wait_ge(k_ps, i + 1)
                act.activation(k_f[:, QC * i:QC * (i + 1)], bank[i][0:KVH * DH, :], ACT.Identity,
                               bias=bk[:, :]).then_inc(k_f_ready, 1)
            act.wait_ge(xn_ready, TT)
            for t in range(TT):
                last = act.activation(square_out[:, :], xn[:, t, :], ACT.Square, accum_out=sumsq[:, t:t + 1])
                if t < TT - 1:
                    link(last)
            last.then_inc(sumsq_ready, 1)
            act.wait_ge(shifted_ready, 1)
            act.activation(probs[:, :, :], probs[:, :, :], ACT.Exp).then_inc(exp0_ready, 1)
            act.wait_ge(logitsT_ps, 1)
            act.wait_ge(bias_rows_in, 16 * 18)
            for i in range(NCH):
                last = act.activation(routeT[0:E0, QC * i:QC * (i + 1)], bank[i][0:E0, :], ACT.Copy)
            last.then_inc(routeT_ready, 1)

            act.wait_ge(k_part_out, 16)
            act.wait_ge(q_part_out[0], 16)
            act.wait_ge(q_part_out[1], 16)
            act.wait_ge(q_part_out[2], 16)
            chunk_ends = [m for m, (g, c, kt) in enumerate(quads) if kt == TPC * (c + 1) - 1]
            out_n = 0
            for kind, n in order:
                if kind == "exp":
                    g, c, kt = quads[n // G]
                    lo = max(0, P * kt - QC * c)
                    act.wait_ge(exp_ps, n + 1)
                    if n >= NP:
                        act.wait_ge(pv_done, (n - NP) // G + 1)
                    act.activation(probsT[:, n % NP, lo:QC], bank[2 + n % 3][:, lo:QC], ACT.Exp
                                   ).then_inc(probsT_ready, 1)
                elif kind == "turn_out":
                    pass
                if kind == "pv" and n in chunk_ends:
                    act.wait_ge(pv_done, n + 1)
                    if out_n >= 2:
                        act.wait_ge(out_turned, out_n - 1)
                    act.activation(out_sb[:, out_n % 2, :], bank[5 + out_n % 2][:, :], ACT.Copy
                                   ).then_inc(out_sb_ready, 1)
                    out_n += 1

            for e in range(E0):
                act.wait_ge(fc_turned, e + 1)
                act.activation(fc1T[:, e % 2, :], bank[0][:, :], ACT.Copy)
                act.activation(fc2T[:, e % 2, :], bank[1][:, :], ACT.Copy).then_inc(fcT_ready, 1)
                act.wait_ge(hidden0_ps, e + 1)
                for a in range(FT):
                    last = act.activation(hidden0[:, e % 2, P * a:P * (a + 1)], bank[3][:, P * a:P * (a + 1)], ACT.Gelu,
                                          bias=hid_bias[:, FT * e + a:FT * e + a + 1])
                last.then_inc(hidden0_ready, 1)
            for i in range(NCH):
                act.wait_ge(attn_turned, i + 1)
                act.activation(attnT[:, QC * i:QC * (i + 1)], bank[i][:, :], ACT.Copy).then_inc(attnT_ready, 1)
            act.wait_ge(f0_ready, 1)
            act.activation(routeT[:, 0:T], routeT[:, 0:T], ACT.Silu).then_inc(silu0_ready, 1)

            evacuate_xnT(1)
            act.wait_ge(wT_ps, 1)
            act.activation(wT[:, :, :], bank[7][:, :], ACT.Copy).then_inc(wT_ready, 1)
            for n in range(3):
                for i in range(NCH):
                    act.wait_ge(rvk_ps, NCH * n + i + 1)
                    dst = (k_T, v_T, r_T)[n][:, QC * i:QC * (i + 1)]
                    act.activation(dst, bank[4 + i % 2][:, :], ACT.Sigmoid if n == 2 else ACT.Copy
                                   ).then_inc(rvk_ready, 1)
            act.wait_ge(decay_ready, 1)
            act.activation(w_col[:, :], decay[:, :], ACT.Exp).then_inc(w_ready, 1)
            act.wait_ge(gate_diff_ready, 1)
            act.activation(sm1[:, 1, :], sm1[:, 0, :], ACT.Exp).then_inc(gate_exp_ready, 1)
            for i in range(NCH):
                act.wait_ge(combine_turned, i + 1)
                act.activation(combineT[:, QC * i:QC * (i + 1)], bank[i][0:E1 + 1, :], ACT.Copy
                               ).then_inc(combineT_ready, 1)
            exps_at = 8
            for n, (e, c) in enumerate(units1):
                if n == exps_at:
                    act.wait_ge(exps_wanted, 1)
                    act.activation(old_w, old_w, ACT.Exp)
                    act.activation(new_w, new_w, ACT.Exp)
                    act.activation(keep_w, keep_w, ACT.Exp)
                    act.activation(add_w, add_w, ACT.Exp).then_inc(exps_ready, 1)
                for a in range(FT):
                    u = n * FT + a
                    act.wait_ge(hid1_ps, u + 1)
                    if n >= 2:
                        act.wait_ge(y1_ps, n - 1)
                    b = E0 * FT + e * FT + a
                    act.activation(hid1[:, u % NHS, :], bank[u % 4][:, :], ACT.Gelu, bias=hid_bias[:, b:b + 1]
                                   ).then_inc(hid1_ready, 1)
            act.wait_ge(y1_read, len(units1))
            act.activation(moe, moe, ACT.Silu).then_inc(silu1_ready, 1)

        @block.vector
        def _(dve):
            steps = [0]

            def link(ins):
                steps[0] += 1
                ins.then_inc(dve_step, 1)
                dve.wait_ge(dve_step, steps[0])

            def settle(s, n):
                dve.wait_ge(s, n)

            dve.memset(part_max[:, :, :, :, :], LOWEST)
            dve.memset(combine[:, :, :], 1.0)
            link(dve.memset(v_aug[:, :, :, :], 0.0))
            link(dve.memset(v_aug[:, :, :, DH:DH + 1], 1.0))

            def stats(layer):
                for t in range(TT):
                    if layer == 0 and t % TPC == 0:
                        dve.wait_ge(x_in[t // TPC], 16)
                    last = dve.bn_stats(bn[:, t, :], x[:, t, :])
                link(last)
                for t in range(TT):
                    last = dve.bn_aggr(mv[:, t, :], bn[:, t, :])
                last.then_inc(stats_ready, 1)
                dve.wait_ge(rstd_ready, layer + 1)
                for t in range(TT):
                    dve.tensor_scalar(xn[:, t, :], x[:, t, :], mv[:, t, 0:1], rstd[:, t:t + 1], ALU.subtract, ALU.mult
                                      ).then_inc(xn_ready, 1)

            def widen():
                dve.wait_ge(bias_tables, 1)
                for n in range(6):
                    dve.tensor_copy(lo_w[:, n, :].rearrange("p (a b) -> p a b", a=TT),
                                    lo_b[:, n, :].unsqueeze(1).broadcast_to([H, TT, P]))
                for n in range(3):
                    last = dve.tensor_copy(slope_w[:, n, :].rearrange("p (a b) -> p a b", a=TT),
                                           sl_b[:, n, :].unsqueeze(1).broadcast_to([H, TT, P]))
                last.then_inc(wide_ready, 1)

            stats(0)
            widen()
            dve.wait_ge(weights_in, 16 * 21)
            dve.tensor_scalar(bqs[:, :], bq[:, :], SCALE, None, ALU.mult).then_inc(bqs_ready, 1)
            dve.wait_ge(bias_turned, 1)
            dve.tensor_scalar(rwT[:, :], bank[6][:, 0:E0], nw_col[:, :], None, ALU.mult).then_inc(rwT_ready, 1)

            dve.wait_ge(q_f_ready, NCH)
            dve.tensor_copy(q_part[:, 0, :], q_f).then_inc(q_part_ready, 1)
            settle(q_part_ready, 1)
            link(dve.tensor_tensor(q_rest, q_f, q_part[:, 0, :], ALU.subtract))
            dve.tensor_copy(q_part[:, 1, :], q_rest).then_inc(q_part_ready, 1)
            settle(q_part_ready, 2)
            link(dve.tensor_tensor(q_rest, q_rest, q_part[:, 1, :], ALU.subtract))
            dve.tensor_copy(q_part[:, 2, :], q_rest).then_inc(q_part_ready, 1)

            dve.wait_ge(v_ps, 1)
            dve.tensor_tensor(v_aug[:, :, :, 0:DH], bank[4][:, :].rearrange("p (a g d) -> p a g d", a=TT, g=KVH),
                              bv_rows[:, :, :].unsqueeze(1).broadcast_to([P, TT, KVH, DH]), ALU.add
                              ).then_inc(v_ready, 1)
            over_tiles = lambda v, n: v.unsqueeze(2).broadcast_to([P, TT, n])
            dve.wait_ge(rrms_ready, 1)
            dve.wait_ge(route_ps, 1)
            link(dve.tensor_tensor(logits[:, :, :], bank[5][:, 0:TT * E0].rearrange("p (a e) -> p a e", a=TT),
                                   over_tiles(rrms[:, :], E0), ALU.mult))
            dve.tensor_tensor(logits[:, :, :], logits[:, :, :], rb_rows[:, :].unsqueeze(1).broadcast_to([P, TT, E0]),
                              ALU.add).then_inc(logits_ready, 1)
            settle(logits_ready, 1)
            dve.wait_ge(k_part_out, 16)
            link(dve.tensor_reduce(row_max[:, :], logits[:, :, :], AX.X, ALU.max))
            dve.tensor_tensor(probs[:, :, :], logits[:, :, :], over_tiles(row_max[:, :], E0), ALU.subtract
                              ).then_inc(shifted_ready, 1)
            for t in range(TT):
                last = dve.scalar_tensor_tensor(x_route[:, t, :], xn[:, t, :], rrms[:, t:t + 1], nw_rows[:, :],
                                                ALU.mult, ALU.mult)
            last.then_inc(x_route_ready, 1)
            dve.wait_ge(exp0_ready, 1)
            link(dve.tensor_reduce(row_sum[:, :], probs[:, :, :], AX.X, ALU.add))
            link(dve.reciprocal(row_sum[:, :], row_sum[:, :]))
            dve.tensor_tensor(probs[:, :, :], probs[:, :, :], over_tiles(row_sum[:, :], E0), ALU.mult
                              ).then_inc(probs_ready, 1)
            dve.wait_ge(routeT_ready, 1)
            routes = routeT[0:E0, 0:T]
            for r in range(CAP // 8):
                link(dve.max(top8[:, :], routes))
                dve.max_index(top_at[:, 8 * r:8 * (r + 1)], top8[:, :], routes)
                link(dve.match_replace(routes, top8[:, :], routes, LOWEST))
            dve.tensor_copy(top_at_f[:, :], top_at[:, :]).then_inc(top_ready, 1)
            dve.wait_ge(top_turned, 1)
            dve.tensor_copy(token_of[:, :], bank[7][:, 0:E0]).then_inc(token_of_ready, 1)

            for kind, n in order:
                if kind == "max":
                    g, j, qt, kc = max_units[n]
                    w = min(QC, P * (qt + 1) - QC * kc)
                    dve.wait_ge(max_ps, n + 1)
                    dve.reduce_max(part_max[:, g % 2, j, qt, kc:kc + 1], bank[n % 2][:, 0:w], AX.X).then_inc(max_read, 1)
                    if n % per_group == per_group - 1:
                        settle(max_read, n + 1)
                        dve.tensor_reduce(neg_max[:, g, :], part_max[:, g % 2, :, :, :].rearrange("p j t c -> p (j t) c"),
                                          AX.X, ALU.max, negate=True).then_inc(neg_max_ready, 1)
                elif kind == "turn_max":
                    dve.wait_ge(max_turned, n + 1)
                    if n:
                        dve.wait_ge(max_rows_in, 48 * n)
                    dve.tensor_copy(max_part[:, 0, :], bank[7][0:G * TT, 0:P])
                    link(dve.tensor_copy(max_rest[:, 0, :], bank[7][0:G * TT, 0:P]))
                    link(dve.tensor_tensor(max_rest[:, 0, :], max_rest[:, 0, :], max_part[:, 0, :], ALU.subtract))
                    link(dve.tensor_copy(max_part[:, 1, :], max_rest[:, 0, :]))
                    link(dve.tensor_tensor(max_rest[:, 1, :], max_rest[:, 0, :], max_part[:, 1, :], ALU.subtract))
                    dve.tensor_copy(max_part[:, 2, :], max_rest[:, 1, :]).then_inc(max_rows_ready, 1)
                    settle(max_rows_ready, n + 1)
                    dve.engine_nop().then_inc(turn_bank_read, 1)
                elif kind == "turn_out":
                    g, c = n // NCH, n % NCH
                    turned = bank[7][:, :].rearrange("p (a j r) -> p a j r", a=TPC, j=G)
                    dve.wait_ge(out_turned, n + 1)
                    link(dve.reciprocal(out_rec[:, :, :], turned[:, :, :, DH]))
                    tok = out_tok[:, TPC * c:TPC * (c + 1), G * DH * g:G * DH * (g + 1)]
                    dve.tensor_tensor(tok.rearrange("p a (j d) -> p a j d", j=G), turned[:, :, :, 0:DH],
                                      out_rec[:, :, :].unsqueeze(3).broadcast_to([P, TPC, G, DH]), ALU.mult
                                      ).then_inc(out_tok_ready, 1)
                    settle(out_tok_ready, n + 1)
                    dve.engine_nop().then_inc(turn_bank_read, 1)

            for e in range(E0):
                dve.wait_ge(taken_turned, e + 1)
                dve.tensor_copy(takenT[:, e % 2, :], bank[2][:, 0:CAP]).then_inc(takenT_ready, 1)
                dve.wait_ge(y0_ps, e + 1)
                if e >= 2:
                    dve.wait_ge(scattered, 16 * (e - 1))
                gate = taken[:, e % 2, D + e:D + e + 1]
                dve.tensor_copy(weighted[:, e % 2, D:D + 1], gate)
                dve.tensor_scalar(weighted[:, e % 2, 0:D], bank[4][:, 0:D], gate, None, ALU.mult
                                  ).then_inc(weighted_ready, 1)
            dve.wait_ge(sums_in, 16)
            sums = routeT[:, :].rearrange("p (a w) -> p a w", a=TT)
            link(dve.tensor_scalar(row_max[:, :], sums[:, :, D], 0.0, None, ALU.is_le))
            link(dve.tensor_tensor(row_sum[:, :], sums[:, :, D], row_max[:, :], ALU.add))
            link(dve.reciprocal(row_sum[:, :], row_sum[:, :]))
            f0 = xn
            link(dve.tensor_tensor(f0[:, :, :], sums[:, :, 0:D], over_tiles(row_sum[:, :], D), ALU.mult))
            dve.tensor_copy(routeT[:, 0:T], f0[:, :, :].rearrange("p a d -> p (a d)")).then_inc(f0_ready, 1)
            silu0 = routeT[:, 0:T].rearrange("p (a d) -> p a d", a=TT)
            dve.wait_ge(silu0_ready, 1)
            for i in range(NCH):
                ts = slice(TPC * i, TPC * (i + 1))
                dve.wait_ge(s0_ps, i + 1)
                dve.tensor_tensor(xn[:, ts, :], bank[4 + i][:, :].rearrange("p (a d) -> p a d", a=TPC),
                                  bo_rows[:, :].unsqueeze(1).broadcast_to([P, TPC, D]), ALU.add).then_inc(s0_read, 1)
                settle(s0_read, i + 1)
                link(dve.tensor_tensor(xn[:, ts, :], xn[:, ts, :], silu0[:, ts, :], ALU.mult))
                link(dve.tensor_tensor(x[:, ts, :], x[:, ts, :], xn[:, ts, :], ALU.add))

            stats(1)
            dve.memset(PP[:, 0:1], NEG_BIG)
            dve.memset(AA[:, 0:1], 0.0)
            link(dve.memset(BB[:, 0:1], 0.0))
            dve.tensor_copy(decay[:, :], decay[:, :]).then_inc(decay_ready, 1)
            dve.wait_ge(gate_ps, 1)
            link(dve.tensor_tensor(gates1[:, :, :], bank[6][:, 0:TT * E1].rearrange("p (a e) -> p a e", a=TT),
                                   gb_rows[:, :].unsqueeze(1).broadcast_to([P, TT, E1]), ALU.add))
            for t in range(TT):
                last = dve.max(top1[:, t, :], gates1[:, t, :])
            link(last)
            for t in range(TT):
                dve.max_index(top1_at[:, t, :], top1[:, t, :], gates1[:, t, :])
            dve.tensor_tensor(sm1[:, 0, :], top1[:, :, 1], top1[:, :, 0], ALU.subtract).then_inc(gate_diff_ready, 1)
            settle(gate_diff_ready, 1)
            for n in range(2):
                link(dve.tensor_copy(row_max[:, :], top1_at[:, :, n]))
                link(dve.tensor_tensor(hot[:, n, :, :], iota8[:, :].unsqueeze(1).broadcast_to([P, TT, E1]),
                                       over_tiles(row_max[:, :], E1), ALU.is_equal))
            dve.wait_ge(gate_exp_ready, 1)
            link(dve.tensor_scalar(sm1[:, 2, :], sm1[:, 1, :], 1.0, None, ALU.add))
            link(dve.reciprocal(sm1[:, 2, :], sm1[:, 2, :]))
            link(dve.tensor_tensor(sm1[:, 3, :], sm1[:, 1, :], sm1[:, 2, :], ALU.mult))
            link(dve.tensor_tensor(hot[:, 0, :, :], hot[:, 0, :, :], over_tiles(sm1[:, 2, :], E1), ALU.mult))
            link(dve.tensor_tensor(hot[:, 1, :, :], hot[:, 1, :, :], over_tiles(sm1[:, 3, :], E1), ALU.mult))
            dve.tensor_tensor(combine[:, :, 0:E1], hot[:, 0, :, :], hot[:, 1, :, :], ALU.add).then_inc(combine_ready, 1)
            settle(combine_ready, 1)
            for i in range(NCH):
                dve.wait_ge(moe_bias_ps, i + 1)
                dve.tensor_copy(moe[:, QC * i:QC * (i + 1)], bank[4 + i % 2][:, :]).then_inc(moe_bias_read, 1)
            settle(moe_bias_read, NCH)

            def wkv():
                dve.wait_ge(w_ready, 1)
                dve.wait_ge(rvk_ready, 3 * NCH)
                yield link(dve.tensor_scalar(w_col[:, :], w_col[:, :], -1.0, None, ALU.mult))
                yield link(dve.tensor_tensor_scan(PP[:, 1:T + 1], w_col[:, :].broadcast_to([P, T]), k_T, NEG_BIG,
                                                  ALU.add, ALU.max))
                yield link(dve.scalar_tensor_tensor(tmp, k_T, first[:, :], PP[:, 0:T], ALU.add, ALU.max))
                yield link(dve.tensor_tensor(old_w, PP[:, 0:T], tmp, ALU.subtract))
                yield link(dve.scalar_tensor_tensor(new_w, k_T, first[:, :], tmp, ALU.add, ALU.subtract))
                yield link(dve.scalar_tensor_tensor(keep_w, PP[:, 0:T], w_col[:, :], PP[:, 1:T + 1], ALU.add,
                                                    ALU.subtract))
                yield dve.tensor_tensor(add_w, k_T, PP[:, 1:T + 1], ALU.subtract).then_inc(exps_wanted, 1)
                yield dve.wait_ge(exps_ready, 1)
                yield link(dve.tensor_tensor(tmp, add_w, v_T, ALU.mult))
                yield link(dve.tensor_tensor_scan(AA[:, 1:T + 1], keep_w, tmp, 0.0, ALU.mult, ALU.add))
                yield link(dve.tensor_tensor_scan(BB[:, 1:T + 1], keep_w, add_w, 0.0, ALU.mult, ALU.add))
                yield link(dve.tensor_tensor(tmp, old_w, AA[:, 0:T], ALU.mult))
                yield link(dve.tensor_tensor(keep_w, new_w, v_T, ALU.mult))
                yield link(dve.tensor_tensor(tmp, tmp, keep_w, ALU.add))
                yield link(dve.tensor_tensor(tmp2, old_w, BB[:, 0:T], ALU.mult))
                yield link(dve.tensor_tensor(tmp2, tmp2, new_w, ALU.add))
                for i in range(NCH):
                    yield link(dve.reciprocal(tmp2[:, QC * i:QC * (i + 1)], tmp2[:, QC * i:QC * (i + 1)]))
                yield link(dve.tensor_tensor(tmp, tmp, tmp2, ALU.mult))
                yield dve.tensor_tensor(tmp, tmp, r_T, ALU.mult).then_inc(rwkv_ready, 1)

            mixing = wkv()
            for n, (e, c) in enumerate(units1):
                if n not in (7, 8, 9):
                    next(mixing, None)
                dve.wait_ge(y1_ps, n + 1)
                y = bank[4 + n % 2]
                for a in range(TPC):
                    t = TPC * c + a
                    s = combine[:, t, e:e + 1]
                    last = dve.scalar_tensor_tensor(moe_t[:, t, :], y[:, P * a:P * (a + 1)], s, moe_t[:, t, :],
                                                    ALU.mult, ALU.add)
                last.then_inc(y1_read, 1)
                settle(y1_read, n + 1)
            for _ in mixing:
                pass
            dve.wait_ge(silu1_ready, 1)
            for i in range(NCH):
                ts = slice(TPC * i, TPC * (i + 1))
                dve.wait_ge(s1_ps, i + 1)
                link(dve.tensor_tensor(xn[:, ts, :], bank[i][:, :].rearrange("p (a d) -> p a d", a=TPC),
                                       moe_t[:, ts, :], ALU.mult))
                dve.tensor_tensor(x[:, ts, :], x[:, ts, :], xn[:, ts, :], ALU.add).then_inc(x2_ready, 1)

        @block.tensor
        def _(pe):
            pe.wait_ge(consts_ready, 1)
            pe.wait_ge(weights_in, 16 * 21)
            pe.transpose(bank[6][:, 0:E0], rw[:, :], ident[0:E0, 0:E0]).then_inc(bias_turned, 1)
            nb = hid_bias_in.shape[0]
            pe.transpose(bank[7][:, 0:nb], hid_bias_in[:, :], ident[0:nb, 0:nb]).then_inc(bias_turned, 1)

            def turn_xn(layer):
                for i in range(NCH):
                    for a in range(TPC):
                        t = TPC * i + a
                        pe.wait_ge(xn_ready, TT * layer + t + 1)
                        last = pe.transpose(bank[i][:, P * a:P * (a + 1)], xn[:, t, :], ident[:, :])
                    last.then_inc(turned_ps, 1)

            turn_xn(0)
            pe.wait_ge(rwT_ready, 1)
            pe.wait_ge(hid_bias_ready, 1)
            for i in range(NCH):
                pe.wait_ge(xnT_ready, i + 1)
                pe.matmul(bank[4 + i][:, :], Wq[:, :], xnT[:, QC * i:QC * (i + 1)], start=True, stop=True
                          ).then_inc(q_ps, 1)
            for i in range(NCH):
                pe.matmul(bank[i][0:KVH * DH, :], Wk[:, :], xnT[:, QC * i:QC * (i + 1)], start=True, stop=True
                          ).then_inc(k_ps, 1)
            pe.wait_ge(q_f_ready, 1)
            for t in range(TT):
                last = pe.matmul(bank[4][:, 32 * t:32 * (t + 1)], xnT[:, P * t:P * (t + 1)], Wv[:, :],
                                 start=True, stop=True)
            last.then_inc(v_ps, 1)
            pe.wait_ge(q_f_ready, 2)
            for t in range(TT):
                last = pe.matmul(bank[5][:, E0 * t:E0 * (t + 1)], xnT[:, P * t:P * (t + 1)], rwT[:, :],
                                 start=True, stop=True)
            last.then_inc(route_ps, 1)
            pe.wait_ge(logits_ready, 1)
            pe.wait_ge(k_f_ready, NCH)
            for t in range(TT):
                last = pe.transpose(bank[t // TPC][0:E0, P * (t % TPC):P * (t % TPC + 1)], logits[:, t, :], ident[:, :])
            last.then_inc(logitsT_ps, 1)
            pe.wait_ge(top_ready, 1)
            pe.transpose(bank[7][:, 0:E0], top_at_f[:, :], ident[0:E0, 0:E0]).then_inc(top_turned, 1)

            pe.wait_ge(routeT_ready, 1)
            pe.wait_ge(token_of_ready, 1)
            pe.wait_ge(v_ready, 1)
            pe.wait_ge(bias_rows_in, 16 * 18)
            pe.wait_ge(k_rows_in, 16 * 18)
            turns = 0
            rows_ready = -1
            for kind, n in order:
                if kind == "max":
                    g, j, qt, kc = max_units[n]
                    if n % per_group == 0:
                        pe.wait_ge(q_rows_in[g], 16 * 9)
                    h, w = G * g + j, min(QC, P * (qt + 1) - QC * kc)
                    diagonal = kc == qt // TPC
                    if n >= 2:
                        pe.wait_ge(max_read, n - 1)
                    mm = pe.matmul(bank[n % 2][:, 0:w], q_stack[0:KROWS, h, P * qt:P * (qt + 1)],
                                   k_stack[0:KROWS, g, QC * kc:QC * kc + w], start=True, stop=True)
                    if diagonal:
                        mm = pe.matmul(bank[n % 2][:, w - P:w], ident_b[:, :], hide_q[:, :], start=False, stop=True,
                                       skip_group_check=True)
                    mm.then_inc(max_ps, 1)
                elif kind == "turn_max":
                    pe.wait_ge(neg_max_ready, n + 1)
                    pe.wait_ge(turn_bank_read, turns) if turns else None
                    turns += 1
                    pe.transpose(bank[7][0:G * TT, 0:P], neg_max[:, n, :], ident[:, :]).then_inc(max_turned, 1)
                elif kind == "exp":
                    m, j = n // G, n % G
                    g, c, kt = quads[m]
                    h, lo = G * g + j, max(0, P * kt - QC * c)
                    if g > rows_ready:
                        pe.wait_ge(max_rows_in, 48 * (g + 1))
                        rows_ready = g
                    if n >= 3:
                        pe.wait_ge(probsT_ready, n - 2)
                    diagonal = kt >= TPC * c
                    mm = pe.matmul(bank[2 + n % 3][:, lo:QC], k_stack[0:KROWS, g, P * kt:P * (kt + 1)],
                                   q_stack[0:KROWS, h, QC * c + lo:QC * (c + 1)], start=True, stop=True)
                    if diagonal:
                        mm = pe.matmul(bank[2 + n % 3][:, lo:lo + P], ident_b[:, :], hide_k[:, :], start=False,
                                       stop=True, skip_group_check=True)
                    mm.then_inc(exp_ps, 1)
                elif kind == "pv":
                    g, c, kt = quads[n]
                    ch, lo = g * NCH + c, max(0, P * kt - QC * c)
                    pe.wait_ge(probsT_ready, G * (n + 1))
                    if kt == 0 and ch >= 2:
                        pe.wait_ge(out_sb_ready, ch - 1)
                    for j in range(G):
                        mm = pe.matmul(bank[5 + ch % 2][BLK * j:BLK * (j + 1), lo:QC], v_aug[:, kt, g, :],
                                       probsT[:, (G * n + j) % NP, lo:QC], start=(kt == 0),
                                       stop=(kt == TPC * (c + 1) - 1))
                    mm.then_inc(pv_done, 1)
                elif kind == "turn_out":
                    pe.wait_ge(out_sb_ready, n + 1)
                    pe.wait_ge(turn_bank_read, turns) if turns else None
                    turns += 1
                    for a in range(TPC):
                        mm = pe.transpose(bank[7][:, P * a:P * (a + 1)], out_sb[:, n % 2, P * a:P * (a + 1)], ident[:, :])
                    mm.then_inc(out_turned, 1)

            pe.wait_ge(fc2b_in, 16)
            pe.wait_ge(max_read, len(max_units))
            pe.wait_ge(probsT_ready, G * len(quads))
            for e in range(E0):
                s = e % 2
                pe.wait_ge(fc_in[s], 32 * (e // 2 + 1))
                if e:
                    pe.wait_ge(fcT_ready, e)
                for a in range(FT):
                    pe.transpose(bank[0][:, P * a:P * (a + 1)], fc1_raw[:, s, P * a:P * (a + 1)], ident[:, :])
                for a in range(FT):
                    mm = pe.transpose(bank[1][:, P * a:P * (a + 1)], fc2_raw[:, s, P * a:P * (a + 1)], ident[:, :])
                mm.then_inc(fc_turned, 1)
                pe.wait_ge(taken_in[s], 16 * (e // 2 + 1))
                if e:
                    pe.wait_ge(takenT_ready, e)
                pe.transpose(bank[2][:, 0:CAP], taken[:, s, 0:D], ident[:, :]).then_inc(taken_turned, 1)
                pe.wait_ge(fcT_ready, e + 1)
                pe.wait_ge(takenT_ready, e + 1)
                if e:
                    pe.wait_ge(hidden0_ready, e)
                for a in range(FT):
                    mm = pe.matmul(bank[3][:, P * a:P * (a + 1)], fc1T[:, s, P * a:P * (a + 1)], takenT[:, s, :],
                                   start=True, stop=True)
                mm.then_inc(hidden0_ps, 1)
                pe.wait_ge(hidden0_ready, e + 1)
                if e:
                    pe.wait_ge(weighted_ready, e)
                pe.matmul(bank[4][:, 0:D], ones_row[:, :], fc2b[:, D * e:D * (e + 1)], start=True, stop=False)
                for a in range(FT):
                    mm = pe.matmul(bank[4][:, 0:D], hidden0[:, s, P * a:P * (a + 1)], fc2T[:, s, P * a:P * (a + 1)],
                                   start=False, stop=(a == FT - 1))
                mm.then_inc(y0_ps, 1)

            pe.wait_ge(out_tok_ready, KVH * NCH)
            pe.wait_ge(fcT_ready, E0)
            for i in range(NCH):
                for a in range(TPC):
                    mm = pe.transpose(bank[i][:, P * a:P * (a + 1)], out_tok[:, TPC * i + a, :], ident[:, :])
                mm.then_inc(attn_turned, 1)
            pe.wait_ge(weighted_ready, E0)
            pe.wait_ge(out_sb_ready, KVH * NCH)
            for i in range(NCH):
                pe.wait_ge(attnT_ready, i + 1)
                for a in range(TPC):
                    t = TPC * i + a
                    mm = pe.matmul(bank[4 + i][:, P * a:P * (a + 1)], attnT[:, P * t:P * (t + 1)], Wo[:, :],
                                   start=True, stop=True)
                mm.then_inc(s0_ps, 1)

            turn_xn(1)
            pe.wait_ge(lay1_in, 16 * 6)
            for n in range(4):
                src = Wrvk[:, n, :] if n < 3 else Wout
                mm = pe.transpose(bank[7][:, P * n:P * (n + 1)], src, ident[:, :])
            mm.then_inc(wT_ps, 1)
            pe.wait_ge(xnT_ready, 2 * NCH)
            for t in range(TT):
                mm = pe.matmul(bank[6][:, E1 * t:E1 * (t + 1)], xnT[:, P * t:P * (t + 1)], gw[:, :],
                               start=True, stop=True)
            mm.then_inc(gate_ps, 1)
            pe.wait_ge(wT_ready, 1)
            for n in range(3):
                for i in range(NCH):
                    u = NCH * n + i
                    if u >= 2:
                        pe.wait_ge(rvk_ready, u - 1)
                    pe.matmul(bank[4 + i % 2][:, :], wT[:, (2, 1, 0)[n], :], xnT[:, QC * i:QC * (i + 1)],
                              start=True, stop=True).then_inc(rvk_ps, 1)
            pe.wait_ge(combine_ready, 1)
            for i in range(NCH):
                for a in range(TPC):
                    t = TPC * i + a
                    mm = pe.transpose(bank[i][0:E1 + 1, P * a:P * (a + 1)], combine[:, t, :], ident[:, :])
                mm.then_inc(combine_turned, 1)
            pe.wait_ge(rvk_ready, 3 * NCH)
            for i in range(NCH):
                pe.wait_ge(combineT_ready, i + 1)
                if i >= 2:
                    pe.wait_ge(moe_bias_read, i - 1)
                for a in range(TPC):
                    t = TPC * i + a
                    mm = pe.matmul(bank[4 + i % 2][:, P * a:P * (a + 1)], combineT[:, P * t:P * (t + 1)], b2_all[:, :],
                                   start=True, stop=True)
                mm.then_inc(moe_bias_ps, 1)
            pe.wait_ge(moe_bias_read, NCH)

            def second(n):
                e, c = units1[n]
                w = w2[:, FT * e:FT * (e + 1), :] if e < E1 else ws2
                pe.wait_ge(hid1_ready, FT * (n + 1))
                if n >= 2:
                    pe.wait_ge(y1_read, n - 1)
                for t in range(TPC):
                    for a in range(FT):
                        mm = pe.matmul(bank[4 + n % 2][:, P * t:P * (t + 1)],
                                       hid1[:, (n * FT + a) % NHS, P * t:P * (t + 1)], w[:, a, :],
                                       start=(a == 0), stop=(a == FT - 1))
                mm.then_inc(y1_ps, 1)

            for n, (e, c) in enumerate(units1):
                w = w1[:, e, :] if e < E1 else ws1
                for a in range(FT):
                    u = n * FT + a
                    if u >= 4:
                        pe.wait_ge(hid1_ready, u - 3)
                    pe.matmul(bank[u % 4][:, :], w[:, P * a:P * (a + 1)], xnT[:, QC * c:QC * (c + 1)],
                              start=True, stop=True).then_inc(hid1_ps, 1)
                if n:
                    second(n - 1)
            second(len(units1) - 1)
            pe.wait_ge(rwkv_ready, 1)
            for i in range(NCH):
                for a in range(TPC):
                    t = TPC * i + a
                    mm = pe.matmul(bank[i][:, P * a:P * (a + 1)], tmp[:, P * t:P * (t + 1)], wT[:, 3, :],
                                   start=True, stop=True)
                mm.then_inc(s1_ps, 1)


_INS = ['L0_attn_qkv', 'L0_attn_Wq', 'L0_attn_bq', 'L0_attn_Wk', 'L0_attn_bk', 'L0_attn_Wv', 'L0_attn_bv', 'L0_attn_Wo',
        'L0_attn_bo', 'L0_attn_slopes', 'L0_ffn_norm_weight', 'L0_ffn_router_weight', 'L0_ffn_router_bias',
        'L0_ffn_fc1_weight', 'L0_ffn_fc1_bias', 'L0_ffn_fc2_weight', 'L0_ffn_fc2_bias', 'L1_attn_W_rvk',
        'L1_attn_W_out', 'L1_attn_time_decay', 'L1_attn_time_first', 'L1_ffn_gate_w', 'L1_ffn_gate_b', 'L1_ffn_w1',
        'L1_ffn_b1', 'L1_ffn_w2', 'L1_ffn_b2', 'L1_ffn_ws1', 'L1_ffn_bs1', 'L1_ffn_ws2', 'L1_ffn_bs2']
_OUTS = [((1, T, D), 'float32')]


def kernel(**inputs):
    import numpy as _np
    import concourse.bacc as _bacc
    from concourse import mybir as _mybir
    from concourse.bass_utils import run_bass_kernel_spmd as _run

    nc = _bacc.Bacc("TRN2", target_bir_lowering=False, num_devices=1)
    arrays, args = {}, []
    for name in _INS:
        a = _np.ascontiguousarray(inputs[name])
        arrays[f"in_{name}_dram"] = a
        args.append(nc.dram_tensor(f"in_{name}_dram", a.shape, _mybir.dt.from_np(a.dtype), kind="ExternalInput").ap())
    for i, (shape, dtype) in enumerate(_OUTS):
        dt = _mybir.dt.from_np(_np.dtype(dtype))
        args.append(nc.dram_tensor(f"out_{i}_dram", shape, dt, kind="ExternalOutput").ap())
    two_layers(nc, *args)
    r = _run(nc, [arrays], core_ids=[0])
    got = tuple(r.results[0][f"out_{i}_dram"] for i in range(len(_OUTS)))
    return got[0]
```

```python
import concourse.bass as bass
import numpy as np
from concourse import mybir
from contextlib import ExitStack

F32, BF16, U32 = mybir.dt.float32, mybir.dt.bfloat16, mybir.dt.uint32
ALU, ACT, AX = mybir.AluOpType, mybir.ActivationFunctionType, mybir.AxisListType

T, D, P = 2048, 128, 128
TT = T // P
QC = 512
NCH = T // QC
TPC = QC // P
EPS = 1e-5

H, KVH, DH = 16, 4, 8
G = H // KVH
SCALE = float(DH) ** -0.5
BLK = 32
BIAS_ROWS = 8
KROWS = 3 * BLK
HIDDEN = -1e30
E0, F0 = 16, 512
CAP = T // E0
FT = F0 // P
TAB = D + E0
ACCW = D + 1
E1, F1 = 8, 512
LOWEST = -3.0e38
BATCH = 4
ROUTE_AT, TOPK_FROM, TOPK_EVERY, EXPERT_STEPS = 8, 20, 4, 1
NEG_BIG = -1e38


def schedule():
    chunks = [(g, c) for g in range(KVH) for c in (range(NCH) if g % 2 == 0 else reversed(range(NCH)))]
    max_units, first_max = [], [0]
    quads = []
    for k, (g, c) in enumerate(chunks):
        max_units += [(k, j, a, kc) for j in range(G) for a in range(TPC) for kc in range(c + 1)]
        first_max.append(len(max_units))
        quads += [(k, kt) for kt in range(TPC * (c + 1))]
    n_chunks, n_max = len(chunks), len(max_units)
    order, side, done, turned = [], [], 0, 0
    late = []

    topk = [("topk", i) for i in range(3 * CAP // 8)]
    experts = [("gather", e) for e in range(BATCH)]
    for b in range(E0 // BATCH):
        es = range(BATCH * b, BATCH * (b + 1))
        for e in es:
            experts += [("fc1", e), ("take", e), ("hidden", e)]
        experts.append(("gelu", b))
        for e in es:
            experts += [("fc2", e), ("y", e), ("scatter", e)]
            if e + BATCH < E0:
                experts.append(("gather", e + BATCH))
    experts += [("wT", 0), ("f0", 0), ("silu0", 0)]
    free = {"gather", "scatter"}

    def emit_max(n):
        nonlocal done, turned
        for _ in range(min(n, n_max - done)):
            order.append(("max", done))
            done += 1
            if topk and done > TOPK_FROM and (done - TOPK_FROM) % TOPK_EVERY == 0:
                order.append(topk.pop(0))
                if not topk:
                    order.append(("token_of", 0))
            if done % 2 == 0 and 0 <= done - ROUTE_AT < 2 * NCH:
                order.append(("routeT", (done - ROUTE_AT) // 2))
            if turned < n_chunks and done == min(first_max[turned + 1] + 5, n_max):
                order.append(("turn_max", turned))
                turned += 1

    emit_max(first_max[1] + 12)
    n_exp = 0
    for m, (k, kt) in enumerate(quads):
        g, c = chunks[k]
        size = TPC * (c + 1)
        need = first_max[min(k + 2, n_chunks)] + 12
        if kt == 0:
            start_done = done
        for j in range(G):
            order.append(("exp", n_exp))
            n_exp += 1
            share = (kt * G + j + 1) / (size * G)
            emit_max(int(start_done + (need - start_done) * share) - done)
        if m:
            order.append(("pv", m - 1))
        for at, step in list(late):
            if at <= m:
                order.append(step)
                late.remove((at, step))
        if not topk and experts:
            for _ in range(EXPERT_STEPS):
                while experts and experts[0][0] in free:
                    order.append(experts.pop(0))
                if experts:
                    order.append(experts.pop(0))
        if kt == size - 1:
            late.append((m + 2, ("turn_out", k)))
            if g == KVH - 1:
                late += [(m + 3, ("attnT", c)), (m + 4, ("s0", c)), (m + 6, ("xn1", c))]
    order.append(("pv", len(quads) - 1))
    order += experts + [step for _, step in late]
    return chunks, max_units, quads, order


MAX_BANKS = (0, 1, 7)
SIDE = ("turn_max", "turn_out", "routeT", "token_of", "fc1", "take", "hidden", "fc2", "y", "wT", "attnT", "s0", "xn1")


def two_layers(nc, x_d, Wq_d, bq_d, Wk_d, bk_d, Wv_d, bv_d, Wo_d, bo_d, slopes_d, nw_d, rw_d, rb_d, fc1_d, fc1b_d,
               fc2_d, fc2b_d, Wrvk_d, Wout_d, decay_d, first_d, gw_d, gb_d, w1_d, b1_d, w2_d, b2_d, ws1_d, bs1_d,
               ws2_d, bs2_d, out_d):
    chunks, max_units, quads, order = schedule()
    side_at = {step: i + 1 for i, step in enumerate(s for s in order if s[0] in SIDE)}
    last_max = {max_units[n][0]: n for n in range(len(max_units))}
    last_quad = {k: m for m, (k, kt) in enumerate(quads)}
    NK = len(chunks)
    with ExitStack() as ctx:
        def sb(name, shape, dt=F32):
            return ctx.enter_context(nc.sbuf_tensor(name, shape, dt))

        def sem(name):
            return ctx.enter_context(nc.semaphore(name))

        def scratch(name, shape, dt=F32):
            return nc.dram_tensor(name, shape, dt, kind="Internal").ap()

        bank = [ctx.enter_context(nc.psum_tensor(f"bank{i}", [P, QC], F32)) for i in range(8)]

        q_parts_d = scratch("q_parts_d", (NCH, 3, D, QC), BF16)
        k_parts_d = scratch("k_parts_d", (3, KVH * DH, T), BF16)
        bias_d = scratch("bias_d", (NCH, 3, 6, H, QC), BF16)
        rows_d = scratch("rows_d", (4, T), BF16)
        table_d = scratch("table_d", (T, TAB))
        sums_d = scratch("sums_d", (T, ACCW))

        q_stack = sb("q_stack", [P, NCH, H, QC], BF16)
        k_stack = sb("k_stack", [P, KVH, T], BF16)
        x = sb("x", [P, TT, D])
        xn = sb("xn", [P, TT, D])
        xnT = sb("xnT", [P, T])
        v_aug = sb("v_aug", [P, TT, KVH, BLK])
        arena = sb("arena", [P, 16384])
        routeT = sb("routeT", [P, TT * ACCW])

        Wq = sb("Wq", [D, D])
        Wqp = sb("Wqp", [D, D])
        Wk = sb("Wk", [D, KVH * DH])
        Wv = sb("Wv", [D, KVH * DH])
        Wo = sb("Wo", [D, D])
        bq = sb("bq", [D, 1])
        bqs = sb("bqs", [D, 1])
        bk = sb("bk", [KVH * DH, 1])
        bv_rows = sb("bv_rows", [P, KVH, DH])
        bo_rows = sb("bo_rows", [P, D])
        nw_rows = sb("nw_rows", [P, D])
        nw_col = sb("nw_col", [D, 1])
        rw = sb("rw", [E0, D])
        rwT = sb("rwT", [D, E0])
        rb_rows = sb("rb_rows", [P, E0])
        slopes = sb("slopes", [H, 1])
        hid_bias_in = sb("hid_bias_in", [E0 * FT + E1 * FT + FT, P])
        hid_bias = sb("hid_bias", [P, E0 * FT + E1 * FT + FT])
        ident = sb("ident", [P, P])
        ident_b = sb("ident_b", [P, P], BF16)
        hide_q = sb("hide_q", [P, P], BF16)
        hide_k = sb("hide_k", [P, P], BF16)
        ones_row = sb("ones_row", [1, P])
        zeros = sb("zeros", [P, ACCW])
        bn = sb("bn", [P, TT, 6])
        mv = sb("mv", [P, TT, 2])
        var_eps = sb("var_eps", [P, TT])
        rstd = sb("rstd", [P, TT])
        minus_half = sb("minus_half", [P, TT])
        sumsq = sb("sumsq", [P, TT])
        rrms = sb("rrms", [P, TT])
        square_out = sb("square_out", [P, D])
        logits = sb("logits", [P, TT, E0])
        probs = sb("probs", [P, TT, E0])
        row_max = sb("row_max", [P, TT])
        row_sum = sb("row_sum", [P, TT])
        top8 = sb("top8", [E0, 8])
        top_at = sb("top_at", [E0, CAP], U32)
        top_at_f = sb("top_at_f", [E0, CAP])
        token_of = sb("token_of", [CAP, E0], U32)
        part_max = sb("part_max", [P, 3, G, TPC, NCH])
        neg_max = sb("neg_max", [P, 2, G * TPC])
        max_part = sb("max_part", [G * TPC, 2, 3, P], BF16)
        max_rest = sb("max_rest", [G * TPC, 2, P])
        out_rec = sb("out_rec", [P, TPC, G])
        gates1 = sb("gates1", [P, TT, E1])
        top1 = sb("top1", [P, TT, 8])
        top1_at = sb("top1_at", [P, TT, 8], U32)
        combine = sb("combine", [P, TT, E1 + 1])
        b2_all = sb("b2_all", [E1 + 1, D])
        gw = sb("gw", [D, E1])
        gb_rows = sb("gb_rows", [P, E1])
        decay = sb("decay", [D, 1])
        w_col = sb("w_col", [D, 1])
        first = sb("first", [D, 1])
        sm1 = sb("sm1", [P, 4, TT])
        hot = sb("hot", [P, 2, TT, E1])
        iota8 = sb("iota8", [P, E1])

        def part(lo, *shape):
            n = int(np.prod(shape))
            v = arena[:, lo:lo + n]
            return v if len(shape) == 1 else v.rearrange("p (a b) -> p a b", a=shape[0])

        q_f, q_rest = part(0, T), part(2048, T)
        q_part = arena[:, 4096:7168].bitcast(BF16).rearrange("p (a t) -> p a t", a=3)
        k_f, k_rest = arena[0:KVH * DH, 7168:9216], arena[0:KVH * DH, 9216:11264]
        k_part = arena[0:KVH * DH, 11264:14336].bitcast(BF16).rearrange("p (a t) -> p a t", a=3)
        x_route = part(14336, TT, D)
        wide = arena[0:H, 0:9216].bitcast(BF16).rearrange("p (i a n t) -> p i a n t", i=2, a=3, n=6)
        j_rows = xnT[0:1, :].bitcast(BF16).rearrange("p (a t) -> p a t", a=2)
        fc2b = xn[0:1, :, :].rearrange("p a d -> p (a d)")
        NP = 8
        probsT = part(0, NP, QC)
        out_tok = part(4096, TT, D)
        fc1_raw, fc2_raw = part(6144, 2, F0), part(7168, 2, F0)
        fc1T, fc2T = part(8192, F0), part(9216, F0)
        wrvk_raw, wout_raw = part(6144, 3, P), part(6528, P)
        out_sb = part(10240, 2, QC)
        taken = part(11264, BATCH, TAB)
        takenT = part(12416, CAP)
        hidden0 = part(12672, BATCH, F0)
        weighted = part(14720, 2, ACCW)
        attnT = part(12672, T)
        lay1 = q_stack[:, :, :, :].rearrange("p c h t -> p (c h t)").bitcast(F32)
        lay1k = k_stack[:, :, :].rearrange("p h t -> p (h t)").bitcast(F32)
        w1 = lay1[:, 0:4096].rearrange("p (e f) -> p e f", e=E1)
        w2 = lay1[:, 4096:8192].rearrange("p (e f) -> p e f", e=E1 * FT)
        ws1 = lay1[:, 8192:8704]
        ws2 = lay1[:, 8704:9216].rearrange("p (e f) -> p e f", e=FT)
        PP = lay1[:, 9216:9216 + T + 1]
        AA = lay1[:, 11272:11272 + T + 1]
        BB = lay1[:, 13328:13328 + T + 1]
        r_T, k_T = lay1k[:, 0:T], lay1k[:, T:2 * T]
        NHS = 8
        hid1 = part(0, NHS, QC)
        v_T = part(4096, T)
        keep_w, add_w = part(6144, T), part(8192, T)
        old_w, new_w = part(10240, T), part(12288, T)
        tmp = part(14336, T)
        combineT = tmp[0:E1 + 1, :]
        tmp2 = routeT[:, 0:T]
        moe = v_aug[:, :, :, :].rearrange("p a b c -> p (a b c)")
        moe_t = moe.rearrange("p (a b) -> p a b", a=TT)
        wT = sb("wT", [P, 4, P])

        slope_rest = sb("slope_rest", [H, 2])
        slope_b = sb("slope_b", [H, 3], BF16)
        slope_f = sb("slope_f", [H, 3])
        i_hi, hi_f = routeT[0:H, 0:TT], routeT[0:H, TT:2 * TT]
        i_lo, lo_f = routeT[0:H, 128:256], routeT[0:H, 256:384]
        hi_b = routeT[0:H, 384:432].bitcast(BF16).rearrange("p (a b) -> p a b", a=6)
        lo_b = routeT[0:H, 512:896].bitcast(BF16).rearrange("p (a b) -> p a b", a=6)

        one_zero = routeT[0:TT, 1088:1216].bitcast(BF16).rearrange("p (a b) -> p a b", a=2)

        x_in = [sem(f"x_in{i}") for i in range(NCH)]
        weights_in = sem("weights_in")
        consts_ready = sem("consts_ready")
        stats_ready = sem("stats_ready")
        rstd_ready = sem("rstd_ready")
        xn_ready = sem("xn_ready")
        turned_ps = sem("turned_ps")
        xnT_ready = sem("xnT_ready")
        bias_turned = sem("bias_turned")
        hid_bias_ready = sem("hid_bias_ready")
        rwT_ready = sem("rwT_ready")
        q_ps = sem("q_ps")
        q_f_ready = sem("q_f_ready")
        k_ps = sem("k_ps")
        k_f_ready = sem("k_f_ready")
        v_ps = sem("v_ps")
        v_ready = sem("v_ready")
        bqs_ready = sem("bqs_ready")
        route_ps = sem("route_ps")
        sumsq_ready = sem("sumsq_ready")
        rrms_ready = sem("rrms_ready")
        x_route_ready = sem("x_route_ready")
        logits_ready = sem("logits_ready")
        shifted_ready = sem("shifted_ready")
        exp0_ready = sem("exp0_ready")
        probs_ready = sem("probs_ready")
        q_part_ready = sem("q_part_ready")
        k_part_ready = sem("k_part_ready")
        q_part_out = sem("q_part_out")
        k_part_out = sem("k_part_out")
        const_rows_ready = sem("const_rows_ready")
        const_rows_out = sem("const_rows_out")
        bias_tables = sem("bias_tables")
        wide_ready = sem("wide_ready")
        bias_out = [sem(f"bias_out{i}") for i in range(2)]
        slope_in = sem("slope_in")
        bias_rows_in = sem("bias_rows_in")
        k_rows_in = sem("k_rows_in")
        q_rows_in = [sem(f"q_rows_in{c}") for c in range(NCH)]
        table_out = sem("table_out")
        sums_zero = sem("sums_zero")
        max_ps = sem("max_ps")
        max_read = sem("max_read")
        neg_max_ready = sem("neg_max_ready")
        max_rows_in = [sem(f"max_rows_in{i}") for i in range(2)]
        exp_ps = sem("exp_ps")
        probsT_ready = sem("probsT_ready")
        pv_done = sem("pv_done")
        out_sb_ready = sem("out_sb_ready")
        top_ready = sem("top_ready")
        side_ps = sem("side_ps")
        side_read = sem("side_read")
        fc1_in = [sem(f"fc1_in{i}") for i in range(2)]
        fc2_in = [sem(f"fc2_in{i}") for i in range(2)]
        fc2b_in = sem("fc2b_in")
        taken_in = [sem(f"taken_in{i}") for i in range(BATCH)]
        gelu0_ready = sem("gelu0_ready")
        scattered = sem("scattered")
        sums_in = sem("sums_in")
        f0_ready = sem("f0_ready")
        silu0_ready = sem("silu0_ready")
        x1_ready = sem("x1_ready")
        lay1_in = sem("lay1_in")
        wT_in = sem("wT_in")
        rvk_ps = sem("rvk_ps")
        rvk_ready = sem("rvk_ready")
        gate_ps = sem("gate_ps")
        gate_diff_ready = sem("gate_diff_ready")
        gate_exp_ready = sem("gate_exp_ready")
        combine_ready = sem("combine_ready")
        combine_turned = sem("combine_turned")
        combineT_ready = sem("combineT_ready")
        moe_bias_ps = sem("moe_bias_ps")
        moe_bias_read = sem("moe_bias_read")
        hid1_ps = sem("hid1_ps")
        hid1_ready = sem("hid1_ready")
        y1_ps = sem("y1_ps")
        y1_read = sem("y1_read")
        decay_ready = sem("decay_ready")
        w_ready = sem("w_ready")
        exps_wanted = sem("exps_wanted")
        exps_ready = sem("exps_ready")
        rwkv_ready = sem("rwkv_ready")
        s1_ps = sem("s1_ps")
        silu1_ready = sem("silu1_ready")
        x2_ready = sem("x2_ready")
        x2_out = sem("x2_out")
        dve_step = sem("dve_step")
        pool_step = sem("pool_step")
        act_step = sem("act_step")

        block = ctx.enter_context(nc.Block())
        units1 = [(e, c) for e in range(E1 + 1) for c in range(NCH)]
        N_WEIGHTS = 28

        @block.sync
        def _(sp):
            x_v = x_d[0].rearrange("(a p) d -> p a d", p=P)
            for i in range(NCH):
                sp.dma_start(x[:, TPC * i:TPC * (i + 1), :], x_v[:, TPC * i:TPC * (i + 1), :]).then_inc(x_in[i], 16)
            col = lambda v: v.rearrange("(p a) -> p a", a=1)
            row = lambda v: v.rearrange("(a p) -> a p", a=1)
            sp.dma_start(slopes[:, :], col(slopes_d)).then_inc(slope_in, 16)
            NB = E0 * FT
            loads = [
                (Wq[:, :], Wq_d), (Wk[:, :], Wk_d), (Wv[:, :], Wv_d), (Wo[:, :], Wo_d),
                (bk[:, :], col(bk_d)), (nw_col[:, :], col(nw_d)),
                (bv_rows[:, :, :], bv_d.rearrange("(a k d) -> a k d", a=1, k=KVH).broadcast_to([P, KVH, DH])),
                (bo_rows[:, :], row(bo_d).broadcast_to([P, D])), (nw_rows[:, :], row(nw_d).broadcast_to([P, D])),
                (rw[:, :], rw_d), (rb_rows[:, :], row(rb_d).broadcast_to([P, E0])),
                (hid_bias_in[0:NB, :], fc1b_d.rearrange("e (a p) -> (e a) p", p=P)),
                (hid_bias_in[NB:NB + E1 * FT, :], b1_d.rearrange("e (a p) -> (e a) p", p=P)),
                (hid_bias_in[NB + E1 * FT:NB + E1 * FT + FT, :], bs1_d.rearrange("(a p) -> a p", p=P)),
                (gw[:, :], gw_d), (gb_rows[:, :], row(gb_d).broadcast_to([P, E1])),
                (b2_all[0:E1, :], b2_d), (b2_all[E1:E1 + 1, :], row(bs2_d)),
                (decay[:, :], col(decay_d)), (first[:, :], col(first_d)),
            ]
            assert len(loads) == 20
            for dst, src in loads:
                sp.dma_start(dst, src).then_inc(weights_in, 16)
            sp.dma_start(bq[:, :], bq_d.rearrange("(h d) -> d h", h=H), allow_slow_non_contiguous=True
                         ).then_inc(weights_in, 16)
            sp.wait_ge(const_rows_ready, 1)
            sp.dma_start(rows_d[0:2, :].rearrange("(o a) t -> o a t", o=1), j_rows).then_inc(const_rows_out, 16)
            for n in range(2):
                sp.dma_start(rows_d[2 + n].rearrange("(a b) -> a b", a=TT), one_zero[:, n, :]).then_inc(const_rows_out, 16)
            sp.wait_ge(const_rows_out, 48)
            for a in range(3):
                r = BLK * a
                sp.dma_start(k_stack[r:r + 2, :, :], rows_d[0:2, :].unsqueeze(1).broadcast_to([2, KVH, T])
                             ).then_inc(k_rows_in, 16)
                sp.dma_start(k_stack[r + 2:r + 8, :, :],
                             rows_d[2:3, :].unsqueeze(1).broadcast_to([6, KVH, T])).then_inc(k_rows_in, 16)
                sp.dma_start(q_stack[r + 6:r + 8, :, :, :].rearrange("r c h t -> r (c h) t"),
                             rows_d[3:4, 0:QC].unsqueeze(1).broadcast_to([2, NCH * H, QC])).then_inc(k_rows_in, 16)
            for c in range(NCH):
                sp.wait_ge(wide_ready, c + 1)
                sp.dma_start(bias_d[c].rearrange("a n h t -> h (a n) t"),
                             wide[:, c % 2, :, :, :].rearrange("h a n t -> h (a n) t")).then_inc(bias_out[c % 2], 16)
            for c in range(NCH):
                sp.wait_ge(bias_out[c % 2], 16 * (c // 2 + 1))
                for a in range(3):
                    r = BLK * a
                    sp.dma_start(q_stack[r:r + 6, c, :, :].rearrange("n h t -> n (h t)"),
                                 bias_d[c, a].rearrange("n h t -> n (h t)")).then_inc(bias_rows_in, 16)
            sp.dma_start(sums_d.rearrange("(a p) w -> p a w", p=P),
                         zeros[:, :].unsqueeze(1).broadcast_to([P, TT, ACCW])).then_inc(sums_zero, 16)
            sp.wait_ge(k_part_ready, 3)
            sp.dma_start(k_parts_d.rearrange("a p t -> p a t"), k_part).then_inc(k_part_out, 16)
            sp.wait_ge(k_part_out, 16)
            for a in range(3):
                for b in range(3):
                    lo = BLK * a + BIAS_ROWS + DH * b
                    sp.dma_start(k_stack[lo:lo + DH, :, :],
                                 k_parts_d[b].rearrange("(g d) t -> d g t", g=KVH)).then_inc(k_rows_in, 16)
            sp.wait_ge(q_part_ready, 3)
            for c in range(NCH):
                sp.dma_start(q_parts_d[c].rearrange("a p t -> p a t"), q_part[:, :, QC * c:QC * (c + 1)]
                             ).then_inc(q_part_out, 16)
            sp.wait_ge(q_part_out, 16 * NCH)
            for c in range(NCH):
                for a in range(3):
                    for b in range(3):
                        lo = BLK * a + BIAS_ROWS + DH * b
                        sp.dma_start(q_stack[lo:lo + DH, c, :, :].rearrange("d h t -> d (h t)"),
                                     q_parts_d[c, a].rearrange("(d h) t -> d (h t)", h=H)).then_inc(q_rows_in[c], 16)
            sp.wait_ge(x_route_ready, 1)
            table_v = table_d.rearrange("(a p) w -> p a w", p=P)
            sp.dma_start(table_v[:, :, 0:D], x_route).then_inc(table_out, 16)
            sp.wait_ge(probs_ready, 1)
            sp.dma_start(table_v[:, :, D:TAB], probs[:, :, :]).then_inc(table_out, 16)
            sp.wait_ge(turned_ps, NCH)
            sp.dma_start(fc2b, fc2b_d.rearrange("(o e) d -> o (e d)", o=1)).then_inc(fc2b_in, 16)
            sp.wait_ge(table_out, 32)

            def load_fc1(e):
                sp.dma_start(fc1_raw[:, e % 2, :].rearrange("p (a d) -> p a d", a=FT),
                             fc1_d[e].rearrange("(a p) d -> p a d", p=P)).then_inc(fc1_in[e % 2], 16)

            def load_fc2(e):
                sp.dma_start(fc2_raw[:, e % 2, :], fc2_d[e]).then_inc(fc2_in[e % 2], 16)

            for e in range(2):
                load_fc1(e)
                load_fc2(e)
            for kind, n in order:
                if kind == "turn_max":
                    g, c = chunks[n]
                    sp.wait_ge(side_read, side_at[kind, n])
                    for i, r in enumerate((6, 7, BLK + 6)):
                        sp.dma_start(q_stack[r:r + 1, c, G * g:G * (g + 1), :].rearrange("o h (a b) -> o (h a) b", b=P),
                                     max_part[:, n % 2, i, :]).then_inc(max_rows_in[n % 2], 16)
                elif kind == "fc1" and n + 2 < E0:
                    sp.wait_ge(side_ps, side_at[kind, n])
                    load_fc1(n + 2)
                elif kind == "fc2" and n + 2 < E0:
                    sp.wait_ge(side_ps, side_at[kind, n])
                    load_fc2(n + 2)
                elif kind == "y" and n == E0 - 1:
                    sp.dma_start(wrvk_raw, Wrvk_d.rearrange("(a p) c -> p a c", p=P)).then_inc(wT_in, 16)
                    sp.dma_start(wout_raw, Wout_d).then_inc(wT_in, 16)
                elif kind == "f0":
                    sp.wait_ge(scattered, 16 * E0)
                    sp.dma_start(routeT[:, :].rearrange("p (a w) -> p a w", a=TT),
                                 sums_d.rearrange("(a p) w -> p a w", p=P)).then_inc(sums_in, 16)
            sp.wait_ge(pv_done, len(quads))
            lay1_loads = [
                (ws1, ws1_d), (w1, w1_d.rearrange("e d f -> d e f")),
                (ws2, ws2_d.rearrange("(a p) d -> p a d", p=P)), (w2, w2_d.rearrange("e (a p) d -> p (e a) d", p=P)),
            ]
            for dst, src in lay1_loads:
                sp.dma_start(dst, src).then_inc(lay1_in, 16)
            out_v = out_d[0].rearrange("(a p) d -> p a d", p=P)
            for i in range(NCH):
                sp.wait_ge(x2_ready, i + 1)
                sp.dma_start(out_v[:, TPC * i:TPC * (i + 1), :], x[:, TPC * i:TPC * (i + 1), :]).then_inc(x2_out, 16)
            sp.wait_ge(x2_out, 16 * NCH)

        @block.gpsimd
        def _(pool):
            steps = [0]

            def link(ins):
                steps[0] += 1
                ins.then_inc(pool_step, 1)
                pool.wait_ge(pool_step, steps[0])

            pool.memset(one_zero[:, 0, :], 1.0)
            pool.memset(one_zero[:, 1, :], 0.0)
            pool.iota(j_rows[:, 0, :].rearrange("o (a b) -> o a b", a=TT), pattern=[[P, TT], [0, P]], base=0,
                      channel_multiplier=0, allow_small_or_imprecise_dtypes=True)
            pool.iota(j_rows[:, 1, :].rearrange("o (a b) -> o a b", a=TT), pattern=[[0, TT], [1, P]], base=0,
                      channel_multiplier=0, allow_small_or_imprecise_dtypes=True).then_inc(const_rows_ready, 1)
            link(pool.memset(ident[:, :], 0.0))
            pool.memset(hide_q[:, :], 0.0)
            pool.memset(ones_row[:, :], 1.0)
            pool.memset(zeros[:, :], 0.0)
            pool.memset(minus_half[:, :], -0.5)
            link(pool.memset(hide_k[:, :], 0.0))
            link(pool.affine_select(out=ident[:, :], in_=ident[:, :], compare_op=ALU.not_equal, fill=1.0, base=0,
                                    pattern=[[-1, P]], channel_multiplier=1))
            pool.affine_select(out=hide_q[:, :], in_=hide_q[:, :], compare_op=ALU.is_ge, fill=HIDDEN, base=0,
                               pattern=[[-1, P]], channel_multiplier=1)
            pool.affine_select(out=hide_k[:, :], in_=hide_k[:, :], compare_op=ALU.is_ge, fill=HIDDEN, base=0,
                               pattern=[[1, P]], channel_multiplier=-1)
            pool.iota(iota8[:, :], pattern=[[1, E1]], base=0, channel_multiplier=0, allow_small_or_imprecise_dtypes=True)
            pool.tensor_copy(ident_b[:, :], ident[:, :]).then_inc(consts_ready, 1)

            pool.iota(i_hi[:, :], pattern=[[P, TT]], base=0, channel_multiplier=0, allow_small_or_imprecise_dtypes=True)
            link(pool.iota(i_lo[:, :], pattern=[[1, P]], base=0, channel_multiplier=0,
                           allow_small_or_imprecise_dtypes=True))
            pool.wait_ge(slope_in, 16)
            link(pool.tensor_copy(slope_b[:, 0:1], slopes[:, :]))
            link(pool.tensor_tensor(slope_rest[:, 0:1], slopes[:, :], slope_b[:, 0:1], ALU.subtract))
            link(pool.tensor_copy(slope_b[:, 1:2], slope_rest[:, 0:1]))
            link(pool.tensor_tensor(slope_rest[:, 1:2], slope_rest[:, 0:1], slope_b[:, 1:2], ALU.subtract))
            link(pool.tensor_copy(slope_b[:, 2:3], slope_rest[:, 1:2]))
            link(pool.tensor_copy(slope_f[:, :], slope_b[:, :]))
            for a in range(3):
                s = slope_f[:, a:a + 1]
                pool.tensor_scalar(hi_f[:, :], i_hi[:, :], s, -1.0, ALU.mult, ALU.mult)
                link(pool.tensor_scalar(lo_f[:, :], i_lo[:, :], s, -1.0, ALU.mult, ALU.mult))
                pool.tensor_copy(hi_b[:, 2 * a, :], hi_f[:, :])
                link(pool.tensor_copy(lo_b[:, 2 * a, :], lo_f[:, :]))
                pool.tensor_tensor(hi_b[:, 2 * a + 1, :], hi_f[:, :], hi_b[:, 2 * a, :], ALU.subtract)
                link(pool.tensor_tensor(lo_b[:, 2 * a + 1, :], lo_f[:, :], lo_b[:, 2 * a, :], ALU.subtract))
            pool.engine_nop().then_inc(bias_tables, 1)

            def inverse_root(out, in_, scale):
                n = in_.shape[1]
                link(pool.tensor_scalar(var_eps[:, 0:n], in_, scale, EPS, ALU.mult, ALU.add))
                return pool.tensor_tensor(out, var_eps[:, 0:n], minus_half[:, 0:n], ALU.pow)

            pool.wait_ge(stats_ready, 1)
            inverse_root(rstd[:, :], mv[:, :, 1], 1.0).then_inc(rstd_ready, 1)

            pool.wait_ge(k_f_ready, NCH)
            link(pool.tensor_copy(k_part[:, 0, :], k_f))
            link(pool.tensor_tensor(k_rest, k_f, k_part[:, 0, :], ALU.subtract))
            link(pool.tensor_copy(k_part[:, 1, :], k_rest))
            link(pool.tensor_tensor(k_rest, k_rest, k_part[:, 1, :], ALU.subtract))
            pool.tensor_copy(k_part[:, 2, :], k_rest).then_inc(k_part_ready, 3)

            pool.wait_ge(sumsq_ready, 1)
            inverse_root(rrms[:, :], sumsq[:, :], 1.0 / D).then_inc(rrms_ready, 1)

            pool.wait_ge(table_out, 32)
            pool.wait_ge(sums_zero, 16)
            for kind, n in order:
                if kind == "gather":
                    pool.wait_ge(side_read, side_at["token_of", 0] if n < BATCH else side_at["y", n - BATCH])
                    pool.indirect_dma_start(
                        taken[:, n % BATCH, :], None, table_d,
                        bass.IndirectOffsetOnAxis(ap=token_of[:, n:n + 1], axis=0)).then_inc(taken_in[n % BATCH], 16)
                elif kind == "scatter":
                    pool.wait_ge(side_read, side_at["y", n])
                    if n:
                        pool.wait_ge(scattered, 16 * n)
                    pool.indirect_dma_start(
                        sums_d, bass.IndirectOffsetOnAxis(ap=token_of[:, n:n + 1], axis=0), weighted[:, n % 2, :], None,
                        compute_op=ALU.add).then_inc(scattered, 16)
                elif kind == "s0":
                    ts = slice(TPC * n, TPC * (n + 1))
                    pool.wait_ge(stats_ready, 1 + NCH - n)
                    inverse_root(rstd[:, ts], mv[:, ts, 1], 1.0).then_inc(rstd_ready, 1)

        @block.scalar
        def _(act):
            steps = [0]

            def link(ins):
                steps[0] += 1
                ins.then_inc(act_step, 1)
                act.wait_ge(act_step, steps[0])

            act.wait_ge(bias_turned, 2)
            act.activation(hid_bias[:, :], bank[7][:, 0:hid_bias.shape[1]], ACT.Copy).then_inc(hid_bias_ready, 1)

            def evacuate_xnT():
                for i in range(NCH):
                    act.wait_ge(turned_ps, i + 1)
                    act.activation(xnT[:, QC * i:QC * (i + 1)], bank[i][:, :], ACT.Copy).then_inc(xnT_ready, 1)

            act.wait_ge(bias_tables, 1)
            for c in range(NCH):
                table = wide[:, c % 2, :, :, :]
                if c < 2:
                    act.activation(table[:, :, 0:2, :],
                                   slope_b[:, :].unsqueeze(2).unsqueeze(3).broadcast_to([H, 3, 2, QC]), ACT.Copy)
                    for a in range(3):
                        act.activation(table[:, a, 4:6, :].rearrange("h n (i t) -> h n i t", i=TPC),
                                       lo_b[:, 2 * a:2 * a + 2, :].unsqueeze(2).broadcast_to([H, 2, TPC, P]), ACT.Copy)
                else:
                    act.wait_ge(bias_out[c % 2], 16)
                for a in range(3):
                    last = act.activation(
                        table[:, a, 2:4, :].rearrange("h n (i t) -> h n i t", i=TPC),
                        hi_b[:, 2 * a:2 * a + 2, TPC * c:TPC * (c + 1)].unsqueeze(3).broadcast_to([H, 2, TPC, P]),
                        ACT.Copy)
                last.then_inc(wide_ready, 1)

            act.wait_ge(const_rows_out, 48)
            evacuate_xnT()
            act.wait_ge(bqs_ready, 1)
            act.wait_ge(bias_out[0], 32)
            act.wait_ge(bias_out[1], 32)
            for i in range(NCH):
                act.wait_ge(q_ps, i + 1)
                act.activation(q_f[:, QC * i:QC * (i + 1)], bank[4 + i][:, :], ACT.Identity, bias=bqs[:, :],
                               scale=SCALE).then_inc(q_f_ready, 1)
            for i in range(NCH):
                act.wait_ge(k_ps, i + 1)
                act.activation(k_f[:, QC * i:QC * (i + 1)], bank[i][0:KVH * DH, :], ACT.Identity,
                               bias=bk[:, :]).then_inc(k_f_ready, 1)
            act.wait_ge(xn_ready, TT)
            for t in range(TT):
                last = act.activation(square_out[:, :], xn[:, t, :], ACT.Square, accum_out=sumsq[:, t:t + 1])
                if t < TT - 1:
                    link(last)
            last.then_inc(sumsq_ready, 1)
            act.wait_ge(shifted_ready, 1)
            act.activation(probs[:, :, :], probs[:, :, :], ACT.Exp).then_inc(exp0_ready, 1)
            act.wait_ge(k_part_out, 16)
            act.wait_ge(q_part_out, 16 * NCH)

            def evacuate(kind, n, out, in_):
                act.wait_ge(side_ps, side_at[kind, n])
                act.activation(out, in_, ACT.Copy).then_inc(side_read, 1)

            for kind, n in order:
                if kind == "exp":
                    k, kt = quads[n // G]
                    lo = max(0, P * kt - QC * chunks[k][1])
                    act.wait_ge(exp_ps, n + 1)
                    if n >= NP:
                        act.wait_ge(pv_done, (n - NP) // G + 1)
                    act.activation(probsT[:, n % NP, lo:QC], bank[2 + n % 3][:, lo:QC], ACT.Exp
                                   ).then_inc(probsT_ready, 1)
                elif kind == "pv" and n == last_quad[quads[n][0]]:
                    k = quads[n][0]
                    act.wait_ge(pv_done, n + 1)
                    if k >= 2:
                        act.wait_ge(side_ps, side_at["turn_out", k - 2])
                    act.activation(out_sb[:, k % 2, :], bank[5][:, :], ACT.Copy).then_inc(out_sb_ready, 1)
                elif kind == "routeT":
                    evacuate(kind, n, routeT[0:E0, QC * n:QC * (n + 1)], bank[6][0:E0, :])
                elif kind == "fc1":
                    evacuate(kind, n, fc1T, bank[6][:, :])
                elif kind == "fc2":
                    evacuate(kind, n, fc2T, bank[6][:, :])
                elif kind == "take":
                    evacuate(kind, n, takenT, bank[6][:, 0:CAP])
                elif kind == "gelu":
                    act.wait_ge(side_read, side_at["hidden", BATCH * (n + 1) - 1])
                    act.activation(hidden0, hidden0, ACT.Gelu).then_inc(gelu0_ready, 1)
                elif kind == "silu0":
                    act.wait_ge(f0_ready, 1)
                    act.activation(routeT[:, 0:T], xn[:, :, :].rearrange("p a d -> p (a d)"), ACT.Silu
                                   ).then_inc(silu0_ready, 1)
                elif kind == "wT":
                    evacuate(kind, n, wT[:, :, :].rearrange("p a d -> p (a d)"), bank[6][:, :])
                elif kind == "attnT":
                    evacuate(kind, n, attnT[:, QC * n:QC * (n + 1)], bank[6][:, :])
                elif kind == "xn1":
                    evacuate(kind, n, xnT[:, QC * n:QC * (n + 1)], bank[6][:, :])

            for n in range(3):
                for i in range(NCH):
                    act.wait_ge(rvk_ps, NCH * n + i + 1)
                    dst = (k_T, v_T, r_T)[n][:, QC * i:QC * (i + 1)]
                    act.activation(dst, bank[4 + i % 2][:, :], ACT.Sigmoid if n == 2 else ACT.Copy
                                   ).then_inc(rvk_ready, 1)
            act.wait_ge(decay_ready, 1)
            act.activation(w_col[:, :], decay[:, :], ACT.Exp).then_inc(w_ready, 1)
            act.wait_ge(gate_diff_ready, 1)
            act.activation(sm1[:, 1, :], sm1[:, 0, :], ACT.Exp).then_inc(gate_exp_ready, 1)
            for i in range(NCH):
                act.wait_ge(combine_turned, i + 1)
                act.activation(combineT[:, QC * i:QC * (i + 1)], bank[i][0:E1 + 1, :], ACT.Copy
                               ).then_inc(combineT_ready, 1)
            exps_at = 8
            for n, (e, c) in enumerate(units1):
                if n == exps_at:
                    act.wait_ge(exps_wanted, 1)
                    act.activation(old_w, old_w, ACT.Exp)
                    act.activation(new_w, new_w, ACT.Exp)
                    act.activation(keep_w, keep_w, ACT.Exp)
                    act.activation(add_w, add_w, ACT.Exp).then_inc(exps_ready, 1)
                for a in range(FT):
                    u = n * FT + a
                    act.wait_ge(hid1_ps, u + 1)
                    if n >= 2:
                        act.wait_ge(y1_ps, n - 1)
                    b = E0 * FT + e * FT + a
                    act.activation(hid1[:, u % NHS, :], bank[u % 4][:, :], ACT.Gelu, bias=hid_bias[:, b:b + 1]
                                   ).then_inc(hid1_ready, 1)
            act.wait_ge(y1_read, len(units1))
            act.activation(moe, moe, ACT.Silu).then_inc(silu1_ready, 1)

        @block.vector
        def _(dve):
            steps = [0]

            def link(ins):
                steps[0] += 1
                ins.then_inc(dve_step, 1)
                dve.wait_ge(dve_step, steps[0])

            def settle(s, n):
                dve.wait_ge(s, n)

            dve.memset(combine[:, :, :], 1.0)
            link(dve.memset(v_aug[:, :, :, :], 0.0))
            link(dve.memset(v_aug[:, :, :, DH:DH + 1], 1.0))

            def stats(tiles):
                for t in tiles:
                    last = dve.bn_stats(bn[:, t, :], x[:, t, :])
                link(last)
                for t in tiles:
                    last = dve.bn_aggr(mv[:, t, :], bn[:, t, :])
                last.then_inc(stats_ready, 1)

            def normalise(tiles):
                for t in tiles:
                    dve.tensor_scalar(xn[:, t, :], x[:, t, :], mv[:, t, 0:1], rstd[:, t:t + 1], ALU.subtract, ALU.mult
                                      ).then_inc(xn_ready, 1)

            for i in range(NCH):
                dve.wait_ge(x_in[i], 16)
            stats(range(TT))
            dve.wait_ge(rstd_ready, 1)
            normalise(range(TT))
            dve.wait_ge(weights_in, 16 * 21)
            dve.tensor_copy(Wqp[:, :].rearrange("i (d h) -> i d h", h=H), Wq[:, :].rearrange("i (h d) -> i d h", h=H))
            dve.tensor_scalar(bqs[:, :], bq[:, :], SCALE, None, ALU.mult).then_inc(bqs_ready, 1)
            dve.wait_ge(bias_turned, 1)
            dve.tensor_scalar(rwT[:, :], bank[6][:, 0:E0], nw_col[:, :], None, ALU.mult).then_inc(rwT_ready, 1)

            dve.wait_ge(q_f_ready, NCH)
            dve.tensor_copy(q_part[:, 0, :], q_f).then_inc(q_part_ready, 1)
            settle(q_part_ready, 1)
            link(dve.tensor_tensor(q_rest, q_f, q_part[:, 0, :], ALU.subtract))
            dve.tensor_copy(q_part[:, 1, :], q_rest).then_inc(q_part_ready, 1)
            settle(q_part_ready, 2)
            link(dve.tensor_tensor(q_rest, q_rest, q_part[:, 1, :], ALU.subtract))
            dve.tensor_copy(q_part[:, 2, :], q_rest).then_inc(q_part_ready, 1)

            dve.wait_ge(v_ps, 1)
            dve.tensor_tensor(v_aug[:, :, :, 0:DH], bank[4][:, :].rearrange("p (a g d) -> p a g d", a=TT, g=KVH),
                              bv_rows[:, :, :].unsqueeze(1).broadcast_to([P, TT, KVH, DH]), ALU.add
                              ).then_inc(v_ready, 1)
            over_tiles = lambda v, n: v.unsqueeze(2).broadcast_to([P, TT, n])
            dve.wait_ge(rrms_ready, 1)
            dve.wait_ge(route_ps, 1)
            link(dve.tensor_tensor(logits[:, :, :], bank[5][:, 0:TT * E0].rearrange("p (a e) -> p a e", a=TT),
                                   over_tiles(rrms[:, :], E0), ALU.mult))
            dve.tensor_tensor(logits[:, :, :], logits[:, :, :], rb_rows[:, :].unsqueeze(1).broadcast_to([P, TT, E0]),
                              ALU.add).then_inc(logits_ready, 1)
            settle(logits_ready, 1)
            dve.wait_ge(k_part_out, 16)
            link(dve.tensor_reduce(row_max[:, :], logits[:, :, :], AX.X, ALU.max))
            dve.tensor_tensor(probs[:, :, :], logits[:, :, :], over_tiles(row_max[:, :], E0), ALU.subtract
                              ).then_inc(shifted_ready, 1)
            for t in range(TT):
                last = dve.scalar_tensor_tensor(x_route[:, t, :], xn[:, t, :], rrms[:, t:t + 1], nw_rows[:, :],
                                                ALU.mult, ALU.mult)
            last.then_inc(x_route_ready, 1)
            dve.wait_ge(exp0_ready, 1)
            link(dve.tensor_reduce(row_sum[:, :], probs[:, :, :], AX.X, ALU.add))
            link(dve.reciprocal(row_sum[:, :], row_sum[:, :]))
            dve.tensor_tensor(probs[:, :, :], probs[:, :, :], over_tiles(row_sum[:, :], E0), ALU.mult
                              ).then_inc(probs_ready, 1)
            routes = routeT[0:E0, 0:T]
            for kind, n in order:
                if kind == "max":
                    k, j, a, kc = max_units[n]
                    c = chunks[k][1]
                    w = min(QC, P * (TPC * c + a + 1) - QC * kc)
                    dve.wait_ge(max_ps, n + 1)
                    dve.reduce_max(part_max[:, k % 3, j, a, kc:kc + 1], bank[MAX_BANKS[n % 3]][:, 0:w], AX.X).then_inc(max_read, 1)
                    if n == last_max[k]:
                        settle(max_read, n + 1)
                        dve.tensor_reduce(
                            neg_max[:, k % 2, :],
                            part_max[:, k % 3, :, :, 0:c + 1].rearrange("p j t c -> p (j t) c"),
                            AX.X, ALU.max, negate=True).then_inc(neg_max_ready, 1)
                elif kind == "turn_max":
                    dve.wait_ge(side_ps, side_at[kind, n])
                    if n >= 2:
                        dve.wait_ge(max_rows_in[n % 2], 48 * (n // 2))
                    turned = bank[6][0:G * TPC, 0:P]
                    link(dve.tensor_copy(max_part[:, n % 2, 0, :], turned))
                    link(dve.tensor_tensor(max_rest[:, 0, :], turned, max_part[:, n % 2, 0, :], ALU.subtract))
                    link(dve.tensor_copy(max_part[:, n % 2, 1, :], max_rest[:, 0, :]))
                    dve.tensor_tensor(max_part[:, n % 2, 2, :], max_rest[:, 0, :], max_part[:, n % 2, 1, :],
                                      ALU.subtract).then_inc(side_read, 1)
                elif kind == "turn_out":
                    g, c = chunks[n]
                    turned = bank[6][:, :].rearrange("p (a j r) -> p a j r", a=TPC, j=G)
                    dve.wait_ge(side_ps, side_at[kind, n])
                    link(dve.reciprocal(out_rec[:, :, :], turned[:, :, :, DH]))
                    tok = out_tok[:, TPC * c:TPC * (c + 1), G * DH * g:G * DH * (g + 1)]
                    dve.tensor_tensor(tok.rearrange("p a (j d) -> p a j d", j=G), turned[:, :, :, 0:DH],
                                      out_rec[:, :, :].unsqueeze(3).broadcast_to([P, TPC, G, DH]), ALU.mult
                                      ).then_inc(side_read, 1)
                elif kind == "topk":
                    if n == 0:
                        dve.wait_ge(side_read, side_at["routeT", NCH - 1])
                    r = n // 3
                    if n % 3 == 0:
                        link(dve.max(top8[:, :], routes))
                    elif n % 3 == 1:
                        link(dve.max_index(top_at[:, 8 * r:8 * (r + 1)], top8[:, :], routes))
                    else:
                        link(dve.match_replace(routes, top8[:, :], routes, LOWEST))
                    if n == 3 * CAP // 8 - 1:
                        dve.tensor_copy(top_at_f[:, :], top_at[:, :]).then_inc(top_ready, 1)
                elif kind == "token_of":
                    dve.wait_ge(side_ps, side_at[kind, n])
                    dve.tensor_copy(token_of[:, :], bank[6][:, 0:E0]).then_inc(side_read, 1)
                elif kind == "hidden":
                    dve.wait_ge(side_ps, side_at[kind, n])
                    dve.tensor_tensor(hidden0[:, n % BATCH, :].rearrange("p (a t) -> p a t", a=FT),
                                      bank[6][:, :].rearrange("p (a t) -> p a t", a=FT),
                                      hid_bias[:, FT * n:FT * (n + 1)].unsqueeze(2).broadcast_to([P, FT, P]), ALU.add
                                      ).then_inc(side_read, 1)
                elif kind == "y":
                    dve.wait_ge(side_ps, side_at[kind, n])
                    if n >= 2:
                        dve.wait_ge(scattered, 16 * (n - 1))
                    gate = taken[:, n % BATCH, D + n:D + n + 1]
                    dve.tensor_copy(weighted[:, n % 2, D:D + 1], gate)
                    dve.tensor_scalar(weighted[:, n % 2, 0:D], bank[6][:, 0:D], gate, None, ALU.mult
                                      ).then_inc(side_read, 1)
                elif kind == "f0":
                    dve.wait_ge(sums_in, 16)
                    sums = routeT[:, :].rearrange("p (a w) -> p a w", a=TT)
                    link(dve.tensor_scalar(row_max[:, :], sums[:, :, D], 0.0, None, ALU.is_le))
                    link(dve.tensor_tensor(row_sum[:, :], sums[:, :, D], row_max[:, :], ALU.add))
                    link(dve.reciprocal(row_sum[:, :], row_sum[:, :]))
                    dve.tensor_tensor(xn[:, :, :], sums[:, :, 0:D], over_tiles(row_sum[:, :], D), ALU.mult
                                      ).then_inc(f0_ready, 1)
                elif kind == "s0":
                    ts = slice(TPC * n, TPC * (n + 1))
                    if n == NCH - 1:
                        dve.wait_ge(silu0_ready, 1)
                    dve.wait_ge(side_ps, side_at[kind, n])
                    dve.tensor_tensor(xn[:, ts, :], bank[6][:, :].rearrange("p (a d) -> p a d", a=TPC),
                                      bo_rows[:, :].unsqueeze(1).broadcast_to([P, TPC, D]), ALU.add
                                      ).then_inc(side_read, 1)
                    settle(side_read, side_at[kind, n])
                    silu0 = routeT[:, QC * n:QC * (n + 1)].rearrange("p (a d) -> p a d", a=TPC)
                    link(dve.tensor_tensor(xn[:, ts, :], xn[:, ts, :], silu0, ALU.mult))
                    link(dve.tensor_tensor(x[:, ts, :], x[:, ts, :], xn[:, ts, :], ALU.add))
                    stats(range(TPC * n, TPC * (n + 1)))
                elif kind == "xn1":
                    dve.wait_ge(rstd_ready, 1 + NCH - n)
                    normalise(range(TPC * n, TPC * (n + 1)))

            dve.memset(PP[:, 0:1], NEG_BIG)
            dve.memset(AA[:, 0:1], 0.0)
            link(dve.memset(BB[:, 0:1], 0.0))
            dve.tensor_copy(decay[:, :], decay[:, :]).then_inc(decay_ready, 1)
            dve.wait_ge(gate_ps, 1)
            link(dve.tensor_tensor(gates1[:, :, :], bank[6][:, 0:TT * E1].rearrange("p (a e) -> p a e", a=TT),
                                   gb_rows[:, :].unsqueeze(1).broadcast_to([P, TT, E1]), ALU.add))
            for t in range(TT):
                last = dve.max(top1[:, t, :], gates1[:, t, :])
            link(last)
            for t in range(TT):
                dve.max_index(top1_at[:, t, :], top1[:, t, :], gates1[:, t, :])
            dve.tensor_tensor(sm1[:, 0, :], top1[:, :, 1], top1[:, :, 0], ALU.subtract).then_inc(gate_diff_ready, 1)
            settle(gate_diff_ready, 1)
            for n in range(2):
                link(dve.tensor_copy(row_max[:, :], top1_at[:, :, n]))
                link(dve.tensor_tensor(hot[:, n, :, :], iota8[:, :].unsqueeze(1).broadcast_to([P, TT, E1]),
                                       over_tiles(row_max[:, :], E1), ALU.is_equal))
            dve.wait_ge(gate_exp_ready, 1)
            link(dve.tensor_scalar(sm1[:, 2, :], sm1[:, 1, :], 1.0, None, ALU.add))
            link(dve.reciprocal(sm1[:, 2, :], sm1[:, 2, :]))
            link(dve.tensor_tensor(sm1[:, 3, :], sm1[:, 1, :], sm1[:, 2, :], ALU.mult))
            link(dve.tensor_tensor(hot[:, 0, :, :], hot[:, 0, :, :], over_tiles(sm1[:, 2, :], E1), ALU.mult))
            link(dve.tensor_tensor(hot[:, 1, :, :], hot[:, 1, :, :], over_tiles(sm1[:, 3, :], E1), ALU.mult))
            dve.tensor_tensor(combine[:, :, 0:E1], hot[:, 0, :, :], hot[:, 1, :, :], ALU.add).then_inc(combine_ready, 1)
            settle(combine_ready, 1)
            for i in range(NCH):
                dve.wait_ge(moe_bias_ps, i + 1)
                dve.tensor_copy(moe[:, QC * i:QC * (i + 1)], bank[4 + i % 2][:, :]).then_inc(moe_bias_read, 1)
            settle(moe_bias_read, NCH)

            def wkv():
                dve.wait_ge(w_ready, 1)
                dve.wait_ge(rvk_ready, 3 * NCH)
                yield link(dve.tensor_scalar(w_col[:, :], w_col[:, :], -1.0, None, ALU.mult))
                yield link(dve.tensor_tensor_scan(PP[:, 1:T + 1], w_col[:, :].broadcast_to([P, T]), k_T, NEG_BIG,
                                                  ALU.add, ALU.max))
                yield link(dve.scalar_tensor_tensor(tmp, k_T, first[:, :], PP[:, 0:T], ALU.add, ALU.max))
                yield link(dve.tensor_tensor(old_w, PP[:, 0:T], tmp, ALU.subtract))
                yield link(dve.scalar_tensor_tensor(new_w, k_T, first[:, :], tmp, ALU.add, ALU.subtract))
                yield link(dve.scalar_tensor_tensor(keep_w, PP[:, 0:T], w_col[:, :], PP[:, 1:T + 1], ALU.add,
                                                    ALU.subtract))
                yield dve.tensor_tensor(add_w, k_T, PP[:, 1:T + 1], ALU.subtract).then_inc(exps_wanted, 1)
                yield dve.wait_ge(exps_ready, 1)
                yield link(dve.tensor_tensor(tmp, add_w, v_T, ALU.mult))
                yield link(dve.tensor_tensor_scan(AA[:, 1:T + 1], keep_w, tmp, 0.0, ALU.mult, ALU.add))
                yield link(dve.tensor_tensor_scan(BB[:, 1:T + 1], keep_w, add_w, 0.0, ALU.mult, ALU.add))
                yield link(dve.tensor_tensor(tmp, old_w, AA[:, 0:T], ALU.mult))
                yield link(dve.tensor_tensor(keep_w, new_w, v_T, ALU.mult))
                yield link(dve.tensor_tensor(tmp, tmp, keep_w, ALU.add))
                yield link(dve.tensor_tensor(tmp2, old_w, BB[:, 0:T], ALU.mult))
                yield link(dve.tensor_tensor(tmp2, tmp2, new_w, ALU.add))
                for i in range(NCH):
                    yield link(dve.reciprocal(tmp2[:, QC * i:QC * (i + 1)], tmp2[:, QC * i:QC * (i + 1)]))
                yield link(dve.tensor_tensor(tmp, tmp, tmp2, ALU.mult))
                yield dve.tensor_tensor(tmp, tmp, r_T, ALU.mult).then_inc(rwkv_ready, 1)

            mixing = wkv()
            for n, (e, c) in enumerate(units1):
                if n not in (7, 8, 9):
                    next(mixing, None)
                dve.wait_ge(y1_ps, n + 1)
                y = bank[4 + n % 2]
                for a in range(TPC):
                    t = TPC * c + a
                    s = combine[:, t, e:e + 1]
                    last = dve.scalar_tensor_tensor(moe_t[:, t, :], y[:, P * a:P * (a + 1)], s, moe_t[:, t, :],
                                                    ALU.mult, ALU.add)
                last.then_inc(y1_read, 1)
                settle(y1_read, n + 1)
            for _ in mixing:
                pass
            dve.wait_ge(silu1_ready, 1)
            for i in range(NCH):
                ts = slice(TPC * i, TPC * (i + 1))
                dve.wait_ge(s1_ps, i + 1)
                link(dve.tensor_tensor(xn[:, ts, :], bank[i][:, :].rearrange("p (a d) -> p a d", a=TPC),
                                       moe_t[:, ts, :], ALU.mult))
                dve.tensor_tensor(x[:, ts, :], x[:, ts, :], xn[:, ts, :], ALU.add).then_inc(x2_ready, 1)

        @block.tensor
        def _(pe):
            pe.wait_ge(consts_ready, 1)
            pe.wait_ge(weights_in, 16 * 21)
            pe.transpose(bank[6][:, 0:E0], rw[:, :], ident[0:E0, 0:E0]).then_inc(bias_turned, 1)
            nb = hid_bias_in.shape[0]
            pe.transpose(bank[7][:, 0:nb], hid_bias_in[:, :], ident[0:nb, 0:nb]).then_inc(bias_turned, 1)

            for i in range(NCH):
                for a in range(TPC):
                    t = TPC * i + a
                    pe.wait_ge(xn_ready, t + 1)
                    last = pe.transpose(bank[i][:, P * a:P * (a + 1)], xn[:, t, :], ident[:, :])
                last.then_inc(turned_ps, 1)
            pe.wait_ge(rwT_ready, 1)
            pe.wait_ge(bqs_ready, 1)
            pe.wait_ge(hid_bias_ready, 1)
            for i in range(NCH):
                pe.wait_ge(xnT_ready, i + 1)
                pe.matmul(bank[4 + i][:, :], Wqp[:, :], xnT[:, QC * i:QC * (i + 1)], start=True, stop=True
                          ).then_inc(q_ps, 1)
            for i in range(NCH):
                pe.matmul(bank[i][0:KVH * DH, :], Wk[:, :], xnT[:, QC * i:QC * (i + 1)], start=True, stop=True
                          ).then_inc(k_ps, 1)
            pe.wait_ge(q_f_ready, 1)
            for t in range(TT):
                last = pe.matmul(bank[4][:, 32 * t:32 * (t + 1)], xnT[:, P * t:P * (t + 1)], Wv[:, :],
                                 start=True, stop=True)
            last.then_inc(v_ps, 1)
            pe.wait_ge(q_f_ready, 2)
            for t in range(TT):
                last = pe.matmul(bank[5][:, E0 * t:E0 * (t + 1)], xnT[:, P * t:P * (t + 1)], rwT[:, :],
                                 start=True, stop=True)
            last.then_inc(route_ps, 1)
            pe.wait_ge(logits_ready, 1)
            pe.wait_ge(k_f_ready, NCH)
            pe.wait_ge(v_ready, 1)
            pe.wait_ge(bias_rows_in, 16 * 3 * NCH)
            pe.wait_ge(k_rows_in, 16 * 18)

            def side(kind, n):
                if side_at[kind, n] > 1:
                    pe.wait_ge(side_read, side_at[kind, n] - 1)
                out = bank[6]
                if kind == "turn_max":
                    pe.wait_ge(neg_max_ready, n + 1)
                    mm = pe.transpose(out[0:G * TPC, 0:P], neg_max[:, n % 2, :], ident[:, :])
                elif kind == "turn_out":
                    pe.wait_ge(out_sb_ready, n + 1)
                    for a in range(TPC):
                        mm = pe.transpose(out[:, P * a:P * (a + 1)], out_sb[:, n % 2, P * a:P * (a + 1)], ident[:, :])
                if kind == "routeT":
                    for a in range(TPC):
                        mm = pe.transpose(out[0:E0, P * a:P * (a + 1)], logits[:, TPC * n + a, :], ident[:, :])
                elif kind == "token_of":
                    pe.wait_ge(top_ready, 1)
                    mm = pe.transpose(out[:, 0:E0], top_at_f[:, :], ident[0:E0, 0:E0])
                elif kind in ("fc1", "fc2"):
                    raw, there = (fc1_raw, fc1_in) if kind == "fc1" else (fc2_raw, fc2_in)
                    pe.wait_ge(there[n % 2], 16 * (n // 2 + 1))
                    for a in range(FT):
                        mm = pe.transpose(out[:, P * a:P * (a + 1)], raw[:, n % 2, P * a:P * (a + 1)], ident[:, :])
                elif kind == "take":
                    pe.wait_ge(taken_in[n % BATCH], 16 * (n // BATCH + 1))
                    mm = pe.transpose(out[:, 0:CAP], taken[:, n % BATCH, 0:D], ident[:, :])
                elif kind == "hidden":
                    for a in range(FT):
                        mm = pe.matmul(out[:, P * a:P * (a + 1)], fc1T[:, P * a:P * (a + 1)], takenT,
                                       start=True, stop=True)
                elif kind == "y":
                    if n % BATCH == 0:
                        pe.wait_ge(gelu0_ready, n // BATCH + 1)
                    pe.matmul(out[:, 0:D], ones_row[:, :], fc2b[:, D * n:D * (n + 1)], start=True, stop=False)
                    for a in range(FT):
                        mm = pe.matmul(out[:, 0:D], hidden0[:, n % BATCH, P * a:P * (a + 1)],
                                       fc2T[:, P * a:P * (a + 1)], start=False, stop=(a == FT - 1))
                elif kind == "wT":
                    pe.wait_ge(wT_in, 32)
                    for a in range(4):
                        mm = pe.transpose(out[:, P * a:P * (a + 1)], wrvk_raw[:, a, :] if a < 3 else wout_raw,
                                          ident[:, :])
                elif kind == "attnT":
                    for a in range(TPC):
                        mm = pe.transpose(out[:, P * a:P * (a + 1)], out_tok[:, TPC * n + a, :], ident[:, :])
                elif kind == "s0":
                    for a in range(TPC):
                        t = TPC * n + a
                        mm = pe.matmul(out[:, P * a:P * (a + 1)], attnT[:, P * t:P * (t + 1)], Wo[:, :],
                                       start=True, stop=True)
                elif kind == "xn1":
                    pe.wait_ge(xn_ready, TT + TPC * (NCH - n))
                    for a in range(TPC):
                        mm = pe.transpose(out[:, P * a:P * (a + 1)], xn[:, TPC * n + a, :], ident[:, :])
                mm.then_inc(side_ps, 1)

            pe.wait_ge(fc2b_in, 16)
            for kind, n in order:
                if kind == "max":
                    k, j, a, kc = max_units[n]
                    g, c = chunks[k]
                    if n == 0 or k != max_units[n - 1][0]:
                        pe.wait_ge(q_rows_in[c], 16 * 9)
                    h, w = G * g + j, min(QC, P * (TPC * c + a + 1) - QC * kc)
                    diagonal = kc == c
                    if n >= 3:
                        pe.wait_ge(max_read, n - 2)
                    mm = pe.matmul(bank[MAX_BANKS[n % 3]][:, 0:w], q_stack[0:KROWS, c, h, P * a:P * (a + 1)],
                                   k_stack[0:KROWS, g, QC * kc:QC * kc + w], start=True, stop=True)
                    if diagonal:
                        mm = pe.matmul(bank[MAX_BANKS[n % 3]][:, w - P:w], ident_b[:, :], hide_q[:, :], start=False, stop=True,
                                       skip_group_check=True)
                    mm.then_inc(max_ps, 1)
                elif kind == "exp":
                    m, j = n // G, n % G
                    k, kt = quads[m]
                    g, c = chunks[k]
                    h, lo = G * g + j, max(0, P * kt - QC * c)
                    if kt == 0 and j == 0:
                        pe.wait_ge(max_rows_in[k % 2], 48 * (k // 2 + 1))
                    if n >= 3:
                        pe.wait_ge(probsT_ready, n - 2)
                    diagonal = kt >= TPC * c
                    mm = pe.matmul(bank[2 + n % 3][:, lo:QC], k_stack[0:KROWS, g, P * kt:P * (kt + 1)],
                                   q_stack[0:KROWS, c, h, lo:QC], start=True, stop=True)
                    if diagonal:
                        mm = pe.matmul(bank[2 + n % 3][:, lo:lo + P], ident_b[:, :], hide_k[:, :], start=False,
                                       stop=True, skip_group_check=True)
                    mm.then_inc(exp_ps, 1)
                elif kind == "pv":
                    k, kt = quads[n]
                    g, c = chunks[k]
                    lo = max(0, P * kt - QC * c)
                    pe.wait_ge(probsT_ready, G * (n + 1))
                    if kt == 0 and k:
                        pe.wait_ge(out_sb_ready, k)
                    for j in range(G):
                        mm = pe.matmul(bank[5][BLK * j:BLK * (j + 1), lo:QC], v_aug[:, kt, g, :],
                                       probsT[:, (G * n + j) % NP, lo:QC], start=(kt == 0),
                                       stop=(kt == TPC * (c + 1) - 1))
                    mm.then_inc(pv_done, 1)
                elif kind in SIDE:
                    side(kind, n)

            pe.wait_ge(side_read, len(side_at))
            for t in range(TT):
                mm = pe.matmul(bank[6][:, E1 * t:E1 * (t + 1)], xnT[:, P * t:P * (t + 1)], gw[:, :],
                               start=True, stop=True)
            mm.then_inc(gate_ps, 1)
            pe.wait_ge(lay1_in, 16 * 4)
            for n in range(3):
                for i in range(NCH):
                    u = NCH * n + i
                    if u >= 2:
                        pe.wait_ge(rvk_ready, u - 1)
                    pe.matmul(bank[4 + i % 2][:, :], wT[:, (2, 1, 0)[n], :], xnT[:, QC * i:QC * (i + 1)],
                              start=True, stop=True).then_inc(rvk_ps, 1)
            pe.wait_ge(combine_ready, 1)
            for i in range(NCH):
                for a in range(TPC):
                    t = TPC * i + a
                    mm = pe.transpose(bank[i][0:E1 + 1, P * a:P * (a + 1)], combine[:, t, :], ident[:, :])
                mm.then_inc(combine_turned, 1)
            pe.wait_ge(rvk_ready, 3 * NCH)
            for i in range(NCH):
                pe.wait_ge(combineT_ready, i + 1)
                if i >= 2:
                    pe.wait_ge(moe_bias_read, i - 1)
                for a in range(TPC):
                    t = TPC * i + a
                    mm = pe.matmul(bank[4 + i % 2][:, P * a:P * (a + 1)], combineT[:, P * t:P * (t + 1)], b2_all[:, :],
                                   start=True, stop=True)
                mm.then_inc(moe_bias_ps, 1)
            pe.wait_ge(moe_bias_read, NCH)

            def second(n):
                e, c = units1[n]
                w = w2[:, FT * e:FT * (e + 1), :] if e < E1 else ws2
                pe.wait_ge(hid1_ready, FT * (n + 1))
                if n >= 2:
                    pe.wait_ge(y1_read, n - 1)
                for t in range(TPC):
                    for a in range(FT):
                        mm = pe.matmul(bank[4 + n % 2][:, P * t:P * (t + 1)],
                                       hid1[:, (n * FT + a) % NHS, P * t:P * (t + 1)], w[:, a, :],
                                       start=(a == 0), stop=(a == FT - 1))
                mm.then_inc(y1_ps, 1)

            for n, (e, c) in enumerate(units1):
                w = w1[:, e, :] if e < E1 else ws1
                for a in range(FT):
                    u = n * FT + a
                    if u >= 4:
                        pe.wait_ge(hid1_ready, u - 3)
                    pe.matmul(bank[u % 4][:, :], w[:, P * a:P * (a + 1)], xnT[:, QC * c:QC * (c + 1)],
                              start=True, stop=True).then_inc(hid1_ps, 1)
                if n:
                    second(n - 1)
            second(len(units1) - 1)
            pe.wait_ge(rwkv_ready, 1)
            for i in range(NCH):
                for a in range(TPC):
                    t = TPC * i + a
                    mm = pe.matmul(bank[i][:, P * a:P * (a + 1)], tmp[:, P * t:P * (t + 1)], wT[:, 3, :],
                                   start=True, stop=True)
                mm.then_inc(s1_ps, 1)


_INS = ['L0_attn_qkv', 'L0_attn_Wq', 'L0_attn_bq', 'L0_attn_Wk', 'L0_attn_bk', 'L0_attn_Wv', 'L0_attn_bv', 'L0_attn_Wo',
        'L0_attn_bo', 'L0_attn_slopes', 'L0_ffn_norm_weight', 'L0_ffn_router_weight', 'L0_ffn_router_bias',
        'L0_ffn_fc1_weight', 'L0_ffn_fc1_bias', 'L0_ffn_fc2_weight', 'L0_ffn_fc2_bias', 'L1_attn_W_rvk',
        'L1_attn_W_out', 'L1_attn_time_decay', 'L1_attn_time_first', 'L1_ffn_gate_w', 'L1_ffn_gate_b', 'L1_ffn_w1',
        'L1_ffn_b1', 'L1_ffn_w2', 'L1_ffn_b2', 'L1_ffn_ws1', 'L1_ffn_bs1', 'L1_ffn_ws2', 'L1_ffn_bs2']
_OUTS = [((1, T, D), 'float32')]


def kernel(**inputs):
    import numpy as _np
    import concourse.bacc as _bacc
    from concourse import mybir as _mybir
    from concourse.bass_utils import run_bass_kernel_spmd as _run

    nc = _bacc.Bacc("TRN2", target_bir_lowering=False, num_devices=1)
    arrays, args = {}, []
    for name in _INS:
        a = _np.ascontiguousarray(inputs[name])
        arrays[f"in_{name}_dram"] = a
        args.append(nc.dram_tensor(f"in_{name}_dram", a.shape, _mybir.dt.from_np(a.dtype), kind="ExternalInput").ap())
    for i, (shape, dtype) in enumerate(_OUTS):
        dt = _mybir.dt.from_np(_np.dtype(dtype))
        args.append(nc.dram_tensor(f"out_{i}_dram", shape, dt, kind="ExternalOutput").ap())
    two_layers(nc, *args)
    r = _run(nc, [arrays], core_ids=[0])
    got = tuple(r.results[0][f"out_{i}_dram"] for i in range(len(_OUTS)))
    return got[0]
```

```python
import concourse.bass as bass
import numpy as np
from concourse import mybir
from contextlib import ExitStack

F32, BF16, U32 = mybir.dt.float32, mybir.dt.bfloat16, mybir.dt.uint32
ALU, ACT, AX = mybir.AluOpType, mybir.ActivationFunctionType, mybir.AxisListType

T, D, P = 2048, 128, 128
TT = T // P
QC = 512
NCH = T // QC
TPC = QC // P
EPS = 1e-5

H, KVH, DH = 16, 4, 8
G = H // KVH
SCALE = float(DH) ** -0.5
BLK = 32
BIAS_ROWS = 8
KROWS = 3 * BLK
HIDDEN = -1e30
E0, F0 = 16, 512
CAP = T // E0
FT = F0 // P
TAB = D + E0
ACCW = D + 1
E1, F1 = 8, 512
NT1 = (2 * T + E1 * (P - 1)) // P
PER_LOAD = 3
ROW = D + E1 + 1
LOWEST = -3.0e38
BATCH = 4
ROUNDS = CAP // 8
TOPK_FROM, TOPK_EVERY = 20, 3
TOKENS_TAKE = 7
QUADS_PER_STEP = 0.7
SIDE_GAP = 3
F0_AFTER, SILU0_AFTER = 5, 3
XN1_GAP = 10
NEG_BIG = -1e38


MAX_BANKS = (0, 1, 7)
SIDE = ("v", "route", "turn_max", "turn_out", "routeT", "token_of", "fc1", "take", "hidden", "fc2", "y", "wT",
        "attnT", "s0", "xn1")


def schedule():
    chunks = [(g, c) for g in range(KVH) for c in (range(NCH) if g % 2 == 0 else reversed(range(NCH)))]
    max_units, first_max = [], [0]
    quads = []
    for k, (g, c) in enumerate(chunks):
        max_units += [(k, j, a, kc) for j in range(G) for a in range(TPC) for kc in range(c + 1)]
        first_max.append(len(max_units))
        quads += [(k, kt) for kt in range(TPC * (c + 1))]
    n_chunks, n_max = len(chunks), len(max_units)
    order, side, done, turned = [], [], 0, 0
    late = []

    topk = ([("segment", i) for i in range(3 * ROUNDS)] + [("candidates", 0)] + [None] * 3
            + [("topk", i) for i in range(3 * ROUNDS)] + [("token_of", 0)])
    experts = [("gather", e) for e in range(BATCH)]
    for b in range(E0 // BATCH):
        es = range(BATCH * b, BATCH * (b + 1))
        for e in es:
            experts += [("fc1", e), ("take", e), ("hidden", e)]
        experts.append(("gelu", b))
        for e in es:
            experts += [("fc2", e), ("y", e), ("scatter", e)]
            if e + BATCH < E0:
                experts.append(("gather", e + BATCH))
    experts += [("sums", 0), ("wT", 0)] + [None] * F0_AFTER + [("f0", 0)] + [None] * SILU0_AFTER + [("silu0", 0)]
    early = [("v", c) for c in range(NCH)] + [("route", 0), ("probs", 0)] + [("routeT", 0)]
    free = {"gather", "scatter", "sums"}

    def emit_max(n):
        nonlocal done, turned
        for _ in range(min(n, n_max - done)):
            order.append(("max", done))
            done += 1
            if topk and done > TOPK_FROM and (done - TOPK_FROM) % TOPK_EVERY == 0:
                step = topk.pop(0)
                if step:
                    order.append(step)
            if done % 2 == 0 and early:
                order.append(early.pop(0))
            if turned < n_chunks and done == min(first_max[turned + 1] + 5, n_max):
                order.append(("turn_max", turned))
                turned += 1

    emit_max(first_max[1] + 12)
    n_exp = waited = steps_done = 0
    for m, (k, kt) in enumerate(quads):
        g, c = chunks[k]
        size = TPC * (c + 1)
        need = first_max[min(k + 2, n_chunks)] + 12
        if kt == 0:
            start_done = done
        for j in range(G):
            order.append(("exp", n_exp))
            n_exp += 1
            share = (kt * G + j + 1) / (size * G)
            emit_max(int(start_done + (need - start_done) * share) - done)
            if j == G - 1 and m:
                order.append(("pv", m - 1))
            recent = any(step[0] in SIDE for step in order[-SIDE_GAP:])
            due = [entry for entry in late if entry[0] <= m and (entry[1][0] == "turn_out" or not experts)
                   and not (entry[1][0] == "xn1" and ("s0", entry[1][1]) in [e[1] for e in late])
                   and not (entry[1][0] == "xn1" and ("s0", entry[1][1]) in order[-XN1_GAP:])]
            waited += not topk
            if due and not recent:
                order.append(due[0][1])
                late.remove(due[0])
            elif not recent and experts and waited / G - TOKENS_TAKE > steps_done * QUADS_PER_STEP:
                steps_done += 1
                while experts and experts[0] and experts[0][0] in free:
                    order.append(experts.pop(0))
                if experts:
                    step = experts.pop(0)
                    if step:
                        order.append(step)
        if kt == size - 1:
            late.append((m + 2, ("turn_out", k)))
            if g == KVH - 1:
                late += [(m + 3, ("attnT", c)), (m + 4, ("s0", c)), (m + 6, ("xn1", c))]
    order.append(("pv", len(quads) - 1))
    order += experts + [step for _, step in late]
    ready = [("gate", c) for c in (3, 2, 1)] + [("rvk", n, c) for n in range(2) for c in (3, 2, 1)]
    at = order.index(("attnT", 0))
    order[at + 1:] = (ready[3:6] + [("s0", 0)] + ready[0:3] + ready[6:9] + [("xn1", 0), ("gate", 0), ("rvk", 0, 0)])
    return chunks, max_units, quads, order


def two_layers(nc, x_d, Wq_d, bq_d, Wk_d, bk_d, Wv_d, bv_d, Wo_d, bo_d, slopes_d, nw_d, rw_d, rb_d, fc1_d, fc1b_d,
               fc2_d, fc2b_d, Wrvk_d, Wout_d, decay_d, first_d, gw_d, gb_d, w1_d, b1_d, w2_d, b2_d, ws1_d, bs1_d,
               ws2_d, bs2_d, out_d):
    chunks, max_units, quads, order = schedule()
    side_at = {step: i + 1 for i, step in enumerate(s for s in order if s[0] in SIDE)}
    woven = [step for step in order if step[0] == "rvk"]
    rvk_units = woven + [("rvk", n, c) for n in range(3) for c in range(NCH) if ("rvk", n, c) not in woven]
    last_max = {max_units[n][0]: n for n in range(len(max_units))}
    last_quad = {k: m for m, (k, kt) in enumerate(quads)}
    NK = len(chunks)
    with ExitStack() as ctx:
        def sb(name, shape, dt=F32):
            return ctx.enter_context(nc.sbuf_tensor(name, shape, dt))

        def sem(name):
            return ctx.enter_context(nc.semaphore(name))

        def scratch(name, shape, dt=F32):
            return nc.dram_tensor(name, shape, dt, kind="Internal").ap()

        bank = [ctx.enter_context(nc.psum_tensor(f"bank{i}", [P, QC], F32)) for i in range(8)]

        q_parts_d = scratch("q_parts_d", (NCH, 3, D, QC), BF16)
        k_parts_d = scratch("k_parts_d", (NCH, 3, KVH * DH, QC), BF16)
        bias_d = scratch("bias_d", (NCH, 6, 3, H, QC), BF16)
        rows_d = scratch("rows_d", (4, T), BF16)
        table_d = scratch("table_d", (T, TAB))
        cand_val_d = scratch("cand_val_d", (E0, NCH, CAP))
        cand_at_d = scratch("cand_at_d", (E0 * NCH * CAP, 1), U32)
        rows1_d = scratch("rows1_d", (NT1 * P, ROW))
        acc_d = [scratch(f"acc_d{i}", (T + P, D)) for i in range(2)]
        sums_d = scratch("sums_d", (T, ACCW))

        q_stack = sb("q_stack", [P, NCH, H, QC], BF16)
        k_stack = sb("k_stack", [P, KVH, T], BF16)
        x = sb("x", [P, TT, D])
        xrow = sb("xrow", [P, TT, ROW])
        xn = xrow[:, :, 0:D]
        xnT = sb("xnT", [P, T])
        v_aug = sb("v_aug", [P, TT, KVH, BLK])
        arena = sb("arena", [P, 16384])
        routeT = sb("routeT", [P, TT * ACCW])

        Wq = sb("Wq", [D, D])
        Wqp = sb("Wqp", [D, D])
        Wk = sb("Wk", [D, KVH * DH])
        Wkp = sb("Wkp", [D, KVH * DH])
        Wv = sb("Wv", [D, KVH * DH])
        Wo = sb("Wo", [D, D])
        bq = sb("bq", [D, 1])
        bqs = sb("bqs", [D, 1])
        bk = sb("bk", [KVH * DH, 1])
        bv_rows = sb("bv_rows", [P, KVH, DH])
        bo_rows = sb("bo_rows", [P, D])
        nw_rows = sb("nw_rows", [P, D])
        nw_col = sb("nw_col", [D, 1])
        rw = sb("rw", [E0, D])
        rwT = sb("rwT", [D, E0])
        rb_rows = sb("rb_rows", [P, E0])
        slopes = sb("slopes", [H, 1])
        hid_bias_in = sb("hid_bias_in", [E0 * FT + E1 * FT + FT, P])
        hid_bias = sb("hid_bias", [P, E0 * FT + E1 * FT + FT])
        ident = sb("ident", [P, P])
        ident_b = sb("ident_b", [P, P], BF16)
        hide_q = sb("hide_q", [P, P], BF16)
        hide_k = sb("hide_k", [P, P], BF16)
        ones_row = sb("ones_row", [1, P])
        zeros = sb("zeros", [P, ACCW])
        bn = sb("bn", [P, TT, 6])
        mv = sb("mv", [P, TT, 2])
        var_eps = sb("var_eps", [P, TT])
        rstd = sb("rstd", [P, TT])
        minus_half = sb("minus_half", [P, TT])
        mean_sq = sb("mean_sq", [P, TT])
        rrms = sb("rrms", [P, TT])
        logits = sb("logits", [P, TT, E0])
        by_place = sb("by_place", [P, TPC, NCH, E0])
        probs = sb("probs", [P, TT, E0])
        row_max = sb("row_max", [P, TT])
        row_sum = sb("row_sum", [P, TT])
        top8 = sb("top8", [NCH * E0, 8])
        list_start = sb("list_start", [E0, 1])
        row_of = sb("row_of", [CAP, E0], U32)
        segment_of = sb("segment_of", [CAP, E0])
        in_segment = sb("in_segment", [CAP, E0], U32)
        token_f = sb("token_f", [CAP, E0])
        token_of = sb("token_of", [CAP, E0], U32)
        part_max = sb("part_max", [P, 3, G, TPC, NCH])
        neg_max = sb("neg_max", [P, 2, G * TPC])
        max_part = sb("max_part", [G * TPC, 2, 3, P], BF16)
        max_rest = sb("max_rest", [G * TPC, 2, P])
        out_rec = sb("out_rec", [P, TPC, G])
        gates1 = sb("gates1", [P, TT, E1])
        combine = sb("combine", [P, TT, E1 + 1])
        b2_all = sb("b2_all", [E1 + 1, D])
        gw = sb("gw", [D, E1])
        gb_rows = sb("gb_rows", [P, E1])
        decay = sb("decay", [D, 1])
        w_col = sb("w_col", [D, 1])
        first = sb("first", [D, 1])
        sm1 = sb("sm1", [P, 4, TT])
        before = sb("before", [P, P])
        all_ones = sb("all_ones", [P, P])
        not_first = sb("not_first", [P, E1, TT])
        multiples = sb("multiples", [P, TT])
        tiles_of = sb("tiles_of", [P, E1])
        tiles_to = sb("tiles_to", [P, E1])
        slot_of = sb("slot_of", [P, 2, TT], U32)
        tile_number = sb("tile_number", [P, NT1])
        expert_hot = sb("expert_hot", [P, NT1, E1], BF16)
        tile_bias = sb("tile_bias", [P, NT1, FT])
        expert_f = sb("expert_f", [1, NT1])
        expert_of = sb("expert_of", [1, NT1], mybir.dt.int32)
        token_number = sb("token_number", [P, TT])
        add_to = sb("add_to", [P, NT1], U32)
        gate1 = sb("gate1", [P, NT1])
        gate_terms = sb("gate_terms", [P, PER_LOAD, E1])
        iota8 = sb("iota8", [P, E1])

        def part(lo, *shape):
            n = int(np.prod(shape))
            v = arena[:, lo:lo + n]
            return v if len(shape) == 1 else v.rearrange("p (a b) -> p a b", a=shape[0])

        q_f, q_rest = part(0, 2, QC), part(1024, 2, QC)
        q_part = part(2048, 1536).bitcast(BF16).rearrange("p (i a t) -> p i a t", i=2, a=3)
        KD = KVH * DH
        k_f, k_rest = part(3584, 2, QC)[0:KD], part(4608, 2, QC)[0:KD]
        k_part = part(5632, 1536)[0:KD].bitcast(BF16).rearrange("p (i a t) -> p i a t", i=2, a=3)
        shared = part(7168, 3072)[0:H].bitcast(BF16).rearrange("p (n a t) -> p n a t", n=4, a=3)
        hi_w = part(10240, 3072)[0:H].bitcast(BF16).rearrange("p (i n a t) -> p i n a t", i=2, n=2, a=3)
        x_route = part(14336, TT, D)
        unused_row = part(13320, ROW)
        fc2b = xrow[0:1, :, :].rearrange("p a d -> p (a d)")[:, 0:E0 * D]
        NP = 8
        probsT = part(0, NP, QC)
        out_tok = part(4096, TT, D)
        fc1_raw, fc2_raw = part(6144, 2, F0), part(7168, 2, F0)
        fc1T, fc2T = part(8192, F0), part(9216, F0)
        wrvk_raw, wout_raw = part(6144, 3, P), part(6528, P)
        out_sb = part(10240, 2, QC)
        taken = part(11264, BATCH, TAB)
        takenT = part(12416, CAP)
        hidden0 = part(12672, BATCH, F0)
        weighted = part(14720, 2, ACCW)
        attnT = part(12672, T)
        lay1 = q_stack[:, :, :, :].rearrange("p c h t -> p (c h t)").bitcast(F32)
        lay1k = k_stack[:, :, :].rearrange("p h t -> p (h t)").bitcast(F32)
        w1 = lay1[:, 0:4096].rearrange("p (e f) -> p e f", e=E1)
        w2 = lay1[:, 4096:8192].rearrange("p (e f) -> p e f", e=E1 * FT)
        ws1 = lay1[:, 8192:8704]
        ws2 = lay1[:, 8704:9216].rearrange("p (e f) -> p e f", e=FT)
        PP = lay1[:, 9216:9216 + T + 1]
        AA = lay1[:, 11272:11272 + T + 1]
        BB = lay1[:, 13328:13328 + T + 1]
        n = TT * E1
        at = [13336 + n * i for i in range(13)]
        chosen, slot = (lay1[:, a:a + n].rearrange("p (a e) -> p a e", a=TT) for a in at[0:2])
        tile_sum, sum_to = (lay1[:, a:a + n].rearrange("p (e a) -> p e a", e=E1) for a in at[2:4])
        weighed = lay1[:, at[4]:at[4] + 2 * n].rearrange("p (n a e) -> p n a e", n=2, a=TT)
        past_end = lay1[:, at[6]:at[6] + NT1 * E1].rearrange("p (j e) -> p j e", e=E1)
        bias_terms = lay1[:, at[6]:at[6] + NT1 * FT * E1].rearrange("p (j a e) -> p j a e", j=NT1, a=FT)
        hot = lay1[:, at[9]:at[9] + 2 * n].rearrange("p (n a e) -> p n a e", n=2, a=TT)
        top1 = lay1[:, at[11]:at[11] + n].rearrange("p (a e) -> p a e", a=TT)
        top1_at = lay1[:, at[12]:at[12] + n].bitcast(U32).rearrange("p (a e) -> p a e", a=TT)
        r_T, k_T = lay1k[:, 0:T], lay1k[:, T:2 * T]
        NHS = 8
        hid1 = part(0, NHS, QC)
        v_T = part(4096, T)
        keep_w, add_w = part(6144, T), part(8192, T)
        old_w, new_w = part(10240, T), part(12288, T)
        tmp = part(14336, T)
        tmp2 = routeT[:, 0:T]
        combineT = tmp2[0:E1 + 1, :]
        RG = 3
        rows1 = lay1[:, 15384:15384 + 2 * PER_LOAD * ROW].rearrange("p (i w) -> p i w", w=ROW)
        w1_now = xnT[:, 0:RG * F1].rearrange("p (i f) -> p i f", i=RG)
        tileT = xnT[:, RG * F1:RG * (F1 + P)].rearrange("p (i f) -> p i f", i=RG)
        hid_t = part(0, RG, F1)
        y_t = part(RG * F1, 4, D)
        acc_in = [part(6144, T), part(8192, T)]
        moe = v_aug[:, :, :, :].rearrange("p a b c -> p (a b c)")
        moe_t = moe.rearrange("p (a b) -> p a b", a=TT)
        wT = sb("wT", [P, 4, P])

        slope_rest = sb("slope_rest", [H, 2])
        slope_b = sb("slope_b", [H, 3], BF16)
        slope_f = sb("slope_f", [H, 3])
        i_hi, hi_f = routeT[0:H, 0:TT], routeT[0:H, TT:4 * TT].rearrange("p (a b) -> p a b", a=3)
        i_lo, lo_f = routeT[0:H, 128:256], routeT[0:H, 1280:1664].rearrange("p (a b) -> p a b", a=3)
        hi_b = routeT[0:H, 384:432].bitcast(BF16).rearrange("p (n a b) -> p n a b", n=2, a=3)
        lo_b = routeT[0:H, 512:896].bitcast(BF16).rearrange("p (n a b) -> p n a b", n=2, a=3)

        by_segment = routeT[0:NCH * E0, 0:QC]
        cand_val = routeT[0:NCH * E0, QC:QC + CAP]
        cand_at = routeT[0:NCH * E0, QC + CAP:QC + 2 * CAP].bitcast(U32)
        routes = routeT[0:E0, 768:768 + NCH * CAP]
        top_at_f, past, segment_f, top_at = (routeT[0:E0, 1280 + CAP * i:1280 + CAP * (i + 1)] for i in range(4))
        top_at = top_at.bitcast(U32)
        const_rows = routeT[0:TT, 1024:1280].bitcast(BF16).rearrange("p (n b) -> p n b", n=4)

        x_in = [sem(f"x_in{i}") for i in range(NCH)]
        wqk_in = sem("wqk_in")
        weights_in = sem("weights_in")
        ident_ready = sem("ident_ready")
        positions_ready = sem("positions_ready")
        consts_ready = sem("consts_ready")
        stats_ready = sem("stats_ready")
        rstd_ready = sem("rstd_ready")
        xn_ready = sem("xn_ready")
        turned_ps = sem("turned_ps")
        xnT_ready = sem("xnT_ready")
        bias_turned = sem("bias_turned")
        hid_bias_ready = sem("hid_bias_ready")
        rwT_ready = sem("rwT_ready")
        q_ps = sem("q_ps")
        q_f_ready = sem("q_f_ready")
        k_f_ready = sem("k_f_ready")
        parts_ready = sem("parts_ready")
        parts_out = [sem(f"parts_out{c}") for c in range(NCH)]
        slopes_ready = sem("slopes_ready")
        lows_ready = sem("lows_ready")
        hi_ready = sem("hi_ready")
        k_ps = sem("k_ps")
        bqs_ready = sem("bqs_ready")
        rrms_ready = sem("rrms_ready")
        v_aug_cleared = sem("v_aug_cleared")
        x_route_ready = sem("x_route_ready")
        logits_ready = sem("logits_ready")
        shifted_ready = sem("shifted_ready")
        exp0_ready = sem("exp0_ready")
        probs_ready = sem("probs_ready")
        const_rows_out = sem("const_rows_out")
        bias_tables = sem("bias_tables")
        bias_out = [sem(f"bias_out{c}") for c in range(NCH)]
        slope_in = sem("slope_in")
        stack_in = [sem(f"stack_in{c}") for c in range(NCH)]
        const_in = sem("const_in")
        table_out = sem("table_out")
        sums_zero = sem("sums_zero")
        max_ps = sem("max_ps")
        max_read = sem("max_read")
        neg_max_ready = sem("neg_max_ready")
        max_rows_in = [sem(f"max_rows_in{i}") for i in range(2)]
        exp_ps = sem("exp_ps")
        probsT_ready = sem("probsT_ready")
        pv_done = sem("pv_done")
        out_sb_ready = sem("out_sb_ready")
        cands_ready = sem("cands_ready")
        cands_out = sem("cands_out")
        cands_in = sem("cands_in")
        list_start_ready = sem("list_start_ready")
        in_segment_in = sem("in_segment_in")
        top_ready = sem("top_ready")
        side_ps = sem("side_ps")
        side_read = sem("side_read")
        fc1_in = [sem(f"fc1_in{i}") for i in range(2)]
        fc2_in = [sem(f"fc2_in{i}") for i in range(2)]
        fc2b_in = sem("fc2b_in")
        taken_in = [sem(f"taken_in{i}") for i in range(BATCH)]
        gelu0_ready = sem("gelu0_ready")
        scattered = sem("scattered")
        sums_in = sem("sums_in")
        f0_ready = sem("f0_ready")
        silu0_ready = sem("silu0_ready")
        shared_in = sem("shared_in")
        lay1_in = sem("lay1_in")
        wT_in = sem("wT_in")
        rvk_ps = sem("rvk_ps")
        rvk_ready = sem("rvk_ready")
        gate_ps = sem("gate_ps")
        gate_diff_ready = sem("gate_diff_ready")
        gate_exp_ready = sem("gate_exp_ready")
        combine_ready = sem("combine_ready")
        combine_turned = sem("combine_turned")
        combineT_ready = sem("combineT_ready")
        prefix_ps = sem("prefix_ps")
        consts1_ready = sem("consts1_ready")
        unused_ready = sem("unused_ready")
        slots_ready = sem("slots_ready")
        chosen_ready = sem("chosen_ready")
        experts_known = sem("experts_known")
        rows1_clear = sem("rows1_clear")
        acc_clear = sem("acc_clear")
        dispatched = sem("dispatched")
        rows1_in = [sem(f"rows1_in{i}") for i in range(2)]
        w1_now_ready = sem("w1_now_ready")
        tile_turned = sem("tile_turned")
        tileT_ready = sem("tileT_ready")
        gate1_ready = sem("gate1_ready")
        hid_t_ps = sem("hid_t_ps")
        hid_t_biased = sem("hid_t_biased")
        hid_t_ready = sem("hid_t_ready")
        y_t_ps = sem("y_t_ps")
        y_t_ready = sem("y_t_ready")
        added = [sem(f"added{i}") for i in range(2)]
        acc_in_ready = [sem(f"acc_in_ready{c}") for c in range(NCH)]
        moe_ready = sem("moe_ready")
        hid1_ps = sem("hid1_ps")
        hid1_ready = sem("hid1_ready")
        y1_ps = sem("y1_ps")
        y1_read = sem("y1_read")
        decay_ready = sem("decay_ready")
        w_ready = sem("w_ready")
        exps_wanted = sem("exps_wanted")
        exps_ready = sem("exps_ready")
        rwkv_ready = sem("rwkv_ready")
        s1_ps = sem("s1_ps")
        silu1_ready = sem("silu1_ready")
        x2_ready = sem("x2_ready")
        x2_out = sem("x2_out")
        dve_step = sem("dve_step")
        pool_step = sem("pool_step")
        act_step = sem("act_step")

        block = ctx.enter_context(nc.Block())
        N_WEIGHTS = 17
        MIX_PER_TILE = 1
        MIX_AT_SHARED = (13, 13, 0, 11)
        expert_bias = hid_bias[:, E0 * FT:(E0 + E1) * FT].rearrange("p (e a) -> p e a", e=E1)
        CLEAR_ROWS = NT1 * P // 3
        HB, YB = (0, 1, 4), (2, 3, 5)

        @block.sync
        def _(sp):
            x_v = x_d[0].rearrange("(a p) d -> p a d", p=P)
            def load_x(i):
                sp.dma_start(x[:, TPC * i:TPC * (i + 1), :], x_v[:, TPC * i:TPC * (i + 1), :]).then_inc(x_in[i], 16)

            col = lambda v: v.rearrange("(p a) -> p a", a=1)
            row = lambda v: v.rearrange("(a p) -> a p", a=1)
            load_x(0)
            sp.dma_start(slopes[:, :], col(slopes_d)).then_inc(slope_in, 16)
            sp.dma_start(Wq[:, :], Wq_d).then_inc(wqk_in, 16)
            sp.dma_start(Wk[:, :], Wk_d).then_inc(wqk_in, 16)
            load_x(1)
            sp.dma_start(bq[:, :], bq_d.rearrange("(h d) -> d h", h=H), allow_slow_non_contiguous=True
                         ).then_inc(wqk_in, 16)
            sp.dma_start(bk[:, :], bk_d.rearrange("(g d) -> d g", g=KVH), allow_slow_non_contiguous=True
                         ).then_inc(wqk_in, 16)
            load_x(2)
            load_x(3)
            NB = E0 * FT
            loads = [
                (rw[:, :], rw_d), (nw_col[:, :], col(nw_d)),
                (hid_bias_in[0:NB, :], fc1b_d.rearrange("e (a p) -> (e a) p", p=P)),
                (hid_bias_in[NB:NB + E1 * FT, :], b1_d.rearrange("e (a p) -> (e a) p", p=P)),
                (hid_bias_in[NB + E1 * FT:NB + E1 * FT + FT, :], bs1_d.rearrange("(a p) -> a p", p=P)),
                (Wv[:, :], Wv_d), (Wo[:, :], Wo_d),
                (bv_rows[:, :, :], bv_d.rearrange("(a k d) -> a k d", a=1, k=KVH).broadcast_to([P, KVH, DH])),
                (bo_rows[:, :], row(bo_d).broadcast_to([P, D])), (nw_rows[:, :], row(nw_d).broadcast_to([P, D])),
                (rb_rows[:, :], row(rb_d).broadcast_to([P, E0])),
                (gw[:, :], gw_d), (gb_rows[:, :], row(gb_d).broadcast_to([P, E1])),
                (b2_all[0:E1, :], b2_d), (b2_all[E1:E1 + 1, :], row(bs2_d)),
                (decay[:, :], col(decay_d)), (first[:, :], col(first_d)),
            ]
            assert len(loads) == N_WEIGHTS
            for dst, src in loads:
                sp.dma_start(dst, src).then_inc(weights_in, 16)
            for c in range(NCH):
                sp.wait_ge(parts_ready, c + 1)
                sp.dma_start(q_parts_d[c].rearrange("a p t -> p a t"), q_part[:, c % 2, :, :]
                             ).then_inc(parts_out[c], 16)
                sp.dma_start(k_parts_d[c].rearrange("a p t -> p a t"), k_part[:, c % 2, :, :]
                             ).then_inc(parts_out[c], 16)
                if c == 0:
                    sp.wait_ge(slopes_ready, 1)
                    sp.wait_ge(lows_ready, 1)
                    for i in range(NCH):
                        sp.dma_start(bias_d[i, 0:4].rearrange("n a h t -> h (n a) t"),
                                     shared.rearrange("h n a t -> h (n a) t")).then_inc(bias_out[i], 16)
                sp.wait_ge(hi_ready, c + 1)
                sp.dma_start(bias_d[c, 4:6].rearrange("n a h t -> h (n a) t"),
                             hi_w[:, c % 2].rearrange("h n a t -> h (n a) t")).then_inc(bias_out[c], 16)
                sp.wait_ge(parts_out[c], 32)
                for a in range(3):
                    lo = BLK * a + BIAS_ROWS
                    sp.dma_start(
                        q_stack[lo:lo + 3 * DH, c, :, :].rearrange("r h t -> r (h t)"),
                        q_parts_d[c, a].rearrange("(o d h) t -> o d (h t)", o=1, h=H).broadcast_to([3, DH, H * QC])
                    ).then_inc(stack_in[c], 16)
                    sp.dma_start(k_stack[lo:lo + 3 * DH, :, QC * c:QC * (c + 1)],
                                 k_parts_d[c].rearrange("b (d g) t -> (b d) g t", g=KVH)).then_inc(stack_in[c], 16)
                sp.wait_ge(bias_out[c], 32)
                for a in range(3):
                    sp.dma_start(q_stack[BLK * a:BLK * a + 6, c, :, :].rearrange("n h t -> n (h t)"),
                                 bias_d[c, :, a].rearrange("n h t -> n (h t)")).then_inc(stack_in[c], 16)
            def clear_for_layer1(n):
                if n < 3:
                    sp.wait_ge(unused_ready, 1)
                    rows = rows1_d[n * CLEAR_ROWS:(n + 1) * CLEAR_ROWS, :]
                    sp.dma_start(rows.rearrange("(j p) w -> p j w", p=P),
                                 unused_row[:, :].unsqueeze(1).broadcast_to([P, CLEAR_ROWS // P, ROW])
                                 ).then_inc(rows1_clear, 16)
                else:
                    sp.dma_start(acc_d[n - 3].rearrange("(a p) d -> p a d", p=P),
                                 zeros[:, 0:D].unsqueeze(1).broadcast_to([P, TT + 1, D])).then_inc(acc_clear, 16)

            def load_fc1(e):
                sp.dma_start(fc1_raw[:, e % 2, :].rearrange("p (a d) -> p a d", a=FT),
                             fc1_d[e].rearrange("(a p) d -> p a d", p=P)).then_inc(fc1_in[e % 2], 16)

            def load_fc2(e):
                sp.dma_start(fc2_raw[:, e % 2, :], fc2_d[e]).then_inc(fc2_in[e % 2], 16)

            for e in range(2):
                load_fc1(e)
                load_fc2(e)
            for kind, n, *more in order:
                if kind == "turn_max":
                    g, c = chunks[n]
                    sp.wait_ge(side_read, side_at[kind, n])
                    for i, r in enumerate((6, 7, BLK + 6)):
                        sp.dma_start(q_stack[r:r + 1, c, G * g:G * (g + 1), :].rearrange("o h (a b) -> o (h a) b", b=P),
                                     max_part[:, n % 2, i, :]).then_inc(max_rows_in[n % 2], 16)
                    if 1 <= n < 6:
                        clear_for_layer1(n - 1)
                elif kind == "candidates":
                    sp.wait_ge(x_route_ready, 1)
                    sp.dma_start(fc2b, fc2b_d.rearrange("(o e) d -> o (e d)", o=1)).then_inc(fc2b_in, 16)
                    sp.wait_ge(cands_ready, 1)
                    sp.dma_start(cand_val_d.rearrange("e s r -> s e r"), cand_val).then_inc(cands_out, 16)
                    sp.dma_start(cand_at_d.rearrange("(e s r) o -> s e (r o)", e=E0, s=NCH), cand_at
                                 ).then_inc(cands_out, 16)
                    sp.wait_ge(cands_out, 32)
                    sp.dma_start(routes, cand_val_d.rearrange("e s r -> e (s r)")).then_inc(cands_in, 16)
                elif kind == "fc1" and n + 2 < E0:
                    sp.wait_ge(side_ps, side_at[kind, n])
                    load_fc1(n + 2)
                elif kind == "fc2" and n + 2 < E0:
                    sp.wait_ge(side_ps, side_at[kind, n])
                    load_fc2(n + 2)
                elif kind == "y" and n == E0 - 1:
                    sp.dma_start(wrvk_raw, Wrvk_d.rearrange("(a p) c -> p a c", p=P)).then_inc(wT_in, 16)
                    sp.dma_start(wout_raw, Wout_d).then_inc(wT_in, 16)
                elif kind == "sums":
                    sp.wait_ge(scattered, 16 * E0)
                    sp.dma_start(routeT[:, :].rearrange("p (a w) -> p a w", a=TT),
                                 sums_d.rearrange("(a p) w -> p a w", p=P)).then_inc(sums_in, 16)
            sp.wait_ge(pv_done, len(quads))
            sp.dma_start(ws1, ws1_d).then_inc(shared_in, 16)
            sp.dma_start(ws2, ws2_d.rearrange("(a p) d -> p a d", p=P)).then_inc(shared_in, 16)
            sp.dma_start(w1, w1_d.rearrange("e d f -> d e f")).then_inc(lay1_in, 16)
            sp.dma_start(w2, w2_d.rearrange("e (a p) d -> p (e a) d", p=P)).then_inc(lay1_in, 16)
            sp.wait_ge(dispatched, 16 * 2 * TT)
            for i in range(NT1 // PER_LOAD):
                if i >= 2:
                    sp.wait_ge(gate1_ready, i - 1)
                    sp.wait_ge(tile_turned, PER_LOAD * (i - 1))
                sp.dma_start(rows1[:, PER_LOAD * (i % 2):PER_LOAD * (i % 2 + 1), :],
                             rows1_d[P * PER_LOAD * i:P * PER_LOAD * (i + 1), :].rearrange("(j p) w -> p j w", p=P)
                             ).then_inc(rows1_in[i % 2], 16)
            sp.wait_ge(rwkv_ready, 1)
            for i in range(2):
                sp.wait_ge(added[i], 16 * len(range(i, NT1, 2)))
            for c in range(NCH):
                for i in range(2):
                    sp.dma_start(acc_in[i][:, QC * c:QC * (c + 1)].rearrange("p (a d) -> p a d", a=TPC),
                                 acc_d[i][QC * c:QC * (c + 1)].rearrange("(a p) d -> p a d", p=P)
                                 ).then_inc(acc_in_ready[c], 16)
            out_v = out_d[0].rearrange("(a p) d -> p a d", p=P)
            for i in range(NCH):
                sp.wait_ge(x2_ready, i + 1)
                sp.dma_start(out_v[:, TPC * i:TPC * (i + 1), :], x[:, TPC * i:TPC * (i + 1), :]).then_inc(x2_out, 16)
            sp.wait_ge(x2_out, 16 * NCH)

        @block.gpsimd
        def _(pool):
            steps = [0]

            def link(ins):
                steps[0] += 1
                ins.then_inc(pool_step, 1)
                pool.wait_ge(pool_step, steps[0])

            def inverse_root(out, in_, ts=slice(0, TT)):
                link(pool.tensor_scalar(var_eps[:, ts], in_, EPS, None, ALU.add))
                return pool.tensor_tensor(out, var_eps[:, ts], minus_half[:, ts], ALU.pow)

            def positions(out, step, mult):
                return pool.iota(out, pattern=[[step, out.shape[1]]], base=0, channel_multiplier=mult,
                                 allow_small_or_imprecise_dtypes=True)

            link(pool.memset(ident[:, :], 0.0))
            pool.affine_select(out=ident[:, :], in_=ident[:, :], compare_op=ALU.not_equal, fill=1.0, base=0,
                               pattern=[[-1, P]], channel_multiplier=1).then_inc(ident_ready, 1)
            positions(i_hi, P, 0)
            positions(i_lo, 1, 0).then_inc(positions_ready, 1)
            pool.memset(minus_half[:, :], -0.5)
            for n in range(NCH):
                pool.wait_ge(stats_ready, n + 1)
                ts = slice(TPC * n, TPC * (n + 1))
                inverse_root(rstd[:, ts], mv[:, ts, 1], ts).then_inc(rstd_ready, 1)
                if n == 0:
                    positions(const_rows[:, 0, :], 0, P)
                    positions(const_rows[:, 1, :], 1, 0)
                    pool.memset(const_rows[:, 2, :], 1.0)
                    link(pool.memset(const_rows[:, 3, :], 0.0))
                    pool.dma_start(rows_d.rearrange("n (a b) -> a n b", a=TT), const_rows).then_inc(const_rows_out, 16)
                elif n == 1:
                    pool.memset(hide_q[:, :], 0.0)
                    link(pool.memset(hide_k[:, :], 0.0))
                    pool.affine_select(out=hide_q[:, :], in_=hide_q[:, :], compare_op=ALU.is_ge, fill=HIDDEN, base=0,
                                       pattern=[[-1, P]], channel_multiplier=1)
                    pool.affine_select(out=hide_k[:, :], in_=hide_k[:, :], compare_op=ALU.is_ge, fill=HIDDEN, base=0,
                                       pattern=[[1, P]], channel_multiplier=-1)
                    pool.tensor_copy(ident_b[:, :], ident[:, :]).then_inc(consts_ready, 1)
            pool.wait_ge(const_rows_out, 16)
            for a in range(3):
                r = BLK * a
                pool.dma_start(k_stack[r:r + 2, :, :], rows_d[0:2, :].unsqueeze(1).broadcast_to([2, KVH, T])
                               ).then_inc(const_in, 16)
                pool.dma_start(k_stack[r + 2:r + 8, :, :],
                               rows_d[2:3, :].unsqueeze(1).broadcast_to([6, KVH, T])).then_inc(const_in, 16)
                pool.dma_start(q_stack[r + 6:r + 8, :, :, :].rearrange("r c h t -> r (c h) t"),
                               rows_d[3:4, 0:QC].unsqueeze(1).broadcast_to([2, NCH * H, QC])
                               ).then_inc(const_in, 16)
            link(pool.memset(v_aug[:, :, :, :], 0.0))
            pool.memset(v_aug[:, :, :, DH:DH + 1], 1.0).then_inc(v_aug_cleared, 1)
            pool.wait_ge(rstd_ready, NCH)
            link(pool.tensor_tensor(mean_sq[:, :], mv[:, :, 1], rstd[:, :], ALU.mult))
            link(pool.tensor_tensor(mean_sq[:, :], mean_sq[:, :], rstd[:, :], ALU.mult))
            inverse_root(rrms[:, :], mean_sq[:, :]).then_inc(rrms_ready, 1)
            pool.memset(ones_row[:, :], 1.0)
            pool.memset(combine[:, :, :], 1.0)
            positions(iota8[:, :], 1, 0)
            pool.iota(list_start[:, :], pattern=[[0, 1]], base=0, channel_multiplier=NCH * CAP,
                      allow_small_or_imprecise_dtypes=True).then_inc(list_start_ready, 1)
            link(pool.memset(zeros[:, :], 0.0))
            link(pool.memset(unused_row[:, :], 0.0))
            pool.iota(unused_row[:, ROW - 1:ROW], pattern=[[0, 1]], base=T, channel_multiplier=1,
                      allow_small_or_imprecise_dtypes=True).then_inc(unused_ready, 1)
            positions(token_number[:, :], P, 1)
            positions(multiples[:, :], P, 0)
            positions(tile_number[:, :], 1, 0)
            link(pool.memset(all_ones[:, :], 1.0))
            link(pool.memset(not_first[:, :, :], 1.0))
            pool.memset(not_first[:, :, 0:1], 0.0)
            pool.affine_select(out=before[:, :], in_=all_ones[:, :], compare_op=ALU.is_gt, fill=0.0, base=0,
                               pattern=[[1, P]], channel_multiplier=-1).then_inc(consts1_ready, 1)
            pool.dma_start(sums_d.rearrange("(a p) w -> p a w", p=P),
                           zeros[:, :].unsqueeze(1).broadcast_to([P, TT, ACCW])).then_inc(sums_zero, 16)
            pool.wait_ge(weights_in, 16 * N_WEIGHTS)
            pool.wait_ge(xn_ready, TT)
            pool.wait_ge(rrms_ready, 1)
            link(pool.tensor_tensor(x_route, xn[:, :, :], nw_rows[:, :].unsqueeze(1).broadcast_to([P, TT, D]),
                                    ALU.mult))
            pool.tensor_tensor(x_route, x_route, rrms[:, :].unsqueeze(2).broadcast_to([P, TT, D]), ALU.mult
                               ).then_inc(x_route_ready, 1)
            pool.wait_ge(x_route_ready, 1)
            table_v = table_d.rearrange("(a p) w -> p a w", p=P)
            pool.dma_start(table_v[:, :, 0:D], x_route).then_inc(table_out, 16)
            pool.wait_ge(probs_ready, 1)
            pool.dma_start(table_v[:, :, D:TAB], probs[:, :, :]).then_inc(table_out, 16)
            pool.wait_ge(table_out, 32)
            pool.wait_ge(sums_zero, 16)
            for kind, n, *more in order:
                if kind == "token_of":
                    pool.wait_ge(side_read, side_at["token_of", 0])
                    for e in range(E0):
                        pool.indirect_dma_start(
                            in_segment[:, e:e + 1], None, cand_at_d,
                            bass.IndirectOffsetOnAxis(ap=row_of[:, e:e + 1], axis=0)).then_inc(in_segment_in, 16)
                    pool.wait_ge(in_segment_in, 16 * E0)
                    link(pool.tensor_copy(token_f[:, :], in_segment[:, :]))
                    link(pool.tensor_tensor(token_f[:, :], token_f[:, :], segment_of[:, :], ALU.add))
                    link(pool.tensor_copy(token_of[:, :], token_f[:, :]))
                elif kind == "gather":
                    if n >= BATCH:
                        pool.wait_ge(side_read, side_at["y", n - BATCH])
                    pool.indirect_dma_start(
                        taken[:, n % BATCH, :], None, table_d,
                        bass.IndirectOffsetOnAxis(ap=token_of[:, n:n + 1], axis=0)).then_inc(taken_in[n % BATCH], 16)
                elif kind == "scatter":
                    pool.wait_ge(side_read, side_at["y", n])
                    if n:
                        pool.wait_ge(scattered, 16 * n)
                    pool.indirect_dma_start(
                        sums_d, bass.IndirectOffsetOnAxis(ap=token_of[:, n:n + 1], axis=0), weighted[:, n % 2, :], None,
                        compute_op=ALU.add).then_inc(scattered, 16)
                elif kind == "s0":
                    ts = slice(TPC * n, TPC * (n + 1))
                    pool.wait_ge(stats_ready, 2 * NCH - n)
                    inverse_root(rstd[:, ts], mv[:, ts, 1], ts).then_inc(rstd_ready, 1)
            pool.wait_ge(slots_ready, 1)
            pool.wait_ge(rows1_clear, 16 * 3)
            for n in range(2):
                for t in range(TT):
                    pool.indirect_dma_start(
                        rows1_d, bass.IndirectOffsetOnAxis(ap=slot_of[:, n, t:t + 1], axis=0), xrow[:, t, :], None
                    ).then_inc(dispatched, 16)
            pool.wait_ge(acc_clear, 32)
            for j in range(NT1):
                pool.wait_ge(y_t_ready, j + 1)
                if j >= 2:
                    pool.wait_ge(added[j % 2], 16 * (j // 2))
                pool.indirect_dma_start(
                    acc_d[j % 2], bass.IndirectOffsetOnAxis(ap=add_to[:, j:j + 1], axis=0), y_t[:, j % 4, :], None,
                    compute_op=ALU.add).then_inc(added[j % 2], 16)

        @block.scalar
        def _(act):
            steps = [0]

            def link(ins):
                steps[0] += 1
                ins.then_inc(act_step, 1)
                act.wait_ge(act_step, steps[0])

            def bias_hi(c):
                if c >= 2:
                    act.wait_ge(bias_out[c - 2], 32)
                for n in range(2):
                    last = act.activation(
                        hi_w[:, c % 2, n].rearrange("h a (i t) -> h a i t", i=TPC),
                        hi_b[:, n, :, TPC * c:TPC * (c + 1)].unsqueeze(3).broadcast_to([H, 3, TPC, P]), ACT.Copy)
                last.then_inc(hi_ready, 1)

            def take_xnT(c):
                act.wait_ge(turned_ps, c + 1)
                act.activation(xnT[:, QC * c:QC * (c + 1)], bank[c % 2][:, :], ACT.Copy).then_inc(xnT_ready, 1)

            def take_qk(c):
                if c >= 2:
                    act.wait_ge(parts_out[c - 2], 32)
                act.wait_ge(bqs_ready, 1)
                act.wait_ge(q_ps, c + 1)
                for out in (q_f[:, c % 2, :], q_part[:, c % 2, 0, :]):
                    last = act.activation(out, bank[2 + c % 2][:, :], ACT.Identity, bias=bqs[:, :], scale=SCALE)
                last.then_inc(q_f_ready, 1)
                act.wait_ge(k_ps, c + 1)
                for out in (k_f[:, c % 2, :], k_part[:, c % 2, 0, :]):
                    last = act.activation(out, bank[4 + c % 2][0:KD, :], ACT.Identity, bias=bk[:, :])
                last.then_inc(k_f_ready, 1)

            take_xnT(0)
            take_qk(0)
            take_xnT(1)
            act.wait_ge(bias_tables, 1)
            for n in range(2):
                last = act.activation(shared[:, n], slope_b[:, :].unsqueeze(2).broadcast_to([H, 3, QC]), ACT.Copy)
            last.then_inc(slopes_ready, 1)
            bias_hi(0)
            for c in range(1, NCH):
                take_qk(c)
                if c + 1 < NCH:
                    take_xnT(c + 1)
                bias_hi(c)
            act.wait_ge(bias_turned, 2)
            act.activation(hid_bias[:, :], bank[7][:, 0:hid_bias.shape[1]], ACT.Copy).then_inc(hid_bias_ready, 1)

            for c in range(NCH):
                act.wait_ge(parts_out[c], 32)
                act.wait_ge(bias_out[c], 32)
            act.wait_ge(const_rows_out, 16)

            def evacuate_rvk(u):
                _, n, c = rvk_units[u]
                act.wait_ge(rvk_ps, u + 1)
                act.activation((k_T, v_T, r_T)[n][:, QC * c:QC * (c + 1)], bank[4 + u % 2][:, :],
                               ACT.Sigmoid if n == 2 else ACT.Copy).then_inc(rvk_ready, 1)

            def evacuate(kind, n, out, in_):
                act.wait_ge(side_ps, side_at[kind, n])
                act.activation(out, in_, ACT.Copy).then_inc(side_read, 1)

            for kind, n, *more in order:
                if kind == "exp":
                    k, kt = quads[n // G]
                    lo = max(0, P * kt - QC * chunks[k][1])
                    act.wait_ge(exp_ps, n + 1)
                    if n >= NP:
                        act.wait_ge(pv_done, (n - NP) // G + 1)
                    act.activation(probsT[:, n % NP, lo:QC], bank[2 + n % 3][:, lo:QC], ACT.Exp
                                   ).then_inc(probsT_ready, 1)
                elif kind == "pv" and n == last_quad[quads[n][0]]:
                    k = quads[n][0]
                    act.wait_ge(pv_done, n + 1)
                    if k >= 2:
                        act.wait_ge(side_ps, side_at["turn_out", k - 2])
                    act.activation(out_sb[:, k % 2, :], bank[5][:, :], ACT.Copy).then_inc(out_sb_ready, 1)
                elif kind == "route":
                    act.wait_ge(shifted_ready, 1)
                    act.activation(probs[:, :, :], probs[:, :, :], ACT.Exp).then_inc(exp0_ready, 1)
                elif kind == "routeT":
                    evacuate(kind, n, by_segment, bank[6][0:NCH * E0, :])
                elif kind == "fc1":
                    evacuate(kind, n, fc1T, bank[6][:, :])
                elif kind == "fc2":
                    evacuate(kind, n, fc2T, bank[6][:, :])
                elif kind == "take":
                    evacuate(kind, n, takenT, bank[6][:, 0:CAP])
                elif kind == "gelu":
                    act.wait_ge(side_read, side_at["hidden", BATCH * (n + 1) - 1])
                    act.activation(hidden0, hidden0, ACT.Gelu).then_inc(gelu0_ready, 1)
                elif kind == "silu0":
                    act.wait_ge(f0_ready, 1)
                    act.activation(routeT[:, 0:T].rearrange("p (a d) -> p a d", a=TT), xn[:, :, :], ACT.Silu
                                   ).then_inc(silu0_ready, 1)
                elif kind == "wT":
                    evacuate(kind, n, wT[:, :, :].rearrange("p a d -> p (a d)"), bank[6][:, :])
                elif kind == "attnT":
                    evacuate(kind, n, attnT[:, QC * n:QC * (n + 1)], bank[6][:, :])
                elif kind == "xn1":
                    evacuate(kind, n, xnT[:, QC * n:QC * (n + 1)], bank[6][:, :])
                elif kind == "rvk":
                    evacuate_rvk(rvk_units.index((kind, n, *more)))

            act.wait_ge(decay_ready, 1)
            act.activation(w_col[:, :], decay[:, :], ACT.Exp).then_inc(w_ready, 1)
            for u in range(len(woven), len(rvk_units)):
                if u == len(rvk_units) - NCH:
                    act.wait_ge(gate_diff_ready, 1)
                    act.activation(sm1[:, 1, :], sm1[:, 0, :], ACT.Exp).then_inc(gate_exp_ready, 1)
                evacuate_rvk(u)
            for i in range(NCH):
                act.wait_ge(combine_turned, i + 1)
                act.activation(combineT[:, QC * i:QC * (i + 1)], bank[i][0:E1 + 1, :], ACT.Copy
                               ).then_inc(combineT_ready, 1)
            for c in range(NCH):
                if c == NCH - 1:
                    act.wait_ge(exps_wanted, 1)
                    act.activation(old_w, old_w, ACT.Exp)
                    act.activation(new_w, new_w, ACT.Exp)
                    act.activation(keep_w, keep_w, ACT.Exp)
                    act.activation(add_w, add_w, ACT.Exp).then_inc(exps_ready, 1)
                for a in range(FT):
                    u = c * FT + a
                    act.wait_ge(hid1_ps, u + 1)
                    if c >= 2:
                        act.wait_ge(y1_ps, c - 1)
                    b = E0 * FT + E1 * FT + a
                    act.activation(hid1[:, u % NHS, :], bank[u % 4][:, :], ACT.Gelu, bias=hid_bias[:, b:b + 1]
                                   ).then_inc(hid1_ready, 1)
            act.wait_ge(lay1_in, 32)
            act.wait_ge(y1_ps, NCH)

            def take_w1(j):
                e = act.value_load(expert_of[0:1, j:j + 1], min_val=0, max_val=E1 - 1)
                if j >= RG:
                    act.wait_ge(hid_t_ps, j - RG + 1)
                act.activation(w1_now[:, j % RG, :], w1[:, bass.ds(e, 1), :].rearrange("p o f -> p (o f)"), ACT.Copy
                               ).then_inc(w1_now_ready, 1)

            def take_tile(j):
                act.wait_ge(tile_turned, j + 1)
                if j >= RG:
                    act.wait_ge(hid_t_ps, j - RG + 1)
                act.activation(tileT[:, j % RG, :], bank[6 + j % 2][:, 0:P], ACT.Copy
                               ).then_inc(tileT_ready, 1)

            def give(j):
                act.wait_ge(gate1_ready, j // PER_LOAD + 1)
                act.wait_ge(y_t_ps, j + 1)
                if j >= 4:
                    act.wait_ge(added[j % 2], 16 * (j // 2 - 1))
                act.activation(y_t[:, j % 4, :], bank[YB[j % 3]][:, 0:D], ACT.Copy, scale=gate1[:, j:j + 1]
                               ).then_inc(y_t_ready, 1)

            take_w1(0)
            take_w1(1)
            take_tile(0)
            for j in range(NT1):
                if j + 2 < NT1:
                    take_w1(j + 2)
                if j + 1 < NT1:
                    take_tile(j + 1)
                act.wait_ge(hid_t_biased, j + 1)
                act.activation(hid_t[:, j % RG, :], hid_t[:, j % RG, :], ACT.Gelu).then_inc(hid_t_ready, 1)
                if j:
                    give(j - 1)
            give(NT1 - 1)
            for i in range(NCH):
                act.wait_ge(moe_ready, i + 1)
                act.activation(moe[:, QC * i:QC * (i + 1)], moe[:, QC * i:QC * (i + 1)], ACT.Silu
                               ).then_inc(silu1_ready, 1)

        @block.vector
        def _(dve):
            steps = [0]

            def link(ins):
                steps[0] += 1
                ins.then_inc(dve_step, 1)
                dve.wait_ge(dve_step, steps[0])

            def settle(s, n):
                dve.wait_ge(s, n)

            def stats(tiles):
                for t in tiles:
                    last = dve.bn_stats(bn[:, t, :], x[:, t, :])
                link(last)
                for t in tiles:
                    last = dve.bn_aggr(mv[:, t, :], bn[:, t, :])
                last.then_inc(stats_ready, 1)

            def normalise(tiles):
                for t in tiles:
                    dve.tensor_scalar(xn[:, t, :], x[:, t, :], mv[:, t, 0:1], rstd[:, t:t + 1], ALU.subtract, ALU.mult
                                      ).then_inc(xn_ready, 1)

            dve.wait_ge(x_in[0], 16)
            stats(range(TPC))
            dve.wait_ge(slope_in, 16)
            dve.wait_ge(positions_ready, 1)
            link(dve.tensor_copy(slope_b[:, 0:1], slopes[:, :]))
            link(dve.tensor_tensor(slope_rest[:, 0:1], slopes[:, :], slope_b[:, 0:1], ALU.subtract))
            link(dve.tensor_copy(slope_b[:, 1:2], slope_rest[:, 0:1]))
            link(dve.tensor_tensor(slope_b[:, 2:3], slope_rest[:, 0:1], slope_b[:, 1:2], ALU.subtract))
            link(dve.tensor_copy(slope_f[:, :], slope_b[:, :]))
            for i_f, f, b in ((i_hi, hi_f, hi_b), (i_lo, lo_f, lo_b)):
                n = i_f.shape[1]
                link(dve.tensor_tensor(f, i_f.unsqueeze(1).broadcast_to([H, 3, n]),
                                       slope_f[:, :].unsqueeze(2).broadcast_to([H, 3, n]), ALU.mult))
                link(dve.tensor_scalar(b[:, 0], f, -1.0, None, ALU.mult))
                last = dve.scalar_tensor_tensor(b[:, 1], f, -1.0, b[:, 0], ALU.mult, ALU.subtract)
            last.then_inc(bias_tables, 1)
            dve.wait_ge(wqk_in, 64)
            dve.tensor_copy(Wqp[:, :].rearrange("i (d h) -> i d h", h=H), Wq[:, :].rearrange("i (h d) -> i d h", h=H))
            dve.tensor_copy(Wkp[:, :].rearrange("i (d g) -> i d g", g=KVH),
                            Wk[:, :].rearrange("i (g d) -> i d g", g=KVH))
            dve.tensor_scalar(bqs[:, :], bq[:, :], SCALE, None, ALU.mult).then_inc(bqs_ready, 1)

            def parts(c):
                i = c % 2
                dve.wait_ge(q_f_ready, c + 1)
                dve.wait_ge(k_f_ready, c + 1)
                qk = ((q_f, q_rest, q_part), (k_f, k_rest, k_part))
                for f, rest, out in qk:
                    last = dve.tensor_tensor(rest[:, i, :], f[:, i, :], out[:, i, 0, :], ALU.subtract)
                link(last)
                for f, rest, out in qk:
                    last = dve.tensor_copy(out[:, i, 1, :], rest[:, i, :])
                link(last)
                for f, rest, out in qk:
                    last = dve.tensor_tensor(out[:, i, 2, :], rest[:, i, :], out[:, i, 1, :], ALU.subtract)
                last.then_inc(parts_ready, 1)

            def normalise_chunk(c):
                dve.wait_ge(rstd_ready, c + 1)
                normalise(range(TPC * c, TPC * (c + 1)))

            normalise_chunk(0)
            for c in range(1, NCH):
                dve.wait_ge(x_in[c], 16)
                stats(range(TPC * c, TPC * (c + 1)))
                if c == 1:
                    normalise_chunk(1)
            for n in range(2):
                last = dve.tensor_copy(shared[:, 2 + n].rearrange("h a (i t) -> h a i t", i=TPC),
                                       lo_b[:, n].unsqueeze(2).broadcast_to([H, 3, TPC, P]))
            last.then_inc(lows_ready, 1)
            parts(0)
            for c in range(1, NCH):
                if c + 1 < NCH:
                    normalise_chunk(c + 1)
                parts(c)
            dve.wait_ge(weights_in, 16 * N_WEIGHTS)
            dve.wait_ge(bias_turned, 1)
            dve.tensor_scalar(rwT[:, :], bank[6][:, 0:E0], nw_col[:, :], None, ALU.mult).then_inc(rwT_ready, 1)
            over_tiles = lambda v, n: v.unsqueeze(2).broadcast_to([P, TT, n])

            for kind, n, *more in order:
                if kind == "max":
                    k, j, a, kc = max_units[n]
                    c = chunks[k][1]
                    w = min(QC, P * (TPC * c + a + 1) - QC * kc)
                    dve.wait_ge(max_ps, n + 1)
                    dve.reduce_max(part_max[:, k % 3, j, a, kc:kc + 1], bank[MAX_BANKS[n % 3]][:, 0:w], AX.X
                                   ).then_inc(max_read, 1)
                    if n == last_max[k]:
                        settle(max_read, n + 1)
                        dve.tensor_reduce(
                            neg_max[:, k % 2, :],
                            part_max[:, k % 3, :, :, 0:c + 1].rearrange("p j t c -> p (j t) c"),
                            AX.X, ALU.max, negate=True).then_inc(neg_max_ready, 1)
                elif kind == "turn_max":
                    dve.wait_ge(side_ps, side_at[kind, n])
                    if n >= 2:
                        dve.wait_ge(max_rows_in[n % 2], 48 * (n // 2))
                    turned = bank[6][0:G * TPC, 0:P]
                    link(dve.tensor_copy(max_part[:, n % 2, 0, :], turned))
                    link(dve.tensor_tensor(max_rest[:, 0, :], turned, max_part[:, n % 2, 0, :], ALU.subtract))
                    link(dve.tensor_copy(max_part[:, n % 2, 1, :], max_rest[:, 0, :]))
                    dve.tensor_tensor(max_part[:, n % 2, 2, :], max_rest[:, 0, :], max_part[:, n % 2, 1, :],
                                      ALU.subtract).then_inc(side_read, 1)
                elif kind == "turn_out":
                    g, c = chunks[n]
                    turned = bank[6][:, :].rearrange("p (a j r) -> p a j r", a=TPC, j=G)
                    dve.wait_ge(side_ps, side_at[kind, n])
                    link(dve.reciprocal(out_rec[:, :, :], turned[:, :, :, DH]))
                    tok = out_tok[:, TPC * c:TPC * (c + 1), G * DH * g:G * DH * (g + 1)]
                    dve.tensor_tensor(tok.rearrange("p a (j d) -> p a j d", j=G), turned[:, :, :, 0:DH],
                                      out_rec[:, :, :].unsqueeze(3).broadcast_to([P, TPC, G, DH]), ALU.mult
                                      ).then_inc(side_read, 1)
                elif kind == "v":
                    dve.wait_ge(v_aug_cleared, 1)
                    dve.wait_ge(side_ps, side_at[kind, n])
                    dve.tensor_tensor(v_aug[:, TPC * n:TPC * (n + 1), :, 0:DH],
                                      bank[6][:, 0:TPC * KD].rearrange("p (a g d) -> p a g d", a=TPC, g=KVH),
                                      bv_rows[:, :, :].unsqueeze(1).broadcast_to([P, TPC, KVH, DH]), ALU.add
                                      ).then_inc(side_read, 1)
                elif kind == "route":
                    dve.wait_ge(rrms_ready, 1)
                    dve.wait_ge(side_ps, side_at[kind, n])
                    dve.tensor_tensor(logits[:, :, :], bank[6][:, 0:TT * E0].rearrange("p (a e) -> p a e", a=TT),
                                      over_tiles(rrms[:, :], E0), ALU.mult).then_inc(side_read, 1)
                    settle(side_read, side_at[kind, n])
                    link(dve.tensor_tensor(logits[:, :, :], logits[:, :, :],
                                           rb_rows[:, :].unsqueeze(1).broadcast_to([P, TT, E0]), ALU.add))
                    dve.tensor_copy(by_place[:, :, :, :],
                                    logits[:, :, :].rearrange("p (s a) e -> p a s e", a=TPC)).then_inc(logits_ready, 1)
                    link(dve.tensor_reduce(row_max[:, :], logits[:, :, :], AX.X, ALU.max))
                    dve.tensor_tensor(probs[:, :, :], logits[:, :, :], over_tiles(row_max[:, :], E0), ALU.subtract
                                      ).then_inc(shifted_ready, 1)
                elif kind == "probs":
                    dve.wait_ge(exp0_ready, 1)
                    link(dve.tensor_reduce(row_sum[:, :], probs[:, :, :], AX.X, ALU.add))
                    link(dve.reciprocal(row_sum[:, :], row_sum[:, :]))
                    dve.tensor_tensor(probs[:, :, :], probs[:, :, :], over_tiles(row_sum[:, :], E0), ALU.mult
                                      ).then_inc(probs_ready, 1)
                elif kind in ("segment", "topk"):
                    if kind == "segment":
                        rows, values, found = NCH * E0, by_segment, cand_at
                        if n == 0:
                            dve.wait_ge(side_read, side_at["routeT", 0])
                    else:
                        rows, values, found = E0, routes, top_at
                        if n == 0:
                            dve.wait_ge(cands_in, 16)
                    now = slice(8 * (n // 3), 8 * (n // 3 + 1))
                    best = cand_val[:, now] if kind == "segment" else top8[0:rows, :]
                    if n % 3 == 0:
                        last = dve.max(best, values)
                    elif n % 3 == 1:
                        last = dve.max_index(found[:, now], best, values)
                    else:
                        last = dve.match_replace(values, best, values, LOWEST)
                    if n < 3 * ROUNDS - 1:
                        link(last)
                    elif kind == "segment":
                        last.then_inc(cands_ready, 1)
                    else:
                        link(last)
                        dve.wait_ge(list_start_ready, 1)
                        link(dve.tensor_copy(top_at_f[:, :], top_at[:, :]))
                        link(dve.tensor_scalar(segment_f[:, :], top_at_f[:, :], float(CAP), float(QC), ALU.is_ge,
                                               ALU.mult))
                        for i in range(2, NCH):
                            link(dve.tensor_scalar(past[:, :], top_at_f[:, :], float(CAP * i), float(QC), ALU.is_ge,
                                                   ALU.mult))
                            link(dve.tensor_tensor(segment_f[:, :], segment_f[:, :], past[:, :], ALU.add))
                        dve.tensor_scalar(top_at_f[:, :], top_at_f[:, :], list_start[:, :], None, ALU.add
                                          ).then_inc(top_ready, 1)
                elif kind == "token_of":
                    dve.wait_ge(side_ps, side_at[kind, n])
                    dve.tensor_copy(row_of[:, :], bank[6][:, 0:E0])
                    dve.tensor_copy(segment_of[:, :], bank[6][:, E0:2 * E0]).then_inc(side_read, 1)
                elif kind == "hidden":
                    if n == 0:
                        dve.wait_ge(rows1_clear, 16 * 3)
                    dve.wait_ge(side_ps, side_at[kind, n])
                    dve.tensor_tensor(hidden0[:, n % BATCH, :].rearrange("p (a t) -> p a t", a=FT),
                                      bank[6][:, :].rearrange("p (a t) -> p a t", a=FT),
                                      hid_bias[:, FT * n:FT * (n + 1)].unsqueeze(2).broadcast_to([P, FT, P]), ALU.add
                                      ).then_inc(side_read, 1)
                elif kind == "y":
                    dve.wait_ge(side_ps, side_at[kind, n])
                    if n >= 2:
                        dve.wait_ge(scattered, 16 * (n - 1))
                    gate = taken[:, n % BATCH, D + n:D + n + 1]
                    dve.tensor_copy(weighted[:, n % 2, D:D + 1], gate)
                    dve.tensor_scalar(weighted[:, n % 2, 0:D], bank[6][:, 0:D], gate, None, ALU.mult
                                      ).then_inc(side_read, 1)
                elif kind == "f0":
                    dve.wait_ge(sums_in, 16)
                    sums = routeT[:, :].rearrange("p (a w) -> p a w", a=TT)
                    link(dve.tensor_scalar(row_max[:, :], sums[:, :, D], 0.0, None, ALU.is_le))
                    link(dve.tensor_tensor(row_sum[:, :], sums[:, :, D], row_max[:, :], ALU.add))
                    link(dve.reciprocal(row_sum[:, :], row_sum[:, :]))
                    dve.tensor_tensor(xn[:, :, :], sums[:, :, 0:D], over_tiles(row_sum[:, :], D), ALU.mult
                                      ).then_inc(f0_ready, 1)
                elif kind == "s0":
                    ts = slice(TPC * n, TPC * (n + 1))
                    if n == NCH - 1:
                        dve.wait_ge(silu0_ready, 1)
                    dve.wait_ge(side_ps, side_at[kind, n])
                    dve.tensor_tensor(xn[:, ts, :], bank[6][:, :].rearrange("p (a d) -> p a d", a=TPC),
                                      bo_rows[:, :].unsqueeze(1).broadcast_to([P, TPC, D]), ALU.add
                                      ).then_inc(side_read, 1)
                    settle(side_read, side_at[kind, n])
                    silu0 = routeT[:, QC * n:QC * (n + 1)].rearrange("p (a d) -> p a d", a=TPC)
                    link(dve.tensor_tensor(xn[:, ts, :], xn[:, ts, :], silu0, ALU.mult))
                    link(dve.tensor_tensor(x[:, ts, :], x[:, ts, :], xn[:, ts, :], ALU.add))
                    stats(range(TPC * n, TPC * (n + 1)))
                elif kind == "xn1":
                    dve.wait_ge(rstd_ready, 2 * NCH - n)
                    normalise(range(TPC * n, TPC * (n + 1)))

            dve.memset(PP[:, 0:1], NEG_BIG)
            dve.memset(AA[:, 0:1], 0.0)
            link(dve.memset(BB[:, 0:1], 0.0))
            dve.tensor_copy(decay[:, :], decay[:, :]).then_inc(decay_ready, 1)
            dve.wait_ge(gate_ps, NCH)
            link(dve.tensor_tensor(gates1[:, :, :], bank[7][:, 0:TT * E1].rearrange("p (a e) -> p a e", a=TT),
                                   gb_rows[:, :].unsqueeze(1).broadcast_to([P, TT, E1]), ALU.add))
            for t in range(TT):
                last = dve.max(top1[:, t, :], gates1[:, t, :])
            link(last)
            dve.tensor_tensor(sm1[:, 0, :], top1[:, :, 1], top1[:, :, 0], ALU.subtract).then_inc(gate_diff_ready, 1)
            for t in range(TT):
                last = dve.max_index(top1_at[:, t, :], top1[:, t, :], gates1[:, t, :])
            link(last)
            for n in range(2):
                link(dve.tensor_copy(row_max[:, :], top1_at[:, :, n]))
                link(dve.tensor_tensor(hot[:, n, :, :], iota8[:, :].unsqueeze(1).broadcast_to([P, TT, E1]),
                                       over_tiles(row_max[:, :], E1), ALU.is_equal))
            dve.tensor_tensor(chosen[:, :, :], hot[:, 0, :, :], hot[:, 1, :, :], ALU.add).then_inc(chosen_ready, 1)
            dve.wait_ge(gate_exp_ready, 1)
            link(dve.tensor_scalar(sm1[:, 2, :], sm1[:, 1, :], 1.0, None, ALU.add))
            link(dve.reciprocal(sm1[:, 2, :], sm1[:, 2, :]))
            link(dve.tensor_tensor(sm1[:, 3, :], sm1[:, 1, :], sm1[:, 2, :], ALU.mult))
            dve.tensor_tensor(weighed[:, 0, :, :], hot[:, 0, :, :], over_tiles(sm1[:, 2, :], E1), ALU.mult)
            link(dve.tensor_tensor(weighed[:, 1, :, :], hot[:, 1, :, :], over_tiles(sm1[:, 3, :], E1), ALU.mult))
            dve.tensor_tensor(combine[:, :, 0:E1], weighed[:, 0, :, :], weighed[:, 1, :, :], ALU.add
                              ).then_inc(combine_ready, 1)
            settle(combine_ready, 1)
            dve.wait_ge(consts1_ready, 1)
            dve.tensor_copy(xrow[:, :, D:D + E1], combine[:, :, 0:E1])
            dve.tensor_copy(xrow[:, :, ROW - 1], token_number[:, :])
            over_slots = lambda v: v.unsqueeze(2).broadcast_to([P, E1, TT])
            dve.wait_ge(prefix_ps, 1)
            link(dve.tensor_copy(tile_sum[:, :, :], bank[7][:, P:2 * P].rearrange("p (a e) -> p e a", a=TT)))
            link(dve.tensor_tensor_scan(sum_to[:, :, :].rearrange("p e a -> p (e a)"),
                                        not_first[:, :, :].rearrange("p e a -> p (e a)"),
                                        tile_sum[:, :, :].rearrange("p e a -> p (e a)"), 0.0, ALU.mult, ALU.add))
            link(dve.tensor_tensor(weighed[:, 0].rearrange("p a e -> p (a e)").rearrange("p (e a) -> p e a", a=TT),
                                   over_slots(sum_to[:, :, TT - 1]),
                                   multiples[:, :].unsqueeze(1).broadcast_to([P, E1, TT]),
                                   ALU.is_gt))
            link(dve.tensor_reduce(tiles_of[:, :],
                                   weighed[:, 0].rearrange("p a e -> p (a e)").rearrange("p (e a) -> p e a", a=TT),
                                   AX.X, ALU.add))
            link(dve.tensor_tensor_scan(tiles_to[:, :], all_ones[:, 0:E1], tiles_of[:, :], 0.0, ALU.mult, ALU.add))
            link(dve.tensor_tensor(tiles_of[:, :], tiles_to[:, :], tiles_of[:, :], ALU.subtract))
            link(dve.tensor_tensor(sum_to[:, :, :], sum_to[:, :, :], tile_sum[:, :, :], ALU.subtract))
            link(dve.scalar_tensor_tensor(sum_to[:, :, :], over_slots(tiles_of[:, :]), float(P), sum_to[:, :, :],
                                          ALU.mult, ALU.add))
            link(dve.tensor_tensor(slot[:, :, :], bank[7][:, 0:P].rearrange("p (a e) -> p a e", a=TT),
                                   sum_to[:, :, :].rearrange("p e a -> p a e"), ALU.add))
            link(dve.tensor_tensor(weighed[:, :, :, :], hot[:, :, :, :],
                                   slot[:, :, :].unsqueeze(1).broadcast_to([P, 2, TT, E1]), ALU.mult))
            link(dve.tensor_reduce(sm1[:, 0:2, :], weighed[:, :, :, :], AX.X, ALU.add))
            dve.tensor_copy(slot_of[:, :, :], sm1[:, 0:2, :]).then_inc(slots_ready, 1)
            over_tile_list = lambda v: v.unsqueeze(1).broadcast_to([P, NT1, E1])
            numbers = tile_number[:, :].unsqueeze(2).broadcast_to([P, NT1, E1])
            link(dve.tensor_tensor(past_end[:, :, :], numbers, over_tile_list(tiles_to[:, :]), ALU.is_ge))
            link(dve.tensor_reduce(expert_f[:, :], past_end[0:1, :, :], AX.X, ALU.add))
            link(dve.tensor_scalar(expert_f[:, :], expert_f[:, :], float(E1 - 1), None, ALU.min))
            dve.tensor_copy(expert_of[:, :], expert_f[:, :]).then_inc(experts_known, 1)
            link(dve.tensor_tensor(expert_hot[:, :, :], numbers, over_tile_list(tiles_of[:, :]), ALU.is_ge))
            link(dve.tensor_tensor(expert_hot[:, :, :], expert_hot[:, :, :], past_end[:, :, :], ALU.subtract))
            link(dve.tensor_tensor(bias_terms,
                                   expert_bias.rearrange("p e a -> p a e").unsqueeze(1).broadcast_to([P, NT1, FT, E1]),
                                   expert_hot[:, :, :].unsqueeze(2).broadcast_to([P, NT1, FT, E1]), ALU.mult))
            link(dve.tensor_reduce(tile_bias[:, :, :], bias_terms, AX.X, ALU.add))

            def wkv():
                dve.wait_ge(w_ready, 1)
                dve.wait_ge(rvk_ready, len(rvk_units))
                yield link(dve.tensor_scalar(w_col[:, :], w_col[:, :], -1.0, None, ALU.mult))
                pieces = [slice(QC * i, QC * (i + 1)) for i in range(NCH)]
                after = lambda v, c: v[:, c.start + 1:c.stop + 1]
                for c in pieces:
                    yield link(dve.tensor_tensor_scan(after(PP, c), w_col[:, :].broadcast_to([P, QC]), k_T[:, c],
                                                      PP[:, c.start:c.start + 1], ALU.add, ALU.max))
                for c in pieces:
                    yield link(dve.scalar_tensor_tensor(tmp[:, c], k_T[:, c], first[:, :], PP[:, c], ALU.add, ALU.max))
                for c in pieces:
                    yield link(dve.tensor_tensor(old_w[:, c], PP[:, c], tmp[:, c], ALU.subtract))
                for c in pieces:
                    yield link(dve.scalar_tensor_tensor(new_w[:, c], k_T[:, c], first[:, :], tmp[:, c], ALU.add,
                                                        ALU.subtract))
                for c in pieces:
                    yield link(dve.scalar_tensor_tensor(keep_w[:, c], PP[:, c], w_col[:, :], after(PP, c), ALU.add,
                                                        ALU.subtract))
                for c in pieces:
                    last = dve.tensor_tensor(add_w[:, c], k_T[:, c], after(PP, c), ALU.subtract)
                    if c is pieces[-1]:
                        yield last.then_inc(exps_wanted, 1)
                    else:
                        yield last
                yield "exps"
                dve.wait_ge(exps_ready, 1)
                pairs = [(pieces[i], pieces[i + 1]) for i in range(0, NCH, 2)]

                def pairwise(out, in0, in1, op):
                    for pair in pairs:
                        for c in pair:
                            last = dve.tensor_tensor(out[:, c], in0[:, c], in1[:, c], op)
                        yield link(last)

                yield from pairwise(tmp, add_w, v_T, ALU.mult)
                for sums, in_ in ((AA, tmp), (BB, add_w)):
                    for c in pieces:
                        yield link(dve.tensor_tensor_scan(after(sums, c), keep_w[:, c], in_[:, c],
                                                          sums[:, c.start:c.start + 1], ALU.mult, ALU.add))
                yield from pairwise(tmp2, old_w, BB, ALU.mult)
                yield from pairwise(tmp2, tmp2, new_w, ALU.add)
                for h in range(0, T, P):
                    yield link(dve.reciprocal(tmp2[:, h:h + P], tmp2[:, h:h + P]))
                yield from pairwise(tmp, old_w, AA, ALU.mult)
                yield from pairwise(keep_w, new_w, v_T, ALU.mult)
                yield from pairwise(tmp, tmp, keep_w, ALU.add)
                yield from pairwise(tmp, tmp, tmp2, ALU.mult)
                yield from pairwise(tmp, tmp, r_T, ALU.mult)
                dve.engine_nop().then_inc(rwkv_ready, 1)

            mixing = wkv()
            for c in range(NCH):
                for _ in range(MIX_AT_SHARED[c]):
                    next(mixing, None)
                dve.wait_ge(y1_ps, c + 1)
                dve.tensor_copy(moe[:, QC * c:QC * (c + 1)], bank[4 + c % 2][:, :]).then_inc(y1_read, 1)
            settle(y1_read, NCH)

            for j in range(NT1):
                if j % PER_LOAD == 0:
                    i = j // PER_LOAD
                    dve.wait_ge(rows1_in[i % 2], 16 * (i // 2 + 1))
                    r = rows1[:, PER_LOAD * (i % 2):PER_LOAD * (i % 2 + 1), :]
                    js = slice(j, j + PER_LOAD)
                    dve.tensor_copy(add_to[:, js], r[:, :, ROW - 1])
                    link(dve.tensor_tensor(gate_terms[:, :, :], r[:, :, D:D + E1], expert_hot[:, js, :], ALU.mult))
                    dve.tensor_reduce(gate1[:, js], gate_terms[:, :, :], AX.X, ALU.add).then_inc(gate1_ready, 1)
                dve.wait_ge(hid_t_ps, j + 1)
                if j >= RG:
                    dve.wait_ge(y_t_ps, j - RG + 1)
                dve.tensor_tensor(hid_t[:, j % RG, :].rearrange("p (a t) -> p a t", a=FT),
                                  bank[HB[j % 3]][:, :].rearrange("p (a t) -> p a t", a=FT),
                                  tile_bias[:, j, :].unsqueeze(2).broadcast_to([P, FT, P]), ALU.add
                                  ).then_inc(hid_t_biased, 1)
                for _ in range(MIX_PER_TILE):
                    next(mixing, None)
            for _ in mixing:
                pass
            settle(rwkv_ready, 1)

            def whole(i):
                c = slice(QC * i, QC * (i + 1))
                dve.wait_ge(acc_in_ready[i], 32)
                link(dve.tensor_tensor(moe[:, c], moe[:, c], acc_in[0][:, c], ALU.add))
                dve.tensor_tensor(moe[:, c], moe[:, c], acc_in[1][:, c], ALU.add).then_inc(moe_ready, 1)

            whole(0)
            for i in range(NCH):
                if i + 1 < NCH:
                    whole(i + 1)
                ts = slice(TPC * i, TPC * (i + 1))
                dve.wait_ge(silu1_ready, i + 1)
                dve.wait_ge(s1_ps, i + 1)
                link(dve.tensor_tensor(xn[:, ts, :], bank[i][:, :].rearrange("p (a d) -> p a d", a=TPC),
                                       moe_t[:, ts, :], ALU.mult))
                dve.tensor_tensor(x[:, ts, :], x[:, ts, :], xn[:, ts, :], ALU.add).then_inc(x2_ready, 1)

        @block.tensor
        def _(pe):
            pe.wait_ge(ident_ready, 1)
            for c in range(NCH):
                if c >= 2:
                    pe.wait_ge(xnT_ready, c - 1)
                for a in range(TPC):
                    t = TPC * c + a
                    pe.wait_ge(xn_ready, t + 1)
                    mm = pe.transpose(bank[c % 2][:, P * a:P * (a + 1)], xn[:, t, :], ident[:, :])
                mm.then_inc(turned_ps, 1)
                pe.wait_ge(xnT_ready, c + 1)
                pe.wait_ge(bqs_ready, 1)
                if c >= 2:
                    pe.wait_ge(q_f_ready, c - 1)
                    pe.wait_ge(k_f_ready, c - 1)
                ts = slice(QC * c, QC * (c + 1))
                pe.matmul(bank[2 + c % 2][:, :], Wqp[:, :], xnT[:, ts], start=True, stop=True).then_inc(q_ps, 1)
                pe.matmul(bank[4 + c % 2][0:KD, :], Wkp[:, :], xnT[:, ts], start=True, stop=True).then_inc(k_ps, 1)
            pe.wait_ge(weights_in, 16 * N_WEIGHTS)
            pe.transpose(bank[6][:, 0:E0], rw[:, :], ident[0:E0, 0:E0]).then_inc(bias_turned, 1)
            nb = hid_bias_in.shape[0]
            pe.transpose(bank[7][:, 0:nb], hid_bias_in[:, :], ident[0:nb, 0:nb]).then_inc(bias_turned, 1)
            pe.wait_ge(q_f_ready, NCH)
            pe.wait_ge(k_f_ready, NCH)
            pe.wait_ge(hid_bias_ready, 1)
            pe.wait_ge(rwT_ready, 1)
            pe.wait_ge(consts_ready, 1)
            pe.wait_ge(const_in, 16 * 9)

            def side(kind, n):
                if side_at[kind, n] > 1:
                    pe.wait_ge(side_read, side_at[kind, n] - 1)
                out = bank[6]
                if kind == "turn_max":
                    pe.wait_ge(neg_max_ready, n + 1)
                    mm = pe.transpose(out[0:G * TPC, 0:P], neg_max[:, n % 2, :], ident[:, :])
                elif kind == "turn_out":
                    pe.wait_ge(out_sb_ready, n + 1)
                    for a in range(TPC):
                        mm = pe.transpose(out[:, P * a:P * (a + 1)], out_sb[:, n % 2, P * a:P * (a + 1)], ident[:, :])
                if kind == "v":
                    for a in range(TPC):
                        t = TPC * n + a
                        mm = pe.matmul(out[:, KD * a:KD * (a + 1)], xnT[:, P * t:P * (t + 1)], Wv[:, :],
                                       start=True, stop=True)
                elif kind == "route":
                    for t in range(TT):
                        mm = pe.matmul(out[:, E0 * t:E0 * (t + 1)], xnT[:, P * t:P * (t + 1)], rwT[:, :],
                                       start=True, stop=True)
                elif kind == "routeT":
                    pe.wait_ge(logits_ready, 1)
                    for a in range(TPC):
                        mm = pe.transpose(out[0:NCH * E0, P * a:P * (a + 1)],
                                          by_place[:, a, :, :].rearrange("p s e -> p (s e)"),
                                          ident[:, :])
                elif kind == "token_of":
                    pe.wait_ge(top_ready, 1)
                    pe.transpose(out[:, 0:E0], top_at_f[:, :], ident[0:E0, 0:E0])
                    mm = pe.transpose(out[:, E0:2 * E0], segment_f[:, :], ident[0:E0, 0:E0])
                elif kind in ("fc1", "fc2"):
                    raw, there = (fc1_raw, fc1_in) if kind == "fc1" else (fc2_raw, fc2_in)
                    pe.wait_ge(there[n % 2], 16 * (n // 2 + 1))
                    for a in range(FT):
                        mm = pe.transpose(out[:, P * a:P * (a + 1)], raw[:, n % 2, P * a:P * (a + 1)], ident[:, :])
                elif kind == "take":
                    pe.wait_ge(taken_in[n % BATCH], 16 * (n // BATCH + 1))
                    mm = pe.transpose(out[:, 0:CAP], taken[:, n % BATCH, 0:D], ident[:, :])
                elif kind == "hidden":
                    for a in range(FT):
                        mm = pe.matmul(out[:, P * a:P * (a + 1)], fc1T[:, P * a:P * (a + 1)], takenT,
                                       start=True, stop=True)
                elif kind == "y":
                    if n == 0:
                        pe.wait_ge(fc2b_in, 16)
                    if n % BATCH == 0:
                        pe.wait_ge(gelu0_ready, n // BATCH + 1)
                    pe.matmul(out[:, 0:D], ones_row[:, :], fc2b[:, D * n:D * (n + 1)], start=True, stop=False)
                    for a in range(FT):
                        mm = pe.matmul(out[:, 0:D], hidden0[:, n % BATCH, P * a:P * (a + 1)],
                                       fc2T[:, P * a:P * (a + 1)], start=False, stop=(a == FT - 1))
                elif kind == "wT":
                    pe.wait_ge(wT_in, 32)
                    for a in range(4):
                        mm = pe.transpose(out[:, P * a:P * (a + 1)], wrvk_raw[:, a, :] if a < 3 else wout_raw,
                                          ident[:, :])
                elif kind == "attnT":
                    for a in range(TPC):
                        mm = pe.transpose(out[:, P * a:P * (a + 1)], out_tok[:, TPC * n + a, :], ident[:, :])
                elif kind == "s0":
                    for a in range(TPC):
                        t = TPC * n + a
                        mm = pe.matmul(out[:, P * a:P * (a + 1)], attnT[:, P * t:P * (t + 1)], Wo[:, :],
                                       start=True, stop=True)
                elif kind == "xn1":
                    pe.wait_ge(xn_ready, TT + TPC * (NCH - n))
                    for a in range(TPC):
                        mm = pe.transpose(out[:, P * a:P * (a + 1)], xn[:, TPC * n + a, :], ident[:, :])
                mm.then_inc(side_ps, 1)

            def rvk_product(u):
                _, n, c = rvk_units[u]
                if u == 0:
                    pe.wait_ge(probsT_ready, G * len(quads))
                    pe.wait_ge(out_sb_ready, NK)
                pe.wait_ge(side_read, side_at["xn1", c])
                if u >= 2:
                    pe.wait_ge(rvk_ready, u - 1)
                pe.matmul(bank[4 + u % 2][:, :], wT[:, 2 - n, :], xnT[:, QC * c:QC * (c + 1)],
                          start=True, stop=True).then_inc(rvk_ps, 1)

            for kind, n, *more in order:
                if kind == "max":
                    k, j, a, kc = max_units[n]
                    g, c = chunks[k]
                    if g == 0 and (n == 0 or k != max_units[n - 1][0]):
                        pe.wait_ge(stack_in[c], 16 * 9)
                    h, w = G * g + j, min(QC, P * (TPC * c + a + 1) - QC * kc)
                    diagonal = kc == c
                    if n >= 3:
                        pe.wait_ge(max_read, n - 2)
                    mm = pe.matmul(bank[MAX_BANKS[n % 3]][:, 0:w], q_stack[0:KROWS, c, h, P * a:P * (a + 1)],
                                   k_stack[0:KROWS, g, QC * kc:QC * kc + w], start=True, stop=True)
                    if diagonal:
                        mm = pe.matmul(bank[MAX_BANKS[n % 3]][:, w - P:w], ident_b[:, :], hide_q[:, :],
                                       start=False, stop=True, skip_group_check=True)
                    mm.then_inc(max_ps, 1)
                elif kind == "exp":
                    m, j = n // G, n % G
                    k, kt = quads[m]
                    g, c = chunks[k]
                    h, lo = G * g + j, max(0, P * kt - QC * c)
                    if kt == 0 and j == 0:
                        pe.wait_ge(max_rows_in[k % 2], 48 * (k // 2 + 1))
                    if n >= 3:
                        pe.wait_ge(probsT_ready, n - 2)
                    diagonal = kt >= TPC * c
                    mm = pe.matmul(bank[2 + n % 3][:, lo:QC], k_stack[0:KROWS, g, P * kt:P * (kt + 1)],
                                   q_stack[0:KROWS, c, h, lo:QC], start=True, stop=True)
                    if diagonal:
                        mm = pe.matmul(bank[2 + n % 3][:, lo:lo + P], ident_b[:, :], hide_k[:, :], start=False,
                                       stop=True, skip_group_check=True)
                    mm.then_inc(exp_ps, 1)
                elif kind == "pv":
                    k, kt = quads[n]
                    g, c = chunks[k]
                    lo = max(0, P * kt - QC * c)
                    pe.wait_ge(probsT_ready, G * (n + 1))
                    if kt == 0 and k:
                        pe.wait_ge(out_sb_ready, k)
                    for j in range(G):
                        mm = pe.matmul(bank[5][BLK * j:BLK * (j + 1), lo:QC], v_aug[:, kt, g, :],
                                       probsT[:, (G * n + j) % NP, lo:QC], start=(kt == 0),
                                       stop=(kt == TPC * (c + 1) - 1))
                    mm.then_inc(pv_done, 1)
                elif kind in SIDE:
                    side(kind, n)
                elif kind == "gate":
                    pe.wait_ge(max_read, len(max_units))
                    pe.wait_ge(side_read, side_at["xn1", n])
                    for t in range(TPC * n, TPC * (n + 1)):
                        mm = pe.matmul(bank[7][:, E1 * t:E1 * (t + 1)], xnT[:, P * t:P * (t + 1)], gw[:, :],
                                       start=True, stop=True)
                    mm.then_inc(gate_ps, 1)
                elif kind == "rvk":
                    rvk_product(rvk_units.index((kind, n, *more)))

            pe.wait_ge(side_read, len(side_at))
            for u in range(len(woven), len(rvk_units) - NCH):
                rvk_product(u)
            pe.wait_ge(consts1_ready, 1)
            pe.wait_ge(chosen_ready, 1)
            picks = chosen[:, :, :].rearrange("p a e -> p (a e)")
            pe.matmul(bank[7][:, 0:P], before[:, :], picks, start=True, stop=True)
            pe.matmul(bank[7][:, P:2 * P], all_ones[:, :], picks, start=True, stop=True).then_inc(prefix_ps, 1)
            for u in range(len(rvk_units) - NCH, len(rvk_units)):
                rvk_product(u)
            pe.wait_ge(combine_ready, 1)
            for i in range(NCH):
                for a in range(TPC):
                    t = TPC * i + a
                    mm = pe.transpose(bank[i][0:E1 + 1, P * a:P * (a + 1)], combine[:, t, :], ident[:, :])
                mm.then_inc(combine_turned, 1)
            pe.wait_ge(shared_in, 32)
            pe.wait_ge(rvk_ready, 3 * NCH)
            pe.wait_ge(combineT_ready, NCH)

            def second(c):
                pe.wait_ge(hid1_ready, FT * (c + 1))
                if c >= 2:
                    pe.wait_ge(y1_read, c - 1)
                for t in range(TPC):
                    out = bank[4 + c % 2][:, P * t:P * (t + 1)]
                    for a in range(FT):
                        pe.matmul(out, hid1[:, (c * FT + a) % NHS, P * t:P * (t + 1)], ws2[:, a, :],
                                  start=(a == 0), stop=False)
                    mm = pe.matmul(out, combineT[:, P * (TPC * c + t):P * (TPC * c + t + 1)], b2_all[:, :],
                                   start=False, stop=True)
                mm.then_inc(y1_ps, 1)

            for c in range(NCH):
                for a in range(FT):
                    u = c * FT + a
                    if u >= 4:
                        pe.wait_ge(hid1_ready, u - 3)
                    pe.matmul(bank[u % 4][:, :], ws1[:, P * a:P * (a + 1)], xnT[:, QC * c:QC * (c + 1)],
                              start=True, stop=True).then_inc(hid1_ps, 1)
                if c:
                    second(c - 1)
            second(NCH - 1)
            pe.wait_ge(y1_read, NCH)
            pe.wait_ge(slots_ready, 1)
            pe.wait_ge(experts_known, 1)
            pe.wait_ge(lay1_in, 32)

            def turn_tile(j):
                i = j // PER_LOAD
                pe.wait_ge(rows1_in[i % 2], 16 * (i // 2 + 1))
                if j >= 2:
                    pe.wait_ge(tileT_ready, j - 1)
                pe.transpose(bank[6 + j % 2][:, 0:P],
                             rows1[:, PER_LOAD * (i % 2) + j % PER_LOAD, 0:D], ident[:, :]).then_inc(tile_turned, 1)

            def products(j):
                e = pe.value_load(expert_of[0:1, j:j + 1], min_val=0, max_val=E1 - 1)
                pe.wait_ge(hid_t_ready, j + 1)
                if j >= 3:
                    pe.wait_ge(y_t_ready, j - 2)
                w = w2.rearrange("p (e a) d -> p e a d", a=FT)
                for a in range(FT):
                    mm = pe.matmul(bank[YB[j % 3]][:, 0:D], hid_t[:, j % RG, P * a:P * (a + 1)],
                                   w[:, bass.ds(e, 1), a, :].rearrange("p o d -> p (o d)"),
                                   start=(a == 0), stop=(a == FT - 1))
                mm.then_inc(y_t_ps, 1)

            turn_tile(0)
            for j in range(NT1):
                if j + 1 < NT1:
                    turn_tile(j + 1)
                pe.wait_ge(w1_now_ready, j + 1)
                pe.wait_ge(tileT_ready, j + 1)
                if j >= 3:
                    pe.wait_ge(hid_t_biased, j - 2)
                for a in range(FT):
                    mm = pe.matmul(bank[HB[j % 3]][:, P * a:P * (a + 1)], w1_now[:, j % RG, P * a:P * (a + 1)],
                                   tileT[:, j % RG, :], start=True, stop=True)
                mm.then_inc(hid_t_ps, 1)
                if j:
                    products(j - 1)
            products(NT1 - 1)
            pe.wait_ge(rwkv_ready, 1)
            pe.wait_ge(y_t_ready, NT1)
            for i in range(NCH):
                for a in range(TPC):
                    t = TPC * i + a
                    mm = pe.matmul(bank[i][:, P * a:P * (a + 1)], tmp[:, P * t:P * (t + 1)], wT[:, 3, :],
                                   start=True, stop=True)
                mm.then_inc(s1_ps, 1)


_INS = ['L0_attn_qkv', 'L0_attn_Wq', 'L0_attn_bq', 'L0_attn_Wk', 'L0_attn_bk', 'L0_attn_Wv', 'L0_attn_bv', 'L0_attn_Wo',
        'L0_attn_bo', 'L0_attn_slopes', 'L0_ffn_norm_weight', 'L0_ffn_router_weight', 'L0_ffn_router_bias',
        'L0_ffn_fc1_weight', 'L0_ffn_fc1_bias', 'L0_ffn_fc2_weight', 'L0_ffn_fc2_bias', 'L1_attn_W_rvk',
        'L1_attn_W_out', 'L1_attn_time_decay', 'L1_attn_time_first', 'L1_ffn_gate_w', 'L1_ffn_gate_b', 'L1_ffn_w1',
        'L1_ffn_b1', 'L1_ffn_w2', 'L1_ffn_b2', 'L1_ffn_ws1', 'L1_ffn_bs1', 'L1_ffn_ws2', 'L1_ffn_bs2']
_OUTS = [((1, T, D), 'float32')]


def kernel(**inputs):
    import numpy as _np
    import concourse.bacc as _bacc
    from concourse import mybir as _mybir
    from concourse.bass_utils import run_bass_kernel_spmd as _run

    nc = _bacc.Bacc("TRN2", target_bir_lowering=False, num_devices=1)
    arrays, args = {}, []
    for name in _INS:
        a = _np.ascontiguousarray(inputs[name])
        arrays[f"in_{name}_dram"] = a
        args.append(nc.dram_tensor(f"in_{name}_dram", a.shape, _mybir.dt.from_np(a.dtype), kind="ExternalInput").ap())
    for i, (shape, dtype) in enumerate(_OUTS):
        dt = _mybir.dt.from_np(_np.dtype(dtype))
        args.append(nc.dram_tensor(f"out_{i}_dram", shape, dt, kind="ExternalOutput").ap())
    two_layers(nc, *args)
    r = _run(nc, [arrays], core_ids=[0])
    got = tuple(r.results[0][f"out_{i}_dram"] for i in range(len(_OUTS)))
    return got[0]
```
